# Optimizing a Trainium2 kernel written in Bass

```python
import numpy as np
import jax
import jax.numpy as jnp

def _softmax(x, axis=-1):
    return jax.nn.softmax(x, axis=axis)

def _gelu(x):
    return jax.nn.gelu(x, approximate=True)

def _silu(x):
    return jax.nn.silu(x)

def _sigmoid(x):
    return jax.nn.sigmoid(x)

def _layernorm(x, axis=-1, eps=1e-05):
    m = jnp.mean(x, axis=axis, keepdims=True)
    v = jnp.var(x, axis=axis, keepdims=True)
    return (x - m) / jnp.sqrt(v + eps)

def _scatter_add(tgt, idx, src, axis=0):
    return tgt.at[idx].add(src)

def _segment_sum(src, seg, n):
    return jax.ops.segment_sum(src, seg, n)
kernel_name = 'mk_vit_tower_d1_tok_img1024_r4_1e1252'

def setup_inputs(seed: int=0):
    np.random.seed(seed)
    _w = jnp.asarray

    def _rec_inputs():
        import jax
        import jax.numpy as jnp
        _rk = jax.random.key(seed)
        x = jax.random.uniform(jax.random.fold_in(_rk, 1), (8, 3, 256, 256), jnp.float32, 0.0, 1)
        return x
    x = _rec_inputs()

    def _L0_tok_setup():
        import jax, jax.numpy as jnp
        import numpy as np
        _GRAY_W = (0.2989, 0.587, 0.114)
        key = jax.random.key(seed)
        x = jax.random.uniform(key, (32, 3, 256, 256), dtype=jnp.float32)
        sx = jnp.array([[-3.0, 0.0, 3.0], [-10.0, 0.0, 10.0], [-3.0, 0.0, 3.0]], dtype=jnp.float32)
        scharr = jnp.stack([sx, sx.T])[:, None, :, :]
        return {'x': x, 'scharr': scharr}
    _L0_tok_all = _L0_tok_setup()
    _L0_tok_in = {k: v for k, v in _L0_tok_all.items() if k in ('scharr',)}
    del _L0_tok_all

    def _L0_attn_setup():
        import jax, jax.numpy as jnp
        import numpy as np
        import math
        DIM = 256
        HEADS = 16
        HEAD_DIM = DIM // HEADS
        FFN_DIM = 1024
        WINDOW = 125
        B, T = (2, 512)

        def _layernorm(x, w, b, eps=1e-05):
            mu = jnp.mean(x, axis=-1, keepdims=True)
            var = jnp.var(x, axis=-1, keepdims=True)
            return (x - mu) / jnp.sqrt(var + eps) * w + b

        def _rotate_half(x):
            x1, x2 = jnp.split(x, 2, axis=-1)
            return jnp.concatenate([-x2, x1], axis=-1)

        def _rope_tables(seq_len, dim, theta=10000.0):
            inv_freq = 1.0 / theta ** (jnp.arange(0, dim, 2, dtype=jnp.float32) / dim)
            t = jnp.arange(seq_len, dtype=jnp.float32)
            freqs = jnp.outer(t, inv_freq)
            emb = jnp.concatenate([freqs, freqs], axis=-1)
            return (jnp.cos(emb), jnp.sin(emb))

        def _block(x, norm1_w, norm1_b, norm2_w, norm2_b, wq, wk, wv, wo, w1, b1, w2, b2, ls1, ls2):
            Bx, Tx, D = x.shape
            h = _layernorm(x, norm1_w, norm1_b)

            def proj(w):
                y = jnp.einsum('btd,ed->bte', h, w)
                return y.reshape(Bx, Tx, HEADS, HEAD_DIM).transpose(0, 2, 1, 3)
            Q, K, V = (proj(wq), proj(wk), proj(wv))
            cos, sin = _rope_tables(Tx, HEAD_DIM)
            cos = cos[None, None]
            sin = sin[None, None]
            Q = Q * cos + _rotate_half(Q) * sin
            K = K * cos + _rotate_half(K) * sin
            idx = jnp.arange(Tx)
            diff = idx[:, None] - idx[None, :]
            mask = jnp.where((diff >= 0) & (diff < WINDOW), 0.0, -jnp.inf)
            scale = math.sqrt(HEAD_DIM)
            scores = jnp.einsum('bhtd,bhsd->bhts', Q, K) / scale + mask[None, None]
            attn = jax.nn.softmax(scores, axis=-1)
            attn_out = jnp.einsum('bhts,bhsd->bhtd', attn, V)
            attn_out = attn_out.transpose(0, 2, 1, 3).reshape(Bx, Tx, D)
            x = x + jnp.einsum('btd,ed->bte', attn_out, wo) * ls1
            h2 = _layernorm(x, norm2_w, norm2_b)
            f = jax.nn.gelu(jnp.einsum('btd,fd->btf', h2, w1) + b1, approximate=False)
            f = jnp.einsum('btf,df->btd', f, w2) + b2
            x = x + f * ls2
            return x
        key = jax.random.key(seed)
        ks = jax.random.split(key, 12)
        s = 0.02
        return {'x': jax.random.normal(ks[0], (B, T, DIM), dtype=jnp.float32), 'norm1_w': jnp.ones((DIM,), jnp.float32), 'norm1_b': jnp.zeros((DIM,), jnp.float32), 'norm2_w': jnp.ones((DIM,), jnp.float32), 'norm2_b': jnp.zeros((DIM,), jnp.float32), 'wq': jax.random.normal(ks[1], (DIM, DIM), jnp.float32) * s, 'wk': jax.random.normal(ks[2], (DIM, DIM), jnp.float32) * s, 'wv': jax.random.normal(ks[3], (DIM, DIM), jnp.float32) * s, 'wo': jax.random.normal(ks[4], (DIM, DIM), jnp.float32) * s, 'w1': jax.random.normal(ks[5], (FFN_DIM, DIM), jnp.float32) * s, 'b1': jnp.zeros((FFN_DIM,), jnp.float32), 'w2': jax.random.normal(ks[6], (DIM, FFN_DIM), jnp.float32) * s, 'b2': jnp.zeros((DIM,), jnp.float32), 'ls1': jnp.full((DIM,), 0.01, jnp.float32), 'ls2': jnp.full((DIM,), 0.01, jnp.float32)}
    _L0_attn_all = _L0_attn_setup()
    _L0_attn_in = {k: v for k, v in _L0_attn_all.items() if k in ('norm1_w', 'norm1_b', 'norm2_w', 'norm2_b', 'wq', 'wk', 'wv', 'wo', 'w1', 'b1', 'w2', 'b2', 'ls1', 'ls2')}
    del _L0_attn_all

    def _L0_ffn_setup():
        import jax, jax.numpy as jnp
        import numpy as np
        DIM = 256
        HID = 128
        N_EXPERTS = 16
        TOP_K = 4
        key = jax.random.key(seed)
        ks = jax.random.split(key, 8)
        s = 0.02
        x = jax.random.normal(ks[0], (2, 256, DIM), dtype=jnp.float32)
        gate_w = jax.random.normal(ks[1], (N_EXPERTS, DIM), dtype=jnp.float32) * s
        w1 = jax.random.normal(ks[2], (N_EXPERTS, HID, DIM), dtype=jnp.float32) * s
        w3 = jax.random.normal(ks[3], (N_EXPERTS, HID, DIM), dtype=jnp.float32) * s
        w2 = jax.random.normal(ks[4], (N_EXPERTS, DIM, HID), dtype=jnp.float32) * s
        sw1 = jax.random.normal(ks[5], (HID, DIM), dtype=jnp.float32) * s
        sw3 = jax.random.normal(ks[6], (HID, DIM), dtype=jnp.float32) * s
        sw2 = jax.random.normal(ks[7], (DIM, HID), dtype=jnp.float32) * s
        return {'x': x, 'gate_w': gate_w, 'w1': w1, 'w3': w3, 'w2': w2, 'sw1': sw1, 'sw3': sw3, 'sw2': sw2}
    _L0_ffn_all = _L0_ffn_setup()
    _L0_ffn_in = {k: v for k, v in _L0_ffn_all.items() if k in ('gate_w', 'w1', 'w3', 'w2', 'sw1', 'sw3', 'sw2')}
    del _L0_ffn_all
    return {'x': x, 'L0_tok_scharr': _L0_tok_in['scharr'], 'L0_attn_norm1_w': _L0_attn_in['norm1_w'], 'L0_attn_norm1_b': _L0_attn_in['norm1_b'], 'L0_attn_norm2_w': _L0_attn_in['norm2_w'], 'L0_attn_norm2_b': _L0_attn_in['norm2_b'], 'L0_attn_wq': _L0_attn_in['wq'], 'L0_attn_wk': _L0_attn_in['wk'], 'L0_attn_wv': _L0_attn_in['wv'], 'L0_attn_wo': _L0_attn_in['wo'], 'L0_attn_w1': _L0_attn_in['w1'], 'L0_attn_b1': _L0_attn_in['b1'], 'L0_attn_w2': _L0_attn_in['w2'], 'L0_attn_b2': _L0_attn_in['b2'], 'L0_attn_ls1': _L0_attn_in['ls1'], 'L0_attn_ls2': _L0_attn_in['ls2'], 'L0_ffn_gate_w': _L0_ffn_in['gate_w'], 'L0_ffn_w1': _L0_ffn_in['w1'], 'L0_ffn_w3': _L0_ffn_in['w3'], 'L0_ffn_w2': _L0_ffn_in['w2'], 'L0_ffn_sw1': _L0_ffn_in['sw1'], 'L0_ffn_sw3': _L0_ffn_in['sw3'], 'L0_ffn_sw2': _L0_ffn_in['sw2']}

def reference(x, L0_tok_scharr, L0_attn_norm1_w, L0_attn_norm1_b, L0_attn_norm2_w, L0_attn_norm2_b, L0_attn_wq, L0_attn_wk, L0_attn_wv, L0_attn_wo, L0_attn_w1, L0_attn_b1, L0_attn_w2, L0_attn_b2, L0_attn_ls1, L0_attn_ls2, L0_ffn_gate_w, L0_ffn_w1, L0_ffn_w3, L0_ffn_w2, L0_ffn_sw1, L0_ffn_sw3, L0_ffn_sw2):
    import jax
    import jax.numpy as jnp

    def _L0_tok_ref(x, scharr):
        import jax, jax.numpy as jnp
        import numpy as np
        _GRAY_W = (0.2989, 0.587, 0.114)
        w = jnp.asarray(_GRAY_W, dtype=x.dtype)
        gray = jnp.einsum('bchw,c->bhw', x, w)[:, None]
        edges = jax.lax.conv_general_dilated(gray, scharr, window_strides=(1, 1), padding='SAME', dimension_numbers=('NCHW', 'OIHW', 'NCHW'))
        abs_edges = jnp.sqrt(jnp.square(edges))
        edge = abs_edges.sum(axis=1) / 2
        return edge

    def _L0_attn_ref(x, norm1_w, norm1_b, norm2_w, norm2_b, wq, wk, wv, wo, w1, b1, w2, b2, ls1, ls2):
        import jax, jax.numpy as jnp
        import numpy as np
        import math
        DIM = 256
        HEADS = 16
        HEAD_DIM = DIM // HEADS
        FFN_DIM = 1024
        WINDOW = 125
        B, T = (2, 512)

        def _layernorm(x, w, b, eps=1e-05):
            mu = jnp.mean(x, axis=-1, keepdims=True)
            var = jnp.var(x, axis=-1, keepdims=True)
            return (x - mu) / jnp.sqrt(var + eps) * w + b

        def _rotate_half(x):
            x1, x2 = jnp.split(x, 2, axis=-1)
            return jnp.concatenate([-x2, x1], axis=-1)

        def _rope_tables(seq_len, dim, theta=10000.0):
            inv_freq = 1.0 / theta ** (jnp.arange(0, dim, 2, dtype=jnp.float32) / dim)
            t = jnp.arange(seq_len, dtype=jnp.float32)
            freqs = jnp.outer(t, inv_freq)
            emb = jnp.concatenate([freqs, freqs], axis=-1)
            return (jnp.cos(emb), jnp.sin(emb))

        def _block(x, norm1_w, norm1_b, norm2_w, norm2_b, wq, wk, wv, wo, w1, b1, w2, b2, ls1, ls2):
            Bx, Tx, D = x.shape
            h = _layernorm(x, norm1_w, norm1_b)

            def proj(w):
                y = jnp.einsum('btd,ed->bte', h, w)
                return y.reshape(Bx, Tx, HEADS, HEAD_DIM).transpose(0, 2, 1, 3)
            Q, K, V = (proj(wq), proj(wk), proj(wv))
            cos, sin = _rope_tables(Tx, HEAD_DIM)
            cos = cos[None, None]
            sin = sin[None, None]
            Q = Q * cos + _rotate_half(Q) * sin
            K = K * cos + _rotate_half(K) * sin
            idx = jnp.arange(Tx)
            diff = idx[:, None] - idx[None, :]
            mask = jnp.where((diff >= 0) & (diff < WINDOW), 0.0, -jnp.inf)
            scale = math.sqrt(HEAD_DIM)
            scores = jnp.einsum('bhtd,bhsd->bhts', Q, K) / scale + mask[None, None]
            attn = jax.nn.softmax(scores, axis=-1)
            attn_out = jnp.einsum('bhts,bhsd->bhtd', attn, V)
            attn_out = attn_out.transpose(0, 2, 1, 3).reshape(Bx, Tx, D)
            x = x + jnp.einsum('btd,ed->bte', attn_out, wo) * ls1
            h2 = _layernorm(x, norm2_w, norm2_b)
            f = jax.nn.gelu(jnp.einsum('btd,fd->btf', h2, w1) + b1, approximate=False)
            f = jnp.einsum('btf,df->btd', f, w2) + b2
            x = x + f * ls2
            return x
        return _block(x, norm1_w, norm1_b, norm2_w, norm2_b, wq, wk, wv, wo, w1, b1, w2, b2, ls1, ls2)

    def _L0_ffn_ref(x, gate_w, w1, w3, w2, sw1, sw3, sw2):
        import jax, jax.numpy as jnp
        import numpy as np
        DIM = 256
        HID = 128
        N_EXPERTS = 16
        TOP_K = 4
        bsz, seq_len, dim = x.shape
        xf = x.reshape(-1, dim)
        T = xf.shape[0]
        probs = jax.nn.softmax(xf @ gate_w.T, axis=-1)
        top_w, top_idx = jax.lax.top_k(probs, TOP_K)
        top_w = top_w / jnp.sum(top_w, axis=-1, keepdims=True)
        rows = jnp.arange(T)[:, None]
        combine = jnp.zeros((T, N_EXPERTS), dtype=xf.dtype).at[rows, top_idx].set(top_w)
        h1 = jnp.einsum('td,ehd->teh', xf, w1)
        h3 = jnp.einsum('td,ehd->teh', xf, w3)
        act = jax.nn.silu(h1) * h3
        eout = jnp.einsum('teh,edh->ted', act, w2)
        moe_out = jnp.einsum('ted,te->td', eout, combine)
        shared = jax.nn.silu(xf @ sw1.T) * (xf @ sw3.T) @ sw2.T
        return (moe_out + shared).reshape(bsz, seq_len, dim)
    h = _L0_tok_ref(x, L0_tok_scharr)
    h = h + _L0_attn_ref(_layernorm(h, axis=-1), L0_attn_norm1_w, L0_attn_norm1_b, L0_attn_norm2_w, L0_attn_norm2_b, L0_attn_wq, L0_attn_wk, L0_attn_wv, L0_attn_wo, L0_attn_w1, L0_attn_b1, L0_attn_w2, L0_attn_b2, L0_attn_ls1, L0_attn_ls2)
    h = h + _L0_ffn_ref(_layernorm(h, axis=-1), L0_ffn_gate_w, L0_ffn_w1, L0_ffn_w3, L0_ffn_w2, L0_ffn_sw1, L0_ffn_sw3, L0_ffn_sw2)
    return h

_drawn_inputs = setup_inputs


def setup_inputs(seed=0):
    import zlib

    import numpy as np

    out = dict(_drawn_inputs(seed))
    spreads = {'L0_attn_norm1_w': (1.0, 0.6),
     'L0_attn_norm1_b': (0.0, 0.8),
     'L0_attn_norm2_w': (1.0, 0.6),
     'L0_attn_norm2_b': (0.0, 0.8),
     'L0_attn_b1': (0.0, 0.8),
     'L0_attn_b2': (0.0, 0.8),
     'L0_attn_ls1': (0.009999999776482582, 0.6),
     'L0_attn_ls2': (0.009999999776482582, 0.6)}
    factors = {'L0_attn_wq': 8.0,
     'L0_attn_wk': 8.0,
     'L0_attn_wv': 8.0,
     'L0_attn_wo': 8.0,
     'L0_attn_w1': 8.0,
     'L0_attn_w2': 8.0,
     'L0_ffn_gate_w': 8.0,
     'L0_ffn_w1': 8.0,
     'L0_ffn_w3': 8.0,
     'L0_ffn_w2': 8.0,
     'L0_ffn_sw1': 8.0,
     'L0_ffn_sw3': 8.0,
     'L0_ffn_sw2': 8.0}
    for name, (base, spread) in spreads.items():
        noise = np.random.default_rng([zlib.crc32(name.encode()), seed]).standard_normal(out[name].shape)
        drawn = base * np.exp(spread * noise) if base else spread * noise
        out[name] = jnp.asarray(drawn.astype(out[name].dtype))
    for name, factor in factors.items():
        out[name] = (out[name] * factor).astype(out[name].dtype)
    return out
```

```python
from contextlib import ExitStack

import numpy as np

import concourse.bass as bass
from concourse import mybir

F32 = mybir.dt.float32
BF16 = mybir.dt.bfloat16
ALU = mybir.AluOpType
ACT = mybir.ActivationFunctionType
AX = mybir.AxisListType

P = 128
NIMG, NCH, D = 8, 3, 256
T = 256
NT = T // P
KC = D // P
TILES = NIMG * NT
HEADS, HD = 16, 16
PAD = 32
WINDOW = 125
FFN = 1024
FC = FFN // P
EXPERTS, HID, TOPK = 16, 128, 4
BLK = 512
NBLK = NIMG * T // BLK
BT = BLK // P
GRAY = (0.2989, 0.587, 0.114)
EPS = 1e-5
MASKED = -1e30
NG = 4
UNITS = 3 * NG

STAGES = """
x_loaded0 x_loaded1 halo_loaded const_a const_b w_loaded0 w_loaded1 memset_done pool_carrier dve_carrier pad_zero eps_set
gray_part gray_ready halo_gray band_part band_ready conv_done abs_ready h_ready
stats0 mv0 lnv0 rs0 newton0 x1_ready stats1 mv1 lnv1 rs1 newton1 xhat_ready
xT_done hT_ready qk_done v_done rope_terms rope_ready v_ready qkT_done qkT_act qkT_dve
scores_done negmax_ready exp_done pT_done pT_copied pv_done recip_ready ao_ready
aoT_done aoT_copied wo_done wo_scaled x2_ready base_ready
stats2 mv2 lnv2 rs2 newton2 xhat2_ready x2T_done h2T_ready
ffn1_done gelu_done ffn2_done ffn_bias ffn_scaled h3_ready stats3 mv3 lnv3 rs3 newton3 xf_ready
xfT_done xfT_copied gate_done gate_max gate_shift gate_exp top_ready keys_set keys_ready replaced picked
sum_ready inv_ready combine_ready moe_h_done silu_done prod_ready moe_out_done acc_ready out_stored
""".split()


def build(nc, x, shift, scharr_rows, scharr, ident, ident16, mask0, mask1, rope_cos_t, rope_sin_t,
          wqkT, wvT, woT, ls1_rows, n1w, n1b, n2w, n2b, w1T, b1, w2T, b2_rows, ls2_rows,
          gateT, e13T, e2T, out):
    with ExitStack() as ctx:
        def sb(name, shape, dt=F32):
            return ctx.enter_context(nc.sbuf_tensor(name, shape, dt))

        def ps(name, shape):
            return ctx.enter_context(nc.psum_tensor(name, shape, F32))

        sem = {n: ctx.enter_context(nc.semaphore(n)) for n in STAGES}

        idf = sb("idf", [P, P])
        idb = sb("idb", [P, P], BF16)
        msk0 = sb("msk0", [P, P], BF16)
        msk1 = sb("msk1", [P, 2 * P], BF16)
        cosT = sb("cosT", [P, NT, 2, HD])
        sinT = sb("sinT", [P, NT, 2, HD])
        shf = sb("shf", [P, 3, P])
        schr = sb("schr", [P, 18])
        band = sb("band", [P, 2, 3, P])
        halo_band = sb("halo_band", [3, 2, NT, P])
        wqk = sb("wqk", [P, KC, 2 * D])
        wv = sb("wv", [P, KC, D])
        wo = sb("wo", [P, KC, D])
        ls1 = sb("ls1", [P, D])
        ls2 = sb("ls2", [P, D])
        b2 = sb("b2", [P, D])
        norm_wb = sb("norm_wb", [P, 4, KC])
        w1 = sb("w1", [P, KC, FFN])
        b1c = sb("b1c", [P, FC])
        w2 = sb("w2", [P, FC, D])
        gate = sb("gate", [P, KC, EXPERTS])
        epsc = sb("epsc", [P, 1])

        Hb = sb("Hb", [P, TILES, D])
        H2T = sb("H2T", [P, KC, NIMG * T])
        XFT = H2T

        xin = sb("xin", [P, 2, NCH, NT, D])
        gray = sb("gray", [P, 2, NT, D + 2])
        halo_all = sb("halo_all", [P, NT, NIMG, D])
        halo = halo_all[0:3]
        edge = sb("edge", [P, 2, NT, D])
        X1 = sb("X1", [P, TILES, D])
        xhat = sb("xhat", [P, NT, D])
        hT = sb("hT", [P, KC, T])
        rcos = sb("rcos", [P, 2, 2, HEADS, HD])
        rsin = sb("rsin", [P, 2, 2, HEADS, HD])
        qkp = sb("qkp", [P, NT, 2, HEADS, PAD])
        V = sb("V", [P, 2, NT, HEADS, HD + 1])
        QKT = sb("QKT", [P, 2, 2, NG, T])
        negmax = sb("negmax", [P, 2, UNITS, 4])
        prob = sb("prob", [P, 2, 512])
        pT = sb("pT", [P, 3, 4, P])
        rinv = sb("rinv", [P, NG, NT, 4])
        AO = sb("AO", [P, 2, NT, D])
        aoT = sb("aoT", [P, KC, T])
        wos = sb("wos", [P, NT, D])
        xhat2 = sb("xhat2", [P, NT, D])
        stats = sb("stats", [P, 3, NT, 6])
        mv = sb("mv", [P, 3, NT, 2])
        lnv = sb("lnv", [P, 3, NT])
        rs = sb("rs", [P, 3, NT])
        nw = sb("nw", [P, 3, 3, NT])

        G = [halo_all[:].rearrange("p t i d -> p (t i d)").rearrange("p (f k) -> p f k", f=FC),
             X1[:].rearrange("p k d -> p (k d)").rearrange("p (f k) -> p f k", f=FC)]
        fb = edge
        fs = rsin[:].rearrange("p u a h d -> p u (a h d)").rearrange("p u (t d) -> p u t d", t=2)
        stats3 = sb("stats3", [P, TILES, 6])
        mv3 = sb("mv3", [P, TILES, 2])
        lnv3 = sb("lnv3", [P, TILES])
        rs3 = sb("rs3", [P, TILES])
        nw3 = sb("nw3", [P, 3, TILES])
        XF = AO
        gmax = sb("gmax", [P, TILES])
        gsh = sb("gsh", [P, TILES, EXPERTS])
        gexp = sb("gexp", [P, TILES, EXPERTS + TOPK])
        top8 = sb("top8", [P, TILES, 8])
        keys = sb("keys", [P, TILES, 8])
        repl = sb("repl", [P, TILES, EXPERTS + TOPK])
        pick = sb("pick", [P, TILES, EXPERTS])
        tsum = sb("tsum", [P, TILES])
        tinv = sb("tinv", [P, TILES])
        comb = sb("comb", [P, EXPERTS + 1, TILES])

        halo_in = [a.rearrange("p (t i d) -> p t i d", t=NT, i=NIMG) for a in (
            H2T[0:3].rearrange("p c k -> p (c k)"), X1[0:3].rearrange("p k d -> p (k d)"),
            QKT[0:3].rearrange("p u a g k -> p (u a g k)"))]

        w13 = sb("w13", [P, 2, KC, 2 * HID])
        we2 = sb("we2", [P, 2, D])
        silu = prob
        hid = rcos[:].rearrange("p u a h d -> p u (a h d)")

        bank = [ps(f"bank{n}", [P, 512]) for n in range(8)]
        S, TP, O, Fb = bank[0:3], bank[3:5], bank[5], bank[6:8]
        Ov = O[:, 0:NT * 4 * (HD + 1)].rearrange("p (t h d) -> p t h d", t=NT, h=4)

        def w(eng, signal, value):
            if not (isinstance(value, int) and value <= 0):
                eng.wait_ge(signal, value)

        def wait_apart(eng, signal, value, carrier):
            eng.wait_ge(signal, value)
            if not isinstance(value, int):
                eng.sem_inc(carrier, 1)

        first_constants = (
            (shf[:], shift), (schr[:], scharr_rows), (idf[:], ident), (wqk[:], wqkT), (wv[:], wvT),
            (norm_wb[:, 0], n1w), (norm_wb[:, 1], n1b), (cosT[:], rope_cos_t), (sinT[:], rope_sin_t),
            (idb[:], ident16), (msk0[:], mask0), (msk1[:], mask1))
        later_constants = (
            (wo[:], woT), (ls1[:], ls1_rows), (norm_wb[:, 2], n2w), (norm_wb[:, 3], n2b),
            (w1[:], w1T), (b1c[:], b1), (w2[:], w2T), (b2[:], b2_rows), (ls2[:], ls2_rows), (gate[:], gateT))

        def at(n, count):
            return slice(n, n + count) if isinstance(n, int) else bass.ds(n, count)

        xv = x.rearrange("i c (t p) d -> p i c t d", p=P)
        ov = out.rearrange("i (t p) d -> p (i t) d", p=P)
        x_loaded = (sem["x_loaded0"], sem["x_loaded1"])
        w_loaded = (sem["w_loaded0"], sem["w_loaded1"])
        Y = [bank[4], bank[5]]
        gate_bank = bank[6]
        stats_sem = (sem["stats0"], sem["stats1"], sem["stats2"])
        mv_sem = (sem["mv0"], sem["mv1"], sem["mv2"])
        lnv_sem = (sem["lnv0"], sem["lnv1"], sem["lnv2"])
        rs_sem = (sem["rs0"], sem["rs1"], sem["rs2"])
        newton_sem = (sem["newton0"], sem["newton1"], sem["newton2"])
        CREDIT_GELU, CREDIT_FFN2, CREDIT_BIAS = 4, 4, 2
        CREDIT_PROD, CREDIT_OUT, CREDIT_ACC = 2, 4, 8
        CREDIT_XFT = 2

        block = ctx.enter_context(nc.Block())

        @block.sync
        def _(sp):
            def load_x(i, u):
                w(sp, sem["gray_ready"], i - 1)
                for c in range(NCH):
                    sp.dma_start(xin[:, u, c], xv[:, at(i, 1), c].rearrange("p i t d -> p (i t) d")
                                 ).then_inc(x_loaded[u], 16)

            load_x(0, 0)
            sp.wait_ge(sem["memset_done"], 4)
            for t in range(NT):
                row = P - t
                for dx, (to, frm, n) in enumerate(((1, 0, D - 1), (0, 0, D), (0, 1, D - 1))):
                    for c in range(NCH):
                        sp.dma_start(halo_in[c][dx:dx + 1, t, :, to:to + n],
                                     x[:, c, row:row + 1, frm:frm + n].rearrange("i a d -> a i d")
                                     ).then_inc(sem["halo_loaded"], 16)
                for f in range(2):
                    dy, col = (2, P - 1) if t == 0 else (0, 0)
                    sp.dma_start(halo_band[:, f, t, col:col + 1],
                                 scharr[f, 0, dy:dy + 1, :].rearrange("a d -> d a")).then_inc(sem["halo_loaded"], 16)
            for dst, src in first_constants:
                sp.dma_start(dst, src).then_inc(sem["const_a"], 16)
            load_x(1, 1)
            for dst, src in later_constants:
                sp.dma_start(dst, src).then_inc(sem["const_b"], 16)

            def load_expert(e, u):
                w(sp, sem["moe_h_done"], NBLK * (e - 1))
                if not isinstance(e, int) or e >= 2:
                    w(sp, sem["moe_out_done"], CREDIT_OUT + 2 * NBLK * (e - 1))
                sp.dma_start(w13[:, u], e13T[:, at(e, 1)].rearrange("p e c h -> p (e c) h")).then_inc(w_loaded[u], 16)
                sp.dma_start(we2[:, u], e2T[:, at(e, 1)].rearrange("p e d -> p (e d)")).then_inc(w_loaded[u], 16)

            load_expert(0, 0)
            load_expert(1, 1)
            with sp.Fori(1, NIMG // 2) as j:
                for u in range(2):
                    load_x(2 * j + u, u)
            with sp.Fori(1, EXPERTS // 2) as j:
                for u in range(2):
                    load_expert(2 * j + u, u)
            load_expert(EXPERTS, 0)
            for b in range(NBLK):
                sp.wait_ge(sem["acc_ready"], CREDIT_ACC + BT * (NBLK * EXPERTS + b + 1))
                sp.dma_start(ov[:, BT * b:BT * b + BT], Hb[:, BT * b:BT * b + BT]).then_inc(sem["out_stored"], 16)
            sp.wait_ge(sem["out_stored"], 16 * NBLK)

        @block.gpsimd
        def _(pool):
            for c in range(NCH):
                pool.memset(halo_in[c], 0.0).then_inc(sem["memset_done"], 1)
            pool.memset(halo_band[:], 0.0).then_inc(sem["memset_done"], 1)
            pool.memset(gray[:], 0.0).then_inc(sem["memset_done"], 1)
            pool.wait_ge(sem["memset_done"], 5)

            def make_gray(i, u):
                w(pool, sem["conv_done"], 2 * (i - 1))
                wait_apart(pool, x_loaded[u], 8 * NCH * (i - u) + 16 * NCH, sem["pool_carrier"])
                g = gray[:, u, :, 1:D + 1]
                for c in range(NCH):
                    pool.tensor_scalar(xin[:, u, c], xin[:, u, c], GRAY[c], None, ALU.mult).then_inc(sem["gray_part"], 1)
                pool.wait_ge(sem["gray_part"], 4 * i + 3)
                pool.tensor_tensor(g, xin[:, u, 0], xin[:, u, 1], ALU.add).then_inc(sem["gray_part"], 1)
                pool.wait_ge(sem["gray_part"], 4 * i + 4)
                pool.tensor_tensor(g, g, xin[:, u, 2], ALU.add).then_inc(sem["gray_ready"], 1)

            def rope_add(m, t):
                pool.wait_ge(sem["rope_terms"], 3 * (NT * m + t + 1))
                w(pool, sem["qkT_done"], 4 * m)
                pool.tensor_tensor(qkp[:, t, :, :, 0:HD], rcos[:, t], rsin[:, t], ALU.add).then_inc(sem["rope_ready"], 1)

            def residual(l):
                pool.wait_ge(sem["wo_scaled"], l + 1)
                x1 = X1[:, at(NT * l, NT)]
                pool.tensor_tensor(x1, wos[:], x1, ALU.add).then_inc(sem["x2_ready"], 1)
                pool.wait_ge(sem["x2_ready"], l + 1)
                h = Hb[:, at(NT * l, NT)]
                pool.tensor_tensor(h, h, x1, ALU.add).then_inc(sem["base_ready"], 1)

            def step(i, u, front, tail, gray_next):
                if gray_next:
                    make_gray(i + 2, u)
                if tail:
                    residual(i - 1)
                if front:
                    for t in range(NT):
                        rope_add(i + 1, t)

            make_gray(0, 0)
            pool.memset(qkp[:], 0.0).then_inc(sem["pad_zero"], 1)
            pool.memset(V[:], 1.0).then_inc(sem["pad_zero"], 1)
            make_gray(1, 1)
            pool.wait_ge(sem["pad_zero"], 2)
            for t in range(NT):
                rope_add(0, t)
            step(0, 0, True, False, True)
            with pool.Fori(0, (NIMG - 4) // 2) as j:
                step(2 * j + 1, 1, True, True, True)
                step(2 * j + 2, 0, True, True, True)
            step(NIMG - 3, 1, True, True, True)
            step(NIMG - 2, 0, True, True, False)
            residual(NIMG - 2)
            residual(NIMG - 1)

        @block.tensor
        def _(pe):
            def conv(m, v):
                pe.wait_ge(sem["gray_ready"], m + 1)
                w(pe, sem["qkT_act"], 2 * m)
                w(pe, sem["qkT_dve"], 2 * m)
                for f in range(2):
                    for dx in range(3):
                        pe.matmul(Fb[f][:], band[:, f, dx], gray[:, v, :, dx:dx + D], start=(dx == 0), stop=False)
                    for t in range(NT):
                        mm = pe.matmul(Fb[f][:, t * D:t * D + D], halo_band[:, f, t],
                                       halo[:, t, at(m, 1)].rearrange("p a d -> p (a d)"),
                                       start=False, stop=(t == NT - 1))
                    mm.then_inc(sem["conv_done"], 1)

            def turn(dst, src):
                for c in range(KC):
                    for t in range(NT):
                        mm = pe.transpose(dst[:, c * T + t * P:c * T + t * P + P], src[:, t, c * P:c * P + P], idf[:])
                return mm

            def project(dst, src, weights):
                for t in range(NT):
                    for c in range(KC):
                        mm = pe.matmul(dst[:, t * D:t * D + D], src[:, c, t * P:t * P + P], weights[:, c],
                                       start=(c == 0), stop=(c == KC - 1))
                return mm

            def norm_turn(m):
                pe.wait_ge(sem["xhat_ready"], NT * (m + 1))
                w(pe, sem["aoT_copied"], m - 1)
                turn(Fb[0], xhat).then_inc(sem["xT_done"], 1)

            def project_qk(m, t):
                if t == 0:
                    pe.wait_ge(sem["hT_ready"], KC * (m + 1))
                    w(pe, sem["wo_scaled"], m - 1)
                for c in range(KC):
                    mm = pe.matmul(Fb[1 - t][:], hT[:, c, t * P:t * P + P], wqk[:, c],
                                   start=(c == 0), stop=(c == KC - 1))
                mm.then_inc(sem["qk_done"], 1)

            def project_v(m):
                pe.wait_ge(sem["rope_terms"], 6 * m + 3)
                project(Fb[1], hT, wv).then_inc(sem["v_done"], 1)

            def turn_qk(m, n):
                t, qk = n // 2, n % 2
                pe.wait_ge(sem["rope_ready"], NT * m + t + 1)
                if n == 0:
                    pe.wait_ge(sem["v_ready"], m + 1)
                if n == 1:
                    pe.wait_ge(sem["rope_terms"], 6 * m + 6)
                    w(pe, sem["h2T_ready"], KC * (m - 1))
                if n == 2:
                    pe.wait_ge(sem["qkT_act"], 2 * m + 1)
                if n == 3:
                    pe.wait_ge(sem["qkT_dve"], 2 * m + 1)
                for g in range(NG):
                    mm = pe.transpose(Fb[1 - n % 2][:, g * P:g * P + P],
                                      qkp[:, t, qk, 4 * g:4 * g + 4].rearrange("p h d -> p (h d)"), idf[:])
                mm.then_inc(sem["qkT_done"], 1)

            def heads_out(l, v, front):
                pe.wait_ge(sem["ao_ready"], NG * (l + 1))
                if front:
                    pe.wait_ge(sem["abs_ready"], 2 * (l + 3))
                else:
                    pe.wait_ge(sem["h2T_ready"], KC * l)
                turn(Fb[0], AO[:, v]).then_inc(sem["aoT_done"], 1)

            def project_out(l):
                pe.wait_ge(sem["aoT_copied"], l + 1)
                w(pe, sem["wo_scaled"], l)
                project(Fb[1], aoT, wo).then_inc(sem["wo_done"], 1)

            def norm2_turn(l, front):
                pe.wait_ge(sem["xhat2_ready"], NT * (l + 1))
                if front:
                    pe.wait_ge(sem["rope_terms"], 6 * (l + 3))
                turn(Fb[0], xhat2).then_inc(sem["x2T_done"], 1)

            def scores(i, u, n):
                g, k = n // 3, n % 3
                if n == 0:
                    pe.wait_ge(sem["qkT_act"], 2 * (i + 1))
                    pe.wait_ge(sem["qkT_dve"], 2 * (i + 1))
                w(pe, sem["exp_done"], UNITS * i + n - 2)
                heads = range(4) if k == 0 else range(2 * k - 2, 2 * k)
                keys = P if k == 0 else 2 * P
                m = (msk0 if k == 0 else msk1)[:].unsqueeze(1).broadcast_to([P, len(heads), keys])
                pe.matmul(S[k][:].rearrange("p (h k) -> p h k", k=keys), idb[:], m, start=True, stop=False)
                r = slice(PAD * g, PAD * g + PAD)
                for slot, j in enumerate(heads):
                    mm = pe.matmul(S[k][:, slot * keys:slot * keys + keys],
                                   QKT[r, u, 0, j, 0:P] if k == 0 else QKT[r, u, 0, j, P:T],
                                   QKT[r, u, 1, j, 0:keys], start=False, stop=(slot == len(heads) - 1))
                mm.then_inc(sem["scores_done"], 1)

            def turn_probs(i, n):
                pe.wait_ge(sem["exp_done"], UNITS * i + n + 1)
                w(pe, sem["pT_copied"], UNITS * i + n - 1)
                for q in range(4):
                    mm = pe.transpose(TP[n % 2][:, q * P:q * P + P], prob[:, n % 2, q * P:q * P + P], idf[:])
                mm.then_inc(sem["pT_done"], 1)

            def attend(i, u, n):
                g, k = n // 3, n % 3
                pe.wait_ge(sem["pT_copied"], UNITS * i + n + 1)
                if k == 0:
                    w(pe, sem["ao_ready"], NG * i + g)
                    if n == 0:
                        pe.wait_ge(sem["v_ready"], i + 1)
                    for j in range(4):
                        mm = pe.matmul(Ov[:, 0, j], pT[:, n % 3, j], V[:, u, 0, 4 * j + g], start=True, stop=True)
                else:
                    for slot in range(2):
                        j = 2 * k - 2 + slot
                        for t in range(NT):
                            mm = pe.matmul(Ov[:, 1, j], pT[:, n % 3, 2 * slot + t], V[:, u, t, 4 * j + g],
                                           start=(t == 0), stop=(t == NT - 1))
                mm.then_inc(sem["pv_done"], 1)

            def step(i, u, front, tail):
                scores(i, u, 0)
                scores(i, u, 1)
                for n in range(UNITS):
                    if n + 2 < UNITS:
                        scores(i, u, n + 2)
                    if front and n == 0:
                        conv(i + 1, 1 - u)
                    if tail and n == 1:
                        heads_out(i - 1, 1 - u, front)
                    if tail and n == 2:
                        project_out(i - 1)
                    if front and n == 3:
                        norm_turn(i + 1)
                    if front and n == 4:
                        project_qk(i + 1, 0)
                        project_qk(i + 1, 1)
                    if front and n == 5:
                        project_v(i + 1)
                    if tail and n == 7:
                        norm2_turn(i - 1, front)
                    if front and n >= 8:
                        turn_qk(i + 1, n - 8)
                    turn_probs(i, n)
                    if n >= 1:
                        attend(i, u, n - 1)
                attend(i, u, UNITS - 1)

            pe.wait_ge(sem["const_a"], 16 * len(first_constants))
            pe.wait_ge(sem["band_ready"], 6)
            pe.wait_ge(sem["halo_gray"], 3)
            conv(0, 0)
            norm_turn(0)
            project_qk(0, 0)
            project_qk(0, 1)
            project_v(0)
            for n in range(4):
                turn_qk(0, n)
            pe.wait_ge(sem["const_b"], 16 * len(later_constants))
            step(0, 0, True, False)
            with pe.Fori(0, (NIMG - 2) // 2) as j:
                step(2 * j + 1, 1, True, True)
                step(2 * j + 2, 0, True, True)
            step(NIMG - 1, 1, False, True)
            heads_out(NIMG - 1, 1, False)
            project_out(NIMG - 1)
            norm2_turn(NIMG - 1, False)

            def ffn(b, u):
                for f in range(FC):
                    pe.wait_ge(sem["gelu_done"], CREDIT_GELU + FC * b + f - 3)
                    for c in range(KC):
                        mm = pe.matmul(bank[f % 4][:], w1[:, c, f * P:f * P + P], H2T[:, c, at(b * BLK, BLK)],
                                       start=(c == 0), stop=(c == KC - 1))
                    mm.then_inc(sem["ffn1_done"], 1)
                pe.wait_ge(sem["gelu_done"], CREDIT_GELU + FC * (b + 1))
                for half in range(2):
                    pe.wait_ge(sem["ffn_bias"], CREDIT_BIAS + 2 * b + half - 1)
                    for t in range(2):
                        for f in range(FC):
                            k = (2 * half + t) * P
                            mm = pe.matmul(Y[half][:, t * D:t * D + D], G[u][:, f, k:k + P], w2[:, f],
                                           start=(f == 0), stop=(f == FC - 1))
                    mm.then_inc(sem["ffn2_done"], 1)

            pe.sem_inc(sem["ffn2_done"], CREDIT_FFN2)
            pe.wait_ge(sem["h2T_ready"], KC * NIMG)
            with pe.Fori(0, NBLK // 2) as j:
                ffn(2 * j, 0)
                ffn(2 * j + 1, 1)

            with pe.Fori(0, NIMG // 2) as j:
                for u in range(2):
                    k = 2 * j + u
                    pe.wait_ge(sem["xf_ready"], NT * (k + 1))
                    pe.wait_ge(sem["xfT_copied"], CREDIT_XFT + k - 1)
                    turn(bank[u], XF[:, u]).then_inc(sem["xfT_done"], 1)
            pe.wait_ge(sem["xfT_copied"], CREDIT_XFT + NIMG)
            for k in range(TILES):
                for c in range(KC):
                    mm = pe.matmul(gate_bank[:, k * EXPERTS:k * EXPERTS + EXPERTS], XFT[:, c, k * P:k * P + P],
                                   gate[:, c], start=(c == 0), stop=(c == KC - 1))
            mm.then_inc(sem["gate_done"], 1)

            def moe_hidden(n, q):
                b, u = q % NBLK, q // NBLK
                if b == 0:
                    pe.wait_ge(w_loaded[u], 4 * n - 16 * u + 32)
                pe.wait_ge(sem["prod_ready"], CREDIT_PROD + n - 1)
                for which in range(2):
                    for c in range(KC):
                        mm = pe.matmul(bank[2 * which + q % 2][:], w13[:, u, c, which * HID:which * HID + HID],
                                       XFT[:, c, b * BLK:b * BLK + BLK], start=(c == 0), stop=(c == KC - 1))
                mm.then_inc(sem["moe_h_done"], 1)

            def moe_out(n, q):
                pe.wait_ge(sem["prod_ready"], CREDIT_PROD + n + 1)
                for half in range(2):
                    pe.wait_ge(sem["acc_ready"], CREDIT_ACC + BT * (n - 2) + 2 * half + 2)
                    for t in range(2):
                        k = (2 * half + t) * P
                        mm = pe.matmul(bank[4 + 2 * (q % 2) + half][:, t * D:t * D + D],
                                       hid[:, q % 2, k:k + P], we2[:, q // NBLK], start=True, stop=True)
                    mm.then_inc(sem["moe_out_done"], 1)

            pe.sem_inc(sem["moe_out_done"], CREDIT_OUT)
            moe_hidden(0, 0)
            with pe.Fori(0, EXPERTS // 2) as j:
                for q in range(2 * NBLK):
                    moe_hidden(2 * NBLK * j + q + 1, (q + 1) % (2 * NBLK))
                    moe_out(2 * NBLK * j + q, q)
            for q in range(NBLK):
                if q + 1 < NBLK:
                    moe_hidden(NBLK * EXPERTS + q + 1, q + 1)
                moe_out(NBLK * EXPERTS + q, q)

        @block.scalar
        def _(act):
            def edges(m):
                w(act, sem["h_ready"], m)
                for f in range(2):
                    act.wait_ge(sem["conv_done"], 2 * m + f + 1)
                    act.activation(edge[:, f], Fb[f][:].rearrange("p (t d) -> p t d", t=NT), ACT.Abs,
                                   scale=0.5).then_inc(sem["abs_ready"], 1)

            def rstd(k, m):
                act.wait_ge(mv_sem[k], NT * (m + 1))
                act.activation(lnv[:, k], mv[:, k, :, 1], ACT.Ln, bias=epsc[:]).then_inc(lnv_sem[k], 1)
                act.wait_ge(lnv_sem[k], m + 1)
                act.activation(rs[:, k], lnv[:, k], ACT.Exp, scale=-0.5).then_inc(rs_sem[k], 1)

            def norm_copy(m):
                act.wait_ge(sem["xT_done"], m + 1)
                w(act, sem["v_done"], m)
                for c in range(KC):
                    act.activation(hT[:, c], Fb[0][:, c * T:c * T + T], ACT.Identity,
                                   scale=norm_wb[:, 0, c:c + 1], bias=norm_wb[:, 1, c:c + 1]).then_inc(sem["hT_ready"], 1)

            def v_copy(m, v):
                act.wait_ge(sem["v_done"], m + 1)
                w(act, sem["pv_done"], UNITS * (m - 1))
                act.activation(V[:, v, :, :, 0:HD], Fb[1][:].rearrange("p (t h d) -> p t h d", t=NT, h=HEADS),
                               ACT.Identity).then_inc(sem["v_ready"], 1)

            def qkT_copy(m, v, n):
                t = n // 2
                act.wait_ge(sem["qkT_done"], 4 * m + n + 1)
                act.activation(QKT[:, v, 0, :, t * P:t * P + P], Fb[1][:].rearrange("p (g k) -> p g k", g=NG),
                               ACT.Identity).then_inc(sem["qkT_act"], 1)

            def ao_copy(l):
                act.wait_ge(sem["aoT_done"], l + 1)
                w(act, sem["wo_done"], l)
                act.activation(aoT[:], Fb[0][:].rearrange("p (c k) -> p c k", c=KC), ACT.Identity
                               ).then_inc(sem["aoT_copied"], 1)

            def norm2_copy(l):
                act.wait_ge(sem["x2T_done"], l + 1)
                for c in range(KC):
                    act.activation(H2T[:, c, at(l * T, T)], Fb[0][:, c * T:c * T + T], ACT.Identity,
                                   scale=norm_wb[:, 2, c:c + 1], bias=norm_wb[:, 3, c:c + 1]).then_inc(sem["h2T_ready"], 1)

            def exps(i, u, n):
                k = n % 3
                heads, keys = (4, P) if k == 0 else (2, 2 * P)
                act.wait_ge(sem["negmax_ready"], UNITS * i + n + 1)
                w(act, sem["pT_done"], UNITS * i + n - 1)
                for h in range(heads):
                    a = act.activation(prob[:, n % 2, h * keys:h * keys + keys], S[k][:, h * keys:h * keys + keys],
                                       ACT.Exp, bias=negmax[:, u, n, h:h + 1])
                a.then_inc(sem["exp_done"], 1)

            def step(i, u, front, tail):
                for n in range(UNITS):
                    exps(i, u, n)
                    if front and n == 0:
                        edges(i + 1)
                    if front and n == 1:
                        rstd(0, i + 1)
                    if tail and n == 1:
                        ao_copy(i - 1)
                    if front and n == 2:
                        rstd(1, i + 1)
                    if front and n == 3:
                        norm_copy(i + 1)
                    if front and n == 5:
                        v_copy(i + 1, 1 - u)
                    if tail and n == 5:
                        rstd(2, i - 1)
                    if tail and n == 7:
                        norm2_copy(i - 1)
                    if front and n in (8, 10):
                        qkT_copy(i + 1, 1 - u, n - 8)

            act.wait_ge(sem["const_a"], 16 * len(first_constants))
            act.wait_ge(sem["eps_set"], 1)
            edges(0)
            rstd(0, 0)
            rstd(1, 0)
            norm_copy(0)
            act.wait_ge(sem["pad_zero"], 2)
            v_copy(0, 0)
            qkT_copy(0, 0, 0)
            qkT_copy(0, 0, 2)
            act.wait_ge(sem["const_b"], 16 * len(later_constants))
            step(0, 0, True, False)
            with act.Fori(0, (NIMG - 2) // 2) as j:
                step(2 * j + 1, 1, True, True)
                step(2 * j + 2, 0, True, True)
            step(NIMG - 1, 1, False, True)
            ao_copy(NIMG - 1)
            rstd(2, NIMG - 1)
            norm2_copy(NIMG - 1)

            act.wait_ge(sem["base_ready"], NIMG)
            act.sem_inc(sem["gelu_done"], CREDIT_GELU)
            with act.Fori(0, NBLK // 2) as j:
                for u in range(2):
                    b = 2 * j + u
                    act.wait_ge(sem["ffn2_done"], CREDIT_FFN2 + 2 * (b - 1))
                    for f in range(FC):
                        act.wait_ge(sem["ffn1_done"], FC * b + f + 1)
                        act.activation(G[u][:, f], bank[f % 4][:], ACT.Gelu, bias=b1c[:, f:f + 1]
                                       ).then_inc(sem["gelu_done"], 1)

            act.sem_inc(sem["xfT_copied"], CREDIT_XFT)
            act.wait_ge(sem["mv3"], TILES)
            act.activation(lnv3[:], mv3[:, :, 1], ACT.Ln, bias=epsc[:]).then_inc(sem["lnv3"], 1)
            act.wait_ge(sem["lnv3"], 1)
            act.activation(rs3[:], lnv3[:], ACT.Exp, scale=-0.5).then_inc(sem["rs3"], 1)
            with act.Fori(0, NIMG // 2) as j:
                for u in range(2):
                    k = 2 * j + u
                    act.wait_ge(sem["xfT_done"], k + 1)
                    act.activation(XFT[:, :, at(k * T, T)], bank[u][:].rearrange("p (c k) -> p c k", c=KC),
                                   ACT.Identity).then_inc(sem["xfT_copied"], 1)
            act.wait_ge(sem["gate_shift"], 1)
            act.activation(gexp[:, :, 0:EXPERTS], gsh[:], ACT.Exp).then_inc(sem["gate_exp"], 1)

            def gated(n, q):
                act.wait_ge(sem["moe_h_done"], n + 1)
                act.wait_ge(sem["prod_ready"], CREDIT_PROD + n - 1)
                act.activation(silu[:, q % 2], bank[q % 2][:], ACT.Silu).then_inc(sem["silu_done"], 1)

            with act.Fori(0, EXPERTS // 2) as j:
                for q in range(2 * NBLK):
                    gated(2 * NBLK * j + q, q)
            for q in range(NBLK):
                gated(NBLK * EXPERTS + q, q)

        @block.vector
        def _(dve):
            def norm_stats(k, m, src):
                for t in range(NT):
                    dve.bn_stats(stats[:, k, t], src(t)).then_inc(stats_sem[k], 1)
                wait_apart(dve, stats_sem[k], NT * (m + 1), sem["dve_carrier"])
                for t in range(NT):
                    dve.bn_aggr(mv[:, k, t], stats[:, k, t]).then_inc(mv_sem[k], 1)

            def normalize(k, m, src, dst, done):
                y, v = rs[:, k], mv[:, k, :, 1]
                dve.wait_ge(rs_sem[k], m + 1)
                dve.scalar_tensor_tensor(out=nw[:, k, 0], in0=v, scalar=EPS, in1=y, op0=ALU.add, op1=ALU.mult
                                         ).then_inc(newton_sem[k], 1)
                dve.wait_ge(newton_sem[k], 3 * m + 1)
                dve.scalar_tensor_tensor(out=nw[:, k, 1], in0=nw[:, k, 0], scalar=-0.5, in1=y,
                                         op0=ALU.mult, op1=ALU.mult).then_inc(newton_sem[k], 1)
                dve.wait_ge(newton_sem[k], 3 * m + 2)
                dve.scalar_tensor_tensor(out=nw[:, k, 2], in0=nw[:, k, 1], scalar=1.5, in1=y,
                                         op0=ALU.add, op1=ALU.mult).then_inc(newton_sem[k], 1)
                dve.wait_ge(newton_sem[k], 3 * m + 3)
                for t in range(NT):
                    dve.tensor_scalar(dst(t), src(t), mv[:, k, t, 0:1], nw[:, k, 2, t:t + 1],
                                      ALU.subtract, ALU.mult).then_inc(done, 1)

            def tile_of(buf, m):
                return lambda t: buf[:, at(NT * m + t, 1)].rearrange("p a d -> p (a d)")

            def edge_sum(m):
                dve.wait_ge(sem["abs_ready"], 2 * (m + 1))
                dve.tensor_tensor(Hb[:, at(NT * m, NT)], edge[:, 0], edge[:, 1], ALU.add).then_inc(sem["h_ready"], 1)
                wait_apart(dve, sem["h_ready"], m + 1, sem["dve_carrier"])
                norm_stats(0, m, tile_of(Hb, m))

            def first_norm(m):
                normalize(0, m, tile_of(Hb, m), tile_of(X1, m), sem["x1_ready"])
                wait_apart(dve, sem["x1_ready"], NT * (m + 1), sem["dve_carrier"])
                norm_stats(1, m, tile_of(X1, m))

            def second_norm(m):
                w(dve, sem["xT_done"], m)
                normalize(1, m, tile_of(X1, m), lambda t: xhat[:, t], sem["xhat_ready"])

            def rope(m, t):
                dve.wait_ge(sem["qk_done"], NT * m + t + 1)
                w(dve, sem["rope_ready"], NT * (m - 1) + t + 1)
                qk = Fb[1 - t][:].rearrange("p (a h d) -> p a h d", a=2, h=HEADS)
                half = HD // 2
                cos = cosT[:, t].unsqueeze(2).broadcast_to([P, 2, HEADS, HD])
                sin = sinT[:, t].unsqueeze(2).broadcast_to([P, 2, HEADS, HD])
                dve.tensor_tensor(rcos[:, t], qk, cos, ALU.mult).then_inc(sem["rope_terms"], 1)
                dve.tensor_tensor(rsin[:, t, :, :, 0:half], qk[:, :, :, half:HD], sin[:, :, :, 0:half], ALU.mult
                                  ).then_inc(sem["rope_terms"], 1)
                dve.tensor_tensor(rsin[:, t, :, :, half:HD], qk[:, :, :, 0:half], sin[:, :, :, half:HD], ALU.mult
                                  ).then_inc(sem["rope_terms"], 1)

            def qkT_copy(m, v, n):
                t = n // 2
                dve.wait_ge(sem["qkT_done"], 4 * m + n + 1)
                dve.tensor_copy(QKT[:, v, 1, :, t * P:t * P + P], Fb[0][:].rearrange("p (g k) -> p g k", g=NG)
                                ).then_inc(sem["qkT_dve"], 1)

            def scale_out(l):
                dve.wait_ge(sem["wo_done"], l + 1)
                w(dve, sem["x2_ready"], l)
                dve.tensor_tensor(wos[:], Fb[1][:].rearrange("p (t d) -> p t d", t=NT),
                                  ls1[:].unsqueeze(1).broadcast_to([P, NT, D]), ALU.mult).then_inc(sem["wo_scaled"], 1)

            def third_stats(l):
                wait_apart(dve, sem["x2_ready"], l + 1, sem["dve_carrier"])
                norm_stats(2, l, tile_of(X1, l))

            def third_norm(l):
                w(dve, sem["x2T_done"], l)
                normalize(2, l, tile_of(X1, l), lambda t: xhat2[:, t], sem["xhat2_ready"])

            def row_max(i, u, n):
                k = n % 3
                heads = 4 if k == 0 else 2
                dve.wait_ge(sem["scores_done"], UNITS * i + n + 1)
                dve.tensor_reduce(negmax[:, u, n, 0:heads], S[k][:].rearrange("p (h k) -> p h k", h=heads),
                                  AX.X, ALU.max, negate=True).then_inc(sem["negmax_ready"], 1)

            def pT_copy(i, n):
                dve.wait_ge(sem["pT_done"], UNITS * i + n + 1)
                w(dve, sem["pv_done"], UNITS * i + n - 2)
                dve.tensor_copy(pT[:, n % 3], TP[n % 2][:].rearrange("p (q k) -> p q k", q=4)).then_inc(sem["pT_copied"], 1)

            def divide(i, u, g):
                dve.wait_ge(sem["pv_done"], UNITS * i + 3 * (g + 1))
                dve.reciprocal(rinv[:, g], Ov[:, :, :, HD]).then_inc(sem["recip_ready"], 1)
                if g == 0:
                    w(dve, sem["aoT_done"], i - 1)
                dve.wait_ge(sem["recip_ready"], NG * i + g + 1)
                ao = AO[:, u].rearrange("p t (h g d) -> p t h g d", g=NG, d=HD)[:, :, :, g]
                dve.tensor_tensor(ao, Ov[:, :, :, 0:HD], rinv[:, g].unsqueeze(3).broadcast_to([P, NT, 4, HD]),
                                  ALU.mult).then_inc(sem["ao_ready"], 1)

            def step(i, u, front, tail):
                row_max(i, u, 0)
                row_max(i, u, 1)
                for n in range(UNITS):
                    if n + 2 < UNITS:
                        row_max(i, u, n + 2)
                    if front and n == 0:
                        edge_sum(i + 1)
                    if front and n == 1:
                        first_norm(i + 1)
                    if front and n == 2:
                        second_norm(i + 1)
                    if tail and n == 2:
                        scale_out(i - 1)
                    if tail and n == 4:
                        third_stats(i - 1)
                    if front and n in (4, 5):
                        rope(i + 1, n - 4)
                    if tail and n == 6:
                        third_norm(i - 1)
                    if front and n in (9, 11):
                        qkT_copy(i + 1, 1 - u, n - 8)
                    pT_copy(i, n)
                    if n % 3 == 0 and n:
                        divide(i, u, n // 3 - 1)
                divide(i, u, NG - 1)

            dve.memset(epsc[:], EPS).then_inc(sem["eps_set"], 1)
            dve.memset(comb[:, EXPERTS], 1.0).then_inc(sem["keys_set"], 1)
            for k in range(TOPK):
                dve.memset(gexp[:, :, EXPERTS + k:EXPERTS + k + 1], -1.0 - k).then_inc(sem["keys_set"], 1)
                dve.memset(keys[:, :, TOPK + k:TOPK + k + 1], -1.0 - k).then_inc(sem["keys_set"], 1)
            dve.wait_ge(sem["const_a"], 16 * len(first_constants))
            for dy in range(3):
                if dy:
                    dve.wait_ge(sem["band_part"], 6 * dy)
                for f in range(2):
                    for dx in range(3):
                        tap = schr[:, 9 * f + 3 * dy + dx:9 * f + 3 * dy + dx + 1]
                        o = band[:, f, dx]
                        done = sem["band_ready"] if dy == 2 else sem["band_part"]
                        if dy == 0:
                            dve.tensor_scalar(o, shf[:, dy], tap, None, ALU.mult).then_inc(done, 1)
                        else:
                            dve.scalar_tensor_tensor(out=o, in0=shf[:, dy], scalar=tap, in1=o,
                                                     op0=ALU.mult, op1=ALU.add).then_inc(done, 1)
            dve.wait_ge(sem["halo_loaded"], 16 * 22)
            dve.tensor_scalar(halo[:], halo_in[0], GRAY[0], None, ALU.mult).then_inc(sem["halo_gray"], 1)
            for c in (1, 2):
                dve.wait_ge(sem["halo_gray"], c)
                dve.scalar_tensor_tensor(out=halo[:], in0=halo_in[c], scalar=GRAY[c], in1=halo[:],
                                         op0=ALU.mult, op1=ALU.add).then_inc(sem["halo_gray"], 1)
            edge_sum(0)
            first_norm(0)
            second_norm(0)
            rope(0, 0)
            rope(0, 1)
            qkT_copy(0, 0, 1)
            qkT_copy(0, 0, 3)
            dve.wait_ge(sem["const_b"], 16 * len(later_constants))
            step(0, 0, True, False)
            with dve.Fori(0, (NIMG - 2) // 2) as j:
                step(2 * j + 1, 1, True, True)
                step(2 * j + 2, 0, True, True)
            step(NIMG - 1, 1, False, True)
            scale_out(NIMG - 1)
            third_stats(NIMG - 1)
            third_norm(NIMG - 1)

            dve.sem_inc(sem["ffn_bias"], CREDIT_BIAS)
            dve.wait_ge(sem["base_ready"], NIMG)
            with dve.Fori(0, NBLK // 2) as j:
                for q in range(4):
                    r = 4 * j + q
                    dve.wait_ge(sem["ffn2_done"], CREDIT_FFN2 + r + 1)
                    y = fb[:, q % 2]
                    dve.tensor_tensor(y, Y[q % 2][:].rearrange("p (t d) -> p t d", t=2),
                                      b2[:].unsqueeze(1).broadcast_to([P, 2, D]), ALU.add).then_inc(sem["ffn_bias"], 1)
                    dve.wait_ge(sem["ffn_bias"], CREDIT_BIAS + r + 1)
                    dve.tensor_tensor(fs[:, q % 2], y, ls2[:].unsqueeze(1).broadcast_to([P, 2, D]),
                                      ALU.mult).then_inc(sem["ffn_scaled"], 1)
                    dve.wait_ge(sem["ffn_scaled"], r + 1)
                    h = Hb[:, at(2 * r, 2)]
                    dve.tensor_tensor(h, h, fs[:, q % 2], ALU.add).then_inc(sem["h3_ready"], 1)
                    wait_apart(dve, sem["h3_ready"], r + 1, sem["dve_carrier"])
                    for t in range(2):
                        dve.bn_stats(stats3[:, at(2 * r + t, 1)].rearrange("p a d -> p (a d)"),
                                     tile_of(Hb, r)(t)).then_inc(sem["stats3"], 1)

            dve.wait_ge(sem["stats3"], TILES)
            for k in range(TILES):
                dve.bn_aggr(mv3[:, k], stats3[:, k]).then_inc(sem["mv3"], 1)
            y, v = rs3[:], mv3[:, :, 1]
            dve.wait_ge(sem["rs3"], 1)
            dve.scalar_tensor_tensor(out=nw3[:, 0], in0=v, scalar=EPS, in1=y, op0=ALU.add, op1=ALU.mult
                                     ).then_inc(sem["newton3"], 1)
            dve.wait_ge(sem["newton3"], 1)
            dve.scalar_tensor_tensor(out=nw3[:, 1], in0=nw3[:, 0], scalar=-0.5, in1=y, op0=ALU.mult, op1=ALU.mult
                                     ).then_inc(sem["newton3"], 1)
            dve.wait_ge(sem["newton3"], 2)
            dve.scalar_tensor_tensor(out=nw3[:, 2], in0=nw3[:, 1], scalar=1.5, in1=y, op0=ALU.add, op1=ALU.mult
                                     ).then_inc(sem["newton3"], 1)
            dve.wait_ge(sem["newton3"], 3)
            for k in range(NIMG):
                w(dve, sem["xfT_done"], k - 1)
                for t in range(NT):
                    n = NT * k + t
                    dve.tensor_scalar(XF[:, k % 2, t], Hb[:, n], mv3[:, n, 0:1], nw3[:, 2, n:n + 1],
                                      ALU.subtract, ALU.mult).then_inc(sem["xf_ready"], 1)
            logits = gate_bank[:, 0:TILES * EXPERTS].rearrange("p (k e) -> p k e", e=EXPERTS)
            dve.wait_ge(sem["gate_done"], 1)
            dve.tensor_reduce(gmax[:], logits, AX.X, ALU.max).then_inc(sem["gate_max"], 1)
            dve.wait_ge(sem["gate_max"], 1)
            dve.tensor_tensor(gsh[:], logits, gmax[:].unsqueeze(2).broadcast_to([P, TILES, EXPERTS]),
                              ALU.subtract).then_inc(sem["gate_shift"], 1)
            dve.wait_ge(sem["gate_exp"], 1)
            for k in range(TILES):
                dve.max(top8[:, k], gexp[:, k, 0:EXPERTS]).then_inc(sem["top_ready"], 1)
            dve.wait_ge(sem["top_ready"], TILES)
            dve.wait_ge(sem["keys_set"], 9)
            dve.tensor_copy(keys[:, :, 0:TOPK], top8[:, :, 0:TOPK]).then_inc(sem["keys_ready"], 1)
            dve.tensor_reduce(tsum[:], top8[:, :, 0:TOPK], AX.X, ALU.add).then_inc(sem["sum_ready"], 1)
            dve.wait_ge(sem["keys_ready"], 1)
            for k in range(TILES):
                dve.match_replace(repl[:, k], keys[:, k], gexp[:, k], -9.0).then_inc(sem["replaced"], 1)
            dve.wait_ge(sem["sum_ready"], 1)
            dve.reciprocal(tinv[:], tsum[:]).then_inc(sem["inv_ready"], 1)
            dve.wait_ge(sem["replaced"], TILES)
            dve.scalar_tensor_tensor(out=pick[:], in0=repl[:, :, 0:EXPERTS], scalar=-8.0, in1=gexp[:, :, 0:EXPERTS],
                                     op0=ALU.is_lt, op1=ALU.mult).then_inc(sem["picked"], 1)
            dve.wait_ge(sem["picked"], 1)
            dve.wait_ge(sem["inv_ready"], 1)
            dve.tensor_tensor(comb[:, 0:EXPERTS].rearrange("p e k -> p k e"), pick[:],
                              tinv[:].unsqueeze(2).broadcast_to([P, TILES, EXPERTS]), ALU.mult
                              ).then_inc(sem["combine_ready"], 1)

            def product(n, q):
                dve.wait_ge(sem["silu_done"], n + 1)
                dve.wait_ge(sem["moe_out_done"], CREDIT_OUT + 2 * (n - 1))
                dve.tensor_tensor(hid[:, q % 2], silu[:, q % 2], bank[2 + q % 2][:], ALU.mult
                                  ).then_inc(sem["prod_ready"], 1)

            def accumulate(n, q, e):
                for t in range(BT):
                    if t % 2 == 0:
                        dve.wait_ge(sem["moe_out_done"], CREDIT_OUT + 2 * n + t // 2 + 1)
                    k = BT * (q % NBLK) + t
                    y = bank[4 + 2 * (q % 2) + t // 2][:, (t % 2) * D:(t % 2) * D + D]
                    dve.wait_ge(sem["acc_ready"], CREDIT_ACC + BT * (n - 1) + t)
                    dve.scalar_tensor_tensor(out=Hb[:, k], in0=y,
                                             scalar=comb[:, at(e, 1), k:k + 1].rearrange("p a b -> p (a b)"),
                                             in1=Hb[:, k], op0=ALU.mult, op1=ALU.add).then_inc(sem["acc_ready"], 1)

            dve.sem_inc(sem["prod_ready"], CREDIT_PROD)
            dve.sem_inc(sem["acc_ready"], CREDIT_ACC)
            dve.wait_ge(sem["combine_ready"], 1)
            product(0, 0)
            with dve.Fori(0, EXPERTS // 2) as j:
                for q in range(2 * NBLK):
                    product(2 * NBLK * j + q + 1, (q + 1) % (2 * NBLK))
                    accumulate(2 * NBLK * j + q, q, 2 * j + q // NBLK)
            for q in range(NBLK):
                if q + 1 < NBLK:
                    product(NBLK * EXPERTS + q + 1, q + 1)
                accumulate(NBLK * EXPERTS + q, q, EXPERTS)


def kernel(**inputs):
    import concourse.bacc as bacc
    import ml_dtypes
    from concourse.bass_utils import run_bass_kernel_spmd

    f = {k: np.asarray(v) for k, v in inputs.items()}

    def chunks(a, rows=P):
        return np.ascontiguousarray(a.reshape(-1, rows, a.shape[-1]).transpose(1, 0, 2))

    def rows(a):
        return np.ascontiguousarray(np.broadcast_to(a, (P, a.size)))

    def columns(a):
        return np.ascontiguousarray(a.reshape(-1, P).T)

    k, m = np.arange(P)[:, None], np.arange(P)[None, :]
    shift = np.stack([(k == m + dy - 1) for dy in range(3)], 1).astype(np.float32)
    ident = np.eye(P, dtype=np.float32)
    q = np.arange(P)[:, None]
    far = np.arange(2 * P)[None, :]
    mask0 = np.where((q - m >= 0) & (q - m < WINDOW), 0.0, MASKED).astype(ml_dtypes.bfloat16)
    mask1 = np.where((P + q - far >= 0) & (P + q - far < WINDOW), 0.0, MASKED).astype(ml_dtypes.bfloat16)
    inv_freq = (np.float32(1.0) / np.float32(10000.0) ** (np.arange(0, HD, 2, dtype=np.float32) / np.float32(HD)))
    angle = np.outer(np.arange(T, dtype=np.float32), inv_freq.astype(np.float32)).astype(np.float32)
    cos = np.concatenate([np.cos(angle), np.cos(angle)], 1)
    sin = np.concatenate([-np.sin(angle), np.sin(angle)], 1)
    scale = np.float32(HD ** -0.5)

    def table(a):
        both = np.stack([a * scale, a], 1).astype(np.float32)
        return np.ascontiguousarray(both.reshape(NT, P, 2, HD).transpose(1, 0, 2, 3))

    a = "L0_attn_"
    e1 = np.concatenate([f["L0_ffn_w1"], f["L0_ffn_sw1"][None]])
    e3 = np.concatenate([f["L0_ffn_w3"], f["L0_ffn_sw3"][None]])
    e2 = np.concatenate([f["L0_ffn_w2"], f["L0_ffn_sw2"][None]])
    e13 = np.concatenate([e1, e3], 1).transpose(0, 2, 1)
    arrays = {
        "x": f["x"], "shift": shift, "scharr_rows": rows(f["L0_tok_scharr"].reshape(-1)),
        "scharr": f["L0_tok_scharr"], "ident": ident, "ident16": ident.astype(ml_dtypes.bfloat16),
        "mask0": mask0, "mask1": mask1, "rope_cos_t": table(cos), "rope_sin_t": table(sin),
        "wqkT": chunks(np.concatenate([f[a + "wq"].T, f[a + "wk"].T], 1)), "wvT": chunks(f[a + "wv"].T),
        "woT": chunks(f[a + "wo"].T), "ls1_rows": rows(f[a + "ls1"]),
        "n1w": columns(f[a + "norm1_w"]), "n1b": columns(f[a + "norm1_b"]),
        "n2w": columns(f[a + "norm2_w"]), "n2b": columns(f[a + "norm2_b"]),
        "w1T": chunks(f[a + "w1"].T), "b1": columns(f[a + "b1"]), "w2T": chunks(f[a + "w2"].T),
        "b2_rows": rows(f[a + "b2"]), "ls2_rows": rows(f[a + "ls2"]), "gateT": chunks(f["L0_ffn_gate_w"].T),
        "e13T": np.ascontiguousarray(e13.reshape(EXPERTS + 1, KC, P, 2 * HID).transpose(2, 0, 1, 3)),
        "e2T": np.ascontiguousarray(e2.transpose(2, 0, 1)),
    }
    nc = bacc.Bacc("TRN2", target_bir_lowering=False, num_devices=1)
    aps = {k: nc.dram_tensor(f"in_{k}", v.shape, mybir.dt.from_np(v.dtype), kind="ExternalInput").ap()
           for k, v in arrays.items()}
    result = nc.dram_tensor("result", (NIMG, T, D), F32, kind="ExternalOutput").ap()
    build(nc, out=result, **aps)
    r = run_bass_kernel_spmd(nc, [{f"in_{k}": v for k, v in arrays.items()}], core_ids=[0])
    return r.results[0]["result"]
```

```python
from contextlib import ExitStack

import numpy as np

import concourse.bass as bass
from concourse import mybir

F32 = mybir.dt.float32
F32R = mybir.dt.float32r
I32 = mybir.dt.int32
BF16 = mybir.dt.bfloat16
ALU = mybir.AluOpType
ACT = mybir.ActivationFunctionType
AX = mybir.AxisListType

P = 128
NIMG, NCH, D = 8, 3, 256
T = 256
NT = T // P
KC = D // P
TILES = NIMG * NT
HEADS, HD = 16, 16
PARTS = 4
PAIRS = HEADS // 2
ROWS = PARTS * HD
WINDOW = 125
FFN = 1024
FC = FFN // P
EXPERTS, HID, TOPK = 16, 128, 4
BLK = 512
NBLK = NIMG * T // BLK
BT = BLK // P
GRAY = (0.2989, 0.587, 0.114)
EPS = 1e-5
ROOT_BITS = float(0x5F3759DF)
MASKED = -1e30
NG = 4
UNITS = 3 * NG

STAGES = """
x_loaded0 x_loaded1 halo_loaded0 halo_loaded1 halo_band_loaded filter_loaded const_a const_b w_loaded0 w_loaded1 memset_done pool_carrier dve_carrier ones_set
gray_part gray_ready band_part band_ready conv_done abs_ready h_ready
stats1 mv1 vars1 root1 x1_ready xhat_ready
xT_done hT_ready qk_done v_done rope_terms rope_ready rope_high rope_low v_ready qkT_done qkT_act qkT_dve
scores_done negmax_ready exp_done pT_done pT_copied pv_done recip_ready ao_ready
aoT_done aoT_copied wo_done wo_scaled x2_ready base_ready
stats2 mv2 vars2 root2 xhat2_ready x2T_done h2_ready h2T_ready h2T_low
w1_high w1_low w2_high w2_low ffn1_done gelu_done hidden_high hidden_low ffn2_done ffn_bias ffn_scaled h3_ready stats3 mv3 vars3 root3 xf_ready
xfT_done xfT_copied xfT_low gate_high gate_low gate_done gate_max gate_shift gate_exp top_ready keys_set keys_ready replaced picked
sum_ready inv_ready combine_ready we_high we_low moe_h_done silu_done prod_ready hid_high hid_low moe_out_done acc_ready out_stored
""".split()


def build(nc, x, shift, scharr_rows, scharr, ident, ident16, mask0, mask1, rope_cos_t, rope_sin_t,
          wqkT, wvT, woT, ls1_rows, n1w, n1b, n2w, n2b, w1T, b1, w2T, b2_rows, ls2_rows,
          gateT, e13T, e2T, out):
    with ExitStack() as ctx:
        def sb(name, shape, dt=F32, until=ctx):
            return until.enter_context(nc.sbuf_tensor(name, shape, dt))

        def ps(name, shape):
            return ctx.enter_context(nc.psum_tensor(name, shape, F32))

        sem = {n: ctx.enter_context(nc.semaphore(n)) for n in STAGES}

        idf = sb("idf", [P, P])
        idb = sb("idb", [P, P], BF16)
        msk0 = sb("msk0", [P, P], BF16)
        msk1 = sb("msk1", [P, 2 * P], BF16)
        wo = sb("wo", [P, KC, D])
        ls1 = sb("ls1", [P, D])
        ls2 = sb("ls2", [P, D])
        b2 = sb("b2", [P, D])
        norm_wb = sb("norm_wb", [P, 4, KC])
        w1 = sb("w1", [P, KC, FFN])
        b1c = sb("b1c", [P, FC])
        w2 = sb("w2", [P, FC, D])
        gate = sb("gate", [P, KC, EXPERTS])

        Hb = sb("Hb", [P, TILES, D])
        XT = sb("XT", [P, KC, NIMG * T], F32R)
        XTlow = sb("XTlow", [P, KC, NIMG * T], F32R)
        stats3 = sb("stats3", [P, TILES, 6])
        mv3 = sb("mv3", [P, TILES, 2])
        vars3 = sb("vars3", [P, 1, TILES])
        root3 = sb("root3", [P, 3, 1, TILES])

        with ExitStack() as phase:
            xin = sb("xin", [P, 2, NCH, NT, D], until=phase)
            gray = sb("gray", [P, 2, NT, D + 2], until=phase)
            halo = sb("halo", [3, 2, NT, D], until=phase)
            edge = sb("edge", [P, 2, NT, D], until=phase)
            xhat = sb("xhat", [P, NT, D], until=phase)
            hT = sb("hT", [P, KC, T], until=phase)
            rcos = sb("rcos", [P, 2, 2, HEADS, HD], until=phase)
            rsin = sb("rsin", [P, 2, 2, HEADS, HD], until=phase)
            cosT = sb("cosT", [P, NT, 2, HD], until=phase)
            sinT = sb("sinT", [P, NT, 2, HD], until=phase)
            shf = sb("shf", [P, 3, P], until=phase)
            schr = sb("schr", [P, 18], until=phase)
            band = sb("band", [P, 2, 3, P], until=phase)
            halo_band = sb("halo_band", [3, 2, NT, P], until=phase)
            wqk = sb("wqk", [P, KC, 2 * D], until=phase)
            wv = sb("wv", [P, KC, D], until=phase)
            x1 = sb("x1", [P, 2, NT, D], until=phase)
            x2 = sb("x2", [P, NT, D], until=phase)
            qkr = sb("qkr", [P, NT, 2, HEADS, HD], until=phase)
            qks = sb("qks", [P, NT, 2, HEADS, PARTS, HD], F32R, phase)
            V = sb("V", [P, 2, NT, HEADS, HD + 1], until=phase)
            QKT = sb("QKT", [P, 2, 2, PAIRS, T], F32R, phase)
            negmax = sb("negmax", [P, 2, UNITS, 4], until=phase)
            prob = sb("prob", [P, 2, 512], until=phase)
            pT = sb("pT", [P, 3, 4, P], until=phase)
            rinv = sb("rinv", [P, NG, NT, 4], until=phase)
            AO = sb("AO", [P, 2, NT, D], until=phase)
            aoT = sb("aoT", [P, KC, T], until=phase)
            wos = sb("wos", [P, NT, D], until=phase)
            xhat2 = sb("xhat2", [P, NT, D], until=phase)
            h2 = sb("h2", [P, KC, T], until=phase)
            stats = sb("stats", [P, 2, NT, 6], until=phase)
            mv = sb("mv", [P, 2, NT, 2], until=phase)
            vars1 = sb("vars1", [P, 2, NT], until=phase)
            vars2 = sb("vars2", [P, 1, NT], until=phase)
            root1 = sb("root1", [P, 3, 2, NT], until=phase)
            root2 = sb("root2", [P, 3, 1, NT], until=phase)

        w13 = sb("w13", [P, 2, KC, 2 * HID])
        we2 = sb("we2", [P, 2, D])
        with ExitStack() as phase:
            w1high = sb("w1high", [P, KC, FFN], F32R, phase)
            w1low = sb("w1low", [P, KC, FFN], F32R, phase)
            w2high = sb("w2high", [P, FC, D], F32R, phase)
            w2low = sb("w2low", [P, FC, D], F32R, phase)
            G = sb("G", [P, 2, FC, BLK], F32R, phase)
            Glow = sb("Glow", [P, 2, FC, BLK], F32R, phase)
            gelu = sb("gelu", [P, 2, BLK], until=phase)
            fb = sb("fb", [P, 2, 2, D], until=phase)
            fs = sb("fs", [P, 2, 2, D], until=phase)

        XF = sb("XF", [P, 2, NT, D])
        gatehigh = sb("gatehigh", [P, KC, EXPERTS], F32R)
        gatelow = sb("gatelow", [P, KC, EXPERTS], F32R)
        gmax = sb("gmax", [P, TILES])
        gsh = sb("gsh", [P, TILES, EXPERTS])
        gexp = sb("gexp", [P, TILES, EXPERTS + TOPK])
        top8 = sb("top8", [P, TILES, 8])
        keys = sb("keys", [P, TILES, 8])
        repl = sb("repl", [P, TILES, EXPERTS + TOPK])
        pick = sb("pick", [P, TILES, EXPERTS])
        tsum = sb("tsum", [P, TILES])
        tinv = sb("tinv", [P, TILES])
        comb = sb("comb", [P, EXPERTS + 1, TILES])
        w13high = sb("w13high", [P, 2, KC, 2 * HID], F32R)
        w13low = sb("w13low", [P, 2, KC, 2 * HID], F32R)
        we2high = sb("we2high", [P, 2, D], F32R)
        we2low = sb("we2low", [P, 2, D], F32R)
        silu = sb("silu", [P, 2, BLK])
        hid = sb("hid", [P, 2, BLK])
        hidhigh = sb("hidhigh", [P, 2, BLK], F32R)
        hidlow = sb("hidlow", [P, 2, BLK], F32R)

        bank = [ps(f"bank{n}", [P, 512]) for n in range(8)]
        S, TP, O, Fb = bank[0:3], bank[3:5], bank[5], bank[6:8]
        Ov = O[:, 0:NT * 4 * (HD + 1)].rearrange("p (t h d) -> p t h d", t=NT, h=4)

        def w(eng, signal, value):
            if not (isinstance(value, int) and value <= 0):
                eng.wait_ge(signal, value)

        def wait_apart(eng, signal, value, carrier):
            eng.wait_ge(signal, value)
            if not isinstance(value, int):
                eng.sem_inc(carrier, 1)

        filters = ((shf[:], shift), (schr[:], scharr_rows))
        first_constants = (
            (idf[:], ident), (wqk[:], wqkT), (wv[:], wvT),
            (norm_wb[:, 0], n1w), (norm_wb[:, 1], n1b), (cosT[:], rope_cos_t), (sinT[:], rope_sin_t),
            (idb[:], ident16), (msk0[:], mask0), (msk1[:], mask1))
        later_constants = (
            (wo[:], woT), (ls1[:], ls1_rows), (norm_wb[:, 2], n2w), (norm_wb[:, 3], n2b),
            (w1[:], w1T), (b1c[:], b1), (w2[:], w2T), (b2[:], b2_rows), (ls2[:], ls2_rows), (gate[:], gateT))

        def at(n, count):
            return slice(n, n + count) if isinstance(n, int) else bass.ds(n, count)

        xv = x.rearrange("i c (t p) d -> p i c t d", p=P)
        ov = out.rearrange("i (t p) d -> p (i t) d", p=P)
        x_loaded = (sem["x_loaded0"], sem["x_loaded1"])
        halo_loaded = (sem["halo_loaded0"], sem["halo_loaded1"])
        w_loaded = (sem["w_loaded0"], sem["w_loaded1"])
        Y = [bank[4], bank[5]]
        gate_bank = bank[6]
        CREDIT_GELU, CREDIT_FFN2, CREDIT_BIAS = 4, 4, 2
        CREDIT_PROD, CREDIT_OUT, CREDIT_ACC = 2, 4, 8
        CREDIT_XFT, CREDIT_HIDDEN, CREDIT_HID, CREDIT_LOW = 2, 2, 2, 1

        block = ctx.enter_context(nc.Block())

        @block.sync
        def _(sp):
            def load_x(i, u):
                w(sp, sem["gray_ready"], i - 1)
                for c in range(NCH):
                    sp.dma_start(xin[:, u, c], xv[:, at(i, 1), c].rearrange("p i t d -> p (i t) d")
                                 ).then_inc(x_loaded[u], 16)

            def load_halo(m, u):
                sp.wait_ge(sem["gray_ready"], m + 1)
                for t in range(NT):
                    row = gray[(0, P - 1)[t]:(1, P)[t], u, 1 - t, :]
                    shifts = bass.AP(tensor=row.tensor, offset=row.offset, ap=[row.ap[0], [1, 3], [1, D]])
                    sp.dma_start(halo[:, u, t], shifts).then_inc(halo_loaded[u], 16)

            load_x(0, 0)
            for dst, src in filters:
                sp.dma_start(dst, src).then_inc(sem["filter_loaded"], 16)
            sp.wait_ge(sem["memset_done"], 1)
            for t in range(NT):
                dy, col = (2, P - 1) if t == 0 else (0, 0)
                for f in range(2):
                    sp.dma_start(halo_band[:, f, t, col:col + 1],
                                 scharr[f, 0, dy:dy + 1, :].rearrange("a d -> d a")
                                 ).then_inc(sem["halo_band_loaded"], 16)
            for dst, src in first_constants:
                sp.dma_start(dst, src).then_inc(sem["const_a"], 16)
            load_x(1, 1)
            load_halo(0, 0)
            for dst, src in later_constants:
                sp.dma_start(dst, src).then_inc(sem["const_b"], 16)

            def load_expert(e, u):
                w(sp, sem["we_low"], 2 * (e - 1))
                sp.dma_start(w13[:, u], e13T[:, at(e, 1)].rearrange("p e c h -> p (e c) h")).then_inc(w_loaded[u], 16)
                sp.dma_start(we2[:, u], e2T[:, at(e, 1)].rearrange("p e d -> p (e d)")).then_inc(w_loaded[u], 16)

            load_halo(1, 1)
            with sp.Fori(1, NIMG // 2) as j:
                for u in range(2):
                    load_x(2 * j + u, u)
                    load_halo(2 * j + u, u)
            load_expert(0, 0)
            load_expert(1, 1)
            with sp.Fori(1, EXPERTS // 2) as j:
                for u in range(2):
                    load_expert(2 * j + u, u)
            load_expert(EXPERTS, 0)
            for b in range(NBLK):
                sp.wait_ge(sem["acc_ready"], CREDIT_ACC + BT * (NBLK * EXPERTS + b + 1))
                sp.dma_start(ov[:, BT * b:BT * b + BT], Hb[:, BT * b:BT * b + BT]).then_inc(sem["out_stored"], 16)
            sp.wait_ge(sem["out_stored"], 16 * NBLK)

        @block.gpsimd
        def _(pool):
            pool.sem_inc(sem["h2T_low"], CREDIT_LOW)
            pool.sem_inc(sem["base_ready"], CREDIT_LOW)
            pool.memset(halo_band[:], 0.0).then_inc(sem["memset_done"], 1)
            pool.memset(gray[:], 0.0).then_inc(sem["memset_done"], 1)
            pool.wait_ge(sem["memset_done"], 2)

            def make_gray(i, u):
                w(pool, sem["conv_done"], 2 * (i - 1))
                wait_apart(pool, x_loaded[u], 8 * NCH * (i - u) + 16 * NCH, sem["pool_carrier"])
                g = gray[:, u, :, 1:D + 1]
                for c in range(NCH):
                    pool.tensor_scalar(xin[:, u, c], xin[:, u, c], GRAY[c], None, ALU.mult).then_inc(sem["gray_part"], 1)
                pool.wait_ge(sem["gray_part"], 4 * i + 3)
                pool.tensor_tensor(g, xin[:, u, 0], xin[:, u, 1], ALU.add).then_inc(sem["gray_part"], 1)
                pool.wait_ge(sem["gray_part"], 4 * i + 4)
                pool.tensor_tensor(g, g, xin[:, u, 2], ALU.add).then_inc(sem["gray_ready"], 1)

            def rope_add(m, t):
                pool.wait_ge(sem["rope_terms"], 3 * (NT * m + t + 1))
                w(pool, sem["rope_low"], 4 * (m - 1) + 2 * t + 2)
                pool.tensor_tensor(qkr[:, t], rcos[:, t], rsin[:, t], ALU.add).then_inc(sem["rope_ready"], 1)

            def rope_low(m, t):
                for qk, (high, low) in enumerate(((slice(0, 4, 2), slice(1, 4, 2)), (slice(0, 2), slice(2, 4)))):
                    pool.wait_ge(sem["rope_high"], 4 * m + 2 * t + qk + 1)
                    pool.tensor_tensor(qks[:, t, qk, :, low], qkr[:, t, qk].unsqueeze(2).broadcast_to([P, HEADS, 2, HD]),
                                       qks[:, t, qk, :, high].bitcast(F32), ALU.subtract).then_inc(sem["rope_low"], 1)

            def residual(l, u):
                pool.wait_ge(sem["wo_scaled"], l + 1)
                pool.wait_ge(sem["base_ready"], CREDIT_LOW + l)
                pool.tensor_tensor(x2[:], wos[:], x1[:, u], ALU.add).then_inc(sem["x2_ready"], 1)
                pool.wait_ge(sem["x2_ready"], l + 1)
                h = Hb[:, at(NT * l, NT)]
                pool.tensor_tensor(h, h, x2[:], ALU.add).then_inc(sem["base_ready"], 1)

            def h2_low(l):
                pool.wait_ge(sem["h2T_ready"], l + 1)
                at_l = at(l * T, T)
                pool.tensor_tensor(XTlow[:, :, at_l], h2[:], XT[:, :, at_l].bitcast(F32), ALU.subtract
                                   ).then_inc(sem["h2T_low"], 1)

            def step(i, u, front, tail, gray_next):
                if gray_next:
                    make_gray(i + 2, u)
                if tail:
                    residual(i - 1, 1 - u)
                if front:
                    for t in range(NT):
                        rope_add(i + 1, t)
                    for t in range(NT):
                        rope_low(i + 1, t)
                if tail:
                    h2_low(i - 1)

            make_gray(0, 0)
            pool.memset(V[:], 1.0).then_inc(sem["ones_set"], 1)
            make_gray(1, 1)
            for t in range(NT):
                rope_add(0, t)
            for t in range(NT):
                rope_low(0, t)
            step(0, 0, True, False, True)
            with pool.Fori(0, (NIMG - 4) // 2) as j:
                step(2 * j + 1, 1, True, True, True)
                step(2 * j + 2, 0, True, True, True)
            step(NIMG - 3, 1, True, True, True)
            step(NIMG - 2, 0, True, True, False)
            pool.wait_ge(sem["w1_high"], 1)
            pool.tensor_tensor(w1low[:], w1[:], w1high[:].bitcast(F32), ALU.subtract).then_inc(sem["w1_low"], 1)
            residual(NIMG - 2, 0)
            pool.wait_ge(sem["w2_high"], 1)
            pool.tensor_tensor(w2low[:], w2[:], w2high[:].bitcast(F32), ALU.subtract).then_inc(sem["w2_low"], 1)
            h2_low(NIMG - 2)
            residual(NIMG - 1, 1)
            h2_low(NIMG - 1)

            pool.sem_inc(sem["hidden_low"], CREDIT_HIDDEN)
            with pool.Fori(0, NBLK // 2) as j:
                for u in range(2):
                    for f in range(FC):
                        pool.wait_ge(sem["hidden_high"], FC * (2 * j + u) + f + 1)
                        pool.tensor_tensor(Glow[:, u, f], gelu[:, f % 2], G[:, u, f].bitcast(F32), ALU.subtract
                                           ).then_inc(sem["hidden_low"], 1)

            def weights_low(e, u, part):
                pool.wait_ge(sem["we_high"], 2 * e + part + 1)
                whole, high, low = ((w13, w13high, w13low), (we2, we2high, we2low))[part]
                pool.tensor_tensor(low[:, u], whole[:, u], high[:, u].bitcast(F32), ALU.subtract
                                   ).then_inc(sem["we_low"], 1)

            def hidden_low(n, q):
                pool.wait_ge(sem["hid_high"], n + 1)
                pool.tensor_tensor(hidlow[:, q % 2], hid[:, q % 2], hidhigh[:, q % 2].bitcast(F32), ALU.subtract
                                   ).then_inc(sem["hid_low"], 1)

            weights_low(0, 0, 0)
            weights_low(0, 0, 1)
            pool.sem_inc(sem["hid_low"], CREDIT_HID)
            with pool.Fori(0, EXPERTS // 2) as j:
                for q in range(2 * NBLK):
                    hidden_low(2 * NBLK * j + q, q)
                    u = q // NBLK
                    if q % NBLK in (1, 2):
                        weights_low(2 * j + u + 1, 1 - u, q % NBLK - 1)
            for q in range(NBLK):
                hidden_low(NBLK * EXPERTS + q, q)

        @block.tensor
        def _(pe):
            def in_parts(pe, dst, factors, first=True, last=True):
                factors = [(tuple(a), tuple(b)) for a, b in factors]
                steps = ([(a[0], y) for a, b in factors for y in b] + [(a[1], b[0]) for a, b in factors])
                for n, (left, right) in enumerate(steps):
                    mm = pe.matmul(dst, left, right, start=(first and n == 0), stop=(last and n == len(steps) - 1))
                return mm

            def conv(m, v):
                pe.wait_ge(halo_loaded[v], 8 * NT * (m - v) + 16 * NT)
                w(pe, sem["qkT_act"], 4 * m)
                w(pe, sem["qkT_dve"], 4 * m)
                for f in range(2):
                    for dx in range(3):
                        pe.matmul(Fb[f][:], band[:, f, dx], gray[:, v, :, dx:dx + D], start=(dx == 0), stop=False)
                    for t in range(NT):
                        mm = pe.matmul(Fb[f][:, t * D:t * D + D], halo_band[:, f, t],
                                       halo[:, v, t],
                                       start=False, stop=(t == NT - 1))
                    mm.then_inc(sem["conv_done"], 1)

            def turn(dst, src):
                for c in range(KC):
                    for t in range(NT):
                        mm = pe.transpose(dst[:, c * T + t * P:c * T + t * P + P], src[:, t, c * P:c * P + P], idf[:])
                return mm

            def project(dst, src, weights):
                for t in range(NT):
                    for c in range(KC):
                        mm = pe.matmul(dst[:, t * D:t * D + D], src[:, c, t * P:t * P + P], weights[:, c],
                                       start=(c == 0), stop=(c == KC - 1))
                return mm

            def norm_turn(m):
                pe.wait_ge(sem["xhat_ready"], NT * (m + 1))
                w(pe, sem["aoT_copied"], m - 1)
                turn(Fb[0], xhat).then_inc(sem["xT_done"], 1)

            def project_qk(m, t):
                if t == 0:
                    pe.wait_ge(sem["hT_ready"], KC * (m + 1))
                    w(pe, sem["wo_scaled"], m - 1)
                for c in range(KC):
                    mm = pe.matmul(Fb[1 - t][:], hT[:, c, t * P:t * P + P], wqk[:, c],
                                   start=(c == 0), stop=(c == KC - 1))
                mm.then_inc(sem["qk_done"], 1)

            def project_v(m):
                pe.wait_ge(sem["rope_terms"], 6 * m + 3)
                project(Fb[1], hT, wv).then_inc(sem["v_done"], 1)

            def turn_qk(m, n):
                t, qk, half = n // 4, n // 2 % 2, n % 2
                pe.wait_ge(sem["rope_low"], 4 * m + 2 * t + qk + 1)
                if n == 0:
                    pe.wait_ge(sem["v_ready"], m + 1)
                if n == 1:
                    pe.wait_ge(sem["rope_terms"], 6 * m + 6)
                    w(pe, sem["h2_ready"], KC * (m - 1))
                if n >= 2:
                    pe.wait_ge(sem["qkT_dve"] if half else sem["qkT_act"], 4 * m + n // 2)
                for j in range(4):
                    heads = slice(8 * half + 2 * j, 8 * half + 2 * j + 2)
                    mm = pe.transpose(Fb[1 - half][:, j * P:j * P + P],
                                      qks[:, t, qk, heads].rearrange("p h a d -> p (h a d)").bitcast(F32), idf[:])
                mm.then_inc(sem["qkT_done"], 1)

            def heads_out(l, v, front):
                pe.wait_ge(sem["ao_ready"], NG * (l + 1))
                if front:
                    pe.wait_ge(sem["abs_ready"], 2 * (l + 3))
                else:
                    pe.wait_ge(sem["h2_ready"], KC * l)
                turn(Fb[0], AO[:, v]).then_inc(sem["aoT_done"], 1)

            def project_out(l):
                pe.wait_ge(sem["aoT_copied"], l + 1)
                project(Fb[1], aoT, wo).then_inc(sem["wo_done"], 1)

            def norm2_turn(l, front):
                pe.wait_ge(sem["xhat2_ready"], NT * (l + 1))
                if front:
                    pe.wait_ge(sem["rope_terms"], 6 * (l + 3))
                turn(Fb[0], xhat2).then_inc(sem["x2T_done"], 1)

            def scores(i, u, n):
                g, k = n // 3, n % 3
                if n == 0:
                    pe.wait_ge(sem["qkT_act"], 4 * (i + 1))
                    pe.wait_ge(sem["qkT_dve"], 4 * (i + 1))
                w(pe, sem["exp_done"], UNITS * i + n - 2)
                heads = range(4) if k == 0 else range(2 * k - 2, 2 * k)
                keys = P if k == 0 else 2 * P
                m = (msk0 if k == 0 else msk1)[:].unsqueeze(1).broadcast_to([P, len(heads), keys])
                pe.matmul(S[k][:].rearrange("p (h k) -> p h k", k=keys), idb[:], m, start=True, stop=False)
                r = slice(ROWS * (g % 2), ROWS * (g % 2) + ROWS)
                for slot, j in enumerate(heads):
                    pair = 4 * (g // 2) + j
                    mm = pe.matmul(S[k][:, slot * keys:slot * keys + keys],
                                   QKT[r, u, 0, pair, 0:P] if k == 0 else QKT[r, u, 0, pair, P:T],
                                   QKT[r, u, 1, pair, 0:keys], start=False, stop=(slot == len(heads) - 1))
                mm.then_inc(sem["scores_done"], 1)

            def turn_probs(i, n):
                pe.wait_ge(sem["exp_done"], UNITS * i + n + 1)
                w(pe, sem["pT_copied"], UNITS * i + n - 1)
                for q in range(4):
                    mm = pe.transpose(TP[n % 2][:, q * P:q * P + P], prob[:, n % 2, q * P:q * P + P], idf[:])
                mm.then_inc(sem["pT_done"], 1)

            def head(g, j):
                return 8 * (g // 2) + 2 * j + g % 2

            def attend(i, u, n):
                g, k = n // 3, n % 3
                pe.wait_ge(sem["pT_copied"], UNITS * i + n + 1)
                if k == 0:
                    w(pe, sem["ao_ready"], NG * i + g)
                    if n == 0:
                        pe.wait_ge(sem["v_ready"], i + 1)
                    for j in range(4):
                        mm = pe.matmul(Ov[:, 0, j], pT[:, n % 3, j], V[:, u, 0, head(g, j)], start=True, stop=True)
                else:
                    for slot in range(2):
                        j = 2 * k - 2 + slot
                        for t in range(NT):
                            mm = pe.matmul(Ov[:, 1, j], pT[:, n % 3, 2 * slot + t], V[:, u, t, head(g, j)],
                                           start=(t == 0), stop=(t == NT - 1))
                mm.then_inc(sem["pv_done"], 1)

            def step(i, u, front, tail):
                scores(i, u, 0)
                scores(i, u, 1)
                for n in range(UNITS):
                    if n + 2 < UNITS:
                        scores(i, u, n + 2)
                    if front and n == 0:
                        conv(i + 1, 1 - u)
                    if tail and n == 1:
                        heads_out(i - 1, 1 - u, front)
                    if tail and n == 2:
                        project_out(i - 1)
                    if front and n == 3:
                        norm_turn(i + 1)
                    if front and n == 4:
                        project_qk(i + 1, 0)
                        project_qk(i + 1, 1)
                    if front and n == 5:
                        project_v(i + 1)
                    if tail and n == 7:
                        norm2_turn(i - 1, front)
                    if front and n >= 8:
                        turn_qk(i + 1, 2 * (n - 8))
                        turn_qk(i + 1, 2 * (n - 8) + 1)
                    turn_probs(i, n)
                    if n >= 1:
                        attend(i, u, n - 1)
                attend(i, u, UNITS - 1)

            pe.wait_ge(sem["const_a"], 16 * len(first_constants))
            pe.wait_ge(sem["band_ready"], 6)
            pe.wait_ge(sem["halo_band_loaded"], 16 * 4)
            conv(0, 0)
            norm_turn(0)
            project_qk(0, 0)
            project_qk(0, 1)
            project_v(0)
            for n in range(8):
                turn_qk(0, n)
            pe.wait_ge(sem["const_b"], 16 * len(later_constants))
            step(0, 0, True, False)
            with pe.Fori(0, (NIMG - 2) // 2) as j:
                step(2 * j + 1, 1, True, True)
                step(2 * j + 2, 0, True, True)
            step(NIMG - 1, 1, False, True)
            heads_out(NIMG - 1, 1, False)
            project_out(NIMG - 1)
            norm2_turn(NIMG - 1, False)

            def ffn(b, u):
                for f in range(FC):
                    pe.wait_ge(sem["gelu_done"], CREDIT_GELU + FC * b + f - 3)
                    mm = in_parts(pe, bank[f % 4][:], (
                        ((part[:, c, f * P:f * P + P] for part in (w1high, w1low)),
                         (part[:, c, at(b * BLK, BLK)] for part in (XT, XTlow))) for c in range(KC)))
                    mm.then_inc(sem["ffn1_done"], 1)
                for half in range(2):
                    pe.wait_ge(sem["ffn_bias"], CREDIT_BIAS + 2 * b + half - 1)
                    for f in range(FC):
                        if half == 0:
                            pe.wait_ge(sem["hidden_low"], CREDIT_HIDDEN + FC * b + f + 1)
                        for t in range(2):
                            k = (2 * half + t) * P
                            mm = in_parts(pe, Y[half][:, t * D:t * D + D], [
                                ((part[:, u, f, k:k + P] for part in (G, Glow)),
                                 (part[:, f] for part in (w2high, w2low)))],
                                f == 0 and t == 0, f == FC - 1 and t == 1)
                    mm.then_inc(sem["ffn2_done"], 1)

            pe.sem_inc(sem["ffn2_done"], CREDIT_FFN2)
            pe.wait_ge(sem["h2T_low"], CREDIT_LOW + NIMG)
            pe.wait_ge(sem["w1_low"], 1)
            pe.wait_ge(sem["w2_low"], 1)
            with pe.Fori(0, NBLK // 2) as j:
                ffn(2 * j, 0)
                ffn(2 * j + 1, 1)

            with pe.Fori(0, NIMG // 2) as j:
                for u in range(2):
                    k = 2 * j + u
                    pe.wait_ge(sem["xf_ready"], NT * (k + 1))
                    pe.wait_ge(sem["xfT_low"], CREDIT_XFT + k - 1)
                    turn(bank[u], XF[:, u]).then_inc(sem["xfT_done"], 1)
            pe.wait_ge(sem["xfT_low"], CREDIT_XFT + NIMG)
            pe.wait_ge(sem["gate_low"], 1)
            for k in range(TILES):
                mm = in_parts(pe, gate_bank[:, k * EXPERTS:k * EXPERTS + EXPERTS], (
                    ((part[:, c, k * P:k * P + P] for part in (XT, XTlow)),
                     (part[:, c] for part in (gatehigh, gatelow))) for c in range(KC)))
            mm.then_inc(sem["gate_done"], 1)

            def moe_hidden(n, q, e):
                b, u = q % NBLK, q // NBLK
                if b == 0:
                    pe.wait_ge(sem["we_low"], 2 * e + 1)
                pe.wait_ge(sem["prod_ready"], CREDIT_PROD + n - 1)
                for which in range(2):
                    mm = in_parts(pe, bank[2 * which + q % 2][:], (
                        ((part[:, u, c, which * HID:which * HID + HID] for part in (w13high, w13low)),
                         (part[:, c, b * BLK:b * BLK + BLK] for part in (XT, XTlow))) for c in range(KC)))
                mm.then_inc(sem["moe_h_done"], 1)

            def moe_out(n, q, e):
                if q % NBLK == 0:
                    pe.wait_ge(sem["we_low"], 2 * e + 2)
                pe.wait_ge(sem["hid_low"], CREDIT_HID + n + 1)
                for half in range(2):
                    pe.wait_ge(sem["acc_ready"], CREDIT_ACC + BT * (n - 2) + 2 * half + 2)
                    for t in range(2):
                        k = (2 * half + t) * P
                        mm = in_parts(pe, bank[4 + 2 * (q % 2) + half][:, t * D:t * D + D], [
                            ((part[:, q % 2, k:k + P] for part in (hidhigh, hidlow)),
                             (part[:, q // NBLK] for part in (we2high, we2low)))])
                    mm.then_inc(sem["moe_out_done"], 1)

            pe.sem_inc(sem["moe_out_done"], CREDIT_OUT)
            moe_hidden(0, 0, 0)
            with pe.Fori(0, EXPERTS // 2) as j:
                for q in range(2 * NBLK):
                    moe_hidden(2 * NBLK * j + q + 1, (q + 1) % (2 * NBLK), 2 * j + (q + 1) // NBLK)
                    moe_out(2 * NBLK * j + q, q, 2 * j + q // NBLK)
            for q in range(NBLK):
                if q + 1 < NBLK:
                    moe_hidden(NBLK * EXPERTS + q + 1, q + 1, EXPERTS)
                moe_out(NBLK * EXPERTS + q, q, EXPERTS)

        @block.scalar
        def _(act):
            def edges(m):
                w(act, sem["h_ready"], m)
                for f in range(2):
                    act.wait_ge(sem["conv_done"], 2 * m + f + 1)
                    act.activation(edge[:, f], Fb[f][:].rearrange("p (t d) -> p t d", t=NT), ACT.Abs,
                                   scale=0.5).then_inc(sem["abs_ready"], 1)

            def norm_copy(m):
                act.wait_ge(sem["xT_done"], m + 1)
                w(act, sem["v_done"], m)
                for c in range(KC):
                    act.activation(hT[:, c], Fb[0][:, c * T:c * T + T], ACT.Identity,
                                   scale=norm_wb[:, 0, c:c + 1], bias=norm_wb[:, 1, c:c + 1]).then_inc(sem["hT_ready"], 1)

            def v_copy(m, v):
                act.wait_ge(sem["v_done"], m + 1)
                w(act, sem["pv_done"], UNITS * (m - 1))
                act.activation(V[:, v, :, :, 0:HD], Fb[1][:].rearrange("p (t h d) -> p t h d", t=NT, h=HEADS),
                               ACT.Identity).then_inc(sem["v_ready"], 1)

            def rope_high(m, t):
                act.wait_ge(sem["rope_ready"], NT * m + t + 1)
                w(act, sem["qkT_done"], 8 * m)
                for qk, high in enumerate((slice(0, 4, 2), slice(0, 2))):
                    act.activation(qks[:, t, qk, :, high], qkr[:, t, qk].unsqueeze(2).broadcast_to([P, HEADS, 2, HD]),
                                   ACT.Identity).then_inc(sem["rope_high"], 1)

            def qkT_copy(m, v, n):
                t, qk = n // 4, n // 2 % 2
                act.wait_ge(sem["qkT_done"], 8 * m + n + 1)
                act.activation(QKT[:, v, qk, 0:4, t * P:t * P + P], Fb[1][:].rearrange("p (j k) -> p j k", j=4),
                               ACT.Identity).then_inc(sem["qkT_act"], 1)

            def ao_copy(l):
                act.wait_ge(sem["aoT_done"], l + 1)
                act.activation(aoT[:], Fb[0][:].rearrange("p (c k) -> p c k", c=KC), ACT.Identity
                               ).then_inc(sem["aoT_copied"], 1)

            def norm2_copy(l):
                act.wait_ge(sem["x2T_done"], l + 1)
                act.wait_ge(sem["h2T_low"], CREDIT_LOW + l)
                for c in range(KC):
                    act.activation(h2[:, c], Fb[0][:, c * T:c * T + T], ACT.Identity,
                                   scale=norm_wb[:, 2, c:c + 1], bias=norm_wb[:, 3, c:c + 1]).then_inc(sem["h2_ready"], 1)
                act.wait_ge(sem["h2_ready"], KC * (l + 1))
                act.activation(XT[:, :, at(l * T, T)], h2[:], ACT.Identity).then_inc(sem["h2T_ready"], 1)

            def exps(i, u, n):
                k = n % 3
                heads, keys = (4, P) if k == 0 else (2, 2 * P)
                act.wait_ge(sem["negmax_ready"], UNITS * i + n + 1)
                w(act, sem["pT_done"], UNITS * i + n - 1)
                for h in range(heads):
                    a = act.activation(prob[:, n % 2, h * keys:h * keys + keys], S[k][:, h * keys:h * keys + keys],
                                       ACT.Exp, bias=negmax[:, u, n, h:h + 1])
                a.then_inc(sem["exp_done"], 1)

            def step(i, u, front, tail):
                for n in range(UNITS):
                    exps(i, u, n)
                    if front and n == 0:
                        edges(i + 1)
                    if tail and n == 1:
                        ao_copy(i - 1)
                    if front and n == 3:
                        norm_copy(i + 1)
                    if front and n == 5:
                        v_copy(i + 1, 1 - u)
                    if tail and n == 7:
                        norm2_copy(i - 1)
                    if front and n in (6, 7):
                        rope_high(i + 1, n - 6)
                    if front and n >= 8:
                        qkT_copy(i + 1, 1 - u, 2 * (n - 8))

            act.wait_ge(sem["const_a"], 16 * len(first_constants))
            edges(0)
            norm_copy(0)
            act.wait_ge(sem["ones_set"], 1)
            v_copy(0, 0)
            for t in range(NT):
                rope_high(0, t)
            for n in range(0, 8, 2):
                qkT_copy(0, 0, n)
            act.wait_ge(sem["const_b"], 16 * len(later_constants))
            step(0, 0, True, False)
            with act.Fori(0, (NIMG - 2) // 2) as j:
                step(2 * j + 1, 1, True, True)
                step(2 * j + 2, 0, True, True)
            act.wait_ge(sem["conv_done"], 2 * NIMG)
            act.wait_ge(sem["h_ready"], NIMG)
            act.wait_ge(sem["v_done"], NIMG)
            act.wait_ge(sem["rope_ready"], NT * NIMG)
            act.activation(w1high[:], w1[:], ACT.Identity).then_inc(sem["w1_high"], 1)
            act.activation(w2high[:], w2[:], ACT.Identity).then_inc(sem["w2_high"], 1)
            step(NIMG - 1, 1, False, True)
            ao_copy(NIMG - 1)
            norm2_copy(NIMG - 1)

            act.wait_ge(sem["h2T_low"], CREDIT_LOW + NIMG)
            act.sem_inc(sem["gelu_done"], CREDIT_GELU)
            with act.Fori(0, NBLK // 2) as j:
                for u in range(2):
                    b = 2 * j + u
                    act.wait_ge(sem["ffn2_done"], CREDIT_FFN2 + 2 * (b - 1))
                    for f in range(FC):
                        act.wait_ge(sem["ffn1_done"], FC * b + f + 1)
                        act.wait_ge(sem["hidden_low"], CREDIT_HIDDEN + FC * b + f - 1)
                        act.activation(gelu[:, f % 2], bank[f % 4][:], ACT.Gelu, bias=b1c[:, f:f + 1]
                                       ).then_inc(sem["gelu_done"], 1)
                        act.wait_ge(sem["gelu_done"], CREDIT_GELU + FC * b + f + 1)
                        act.activation(G[:, u, f], gelu[:, f % 2], ACT.Identity).then_inc(sem["hidden_high"], 1)

            def weights_high(e, u):
                act.wait_ge(w_loaded[u], 16 * (e - u) + 32)
                act.wait_ge(sem["moe_out_done"], CREDIT_OUT + 2 * NBLK * (e - 1))
                act.activation(w13high[:, u], w13[:, u], ACT.Identity).then_inc(sem["we_high"], 1)
                act.activation(we2high[:, u], we2[:, u], ACT.Identity).then_inc(sem["we_high"], 1)

            act.wait_ge(sem["xf_ready"], 1)
            act.activation(gatehigh[:], gate[:], ACT.Identity).then_inc(sem["gate_high"], 1)
            act.wait_ge(w_loaded[0], 32)
            act.activation(w13high[:, 0], w13[:, 0], ACT.Identity).then_inc(sem["we_high"], 1)
            act.activation(we2high[:, 0], we2[:, 0], ACT.Identity).then_inc(sem["we_high"], 1)
            with act.Fori(0, NIMG // 2) as j:
                for u in range(2):
                    k = 2 * j + u
                    act.wait_ge(sem["xfT_done"], k + 1)
                    act.activation(XT[:, :, at(k * T, T)], bank[u][:].rearrange("p (c k) -> p c k", c=KC),
                                   ACT.Identity).then_inc(sem["xfT_copied"], 1)
            act.wait_ge(sem["gate_shift"], 1)
            act.activation(gexp[:, :, 0:EXPERTS], gsh[:], ACT.Exp).then_inc(sem["gate_exp"], 1)

            def gated(n, q):
                act.wait_ge(sem["moe_h_done"], n + 1)
                act.wait_ge(sem["prod_ready"], CREDIT_PROD + n - 1)
                act.activation(silu[:, q % 2], bank[q % 2][:], ACT.Silu).then_inc(sem["silu_done"], 1)
                act.wait_ge(sem["prod_ready"], CREDIT_PROD + n + 1)
                act.wait_ge(sem["moe_out_done"], CREDIT_OUT + 2 * (n - 1))
                act.activation(hidhigh[:, q % 2], hid[:, q % 2], ACT.Identity).then_inc(sem["hid_high"], 1)

            with act.Fori(0, EXPERTS // 2) as j:
                for q in range(2 * NBLK):
                    gated(2 * NBLK * j + q, q)
                    u = q // NBLK
                    if q % NBLK == 1:
                        weights_high(2 * j + u + 1, 1 - u)
            for q in range(NBLK):
                gated(NBLK * EXPERTS + q, q)

        @block.vector
        def _(dve):
            def norm_stats(k, m, src, counted, found):
                for t in range(NT):
                    dve.bn_stats(stats[:, k, t], src(t)).then_inc(counted, 1)
                wait_apart(dve, counted, NT * (m + 1), sem["dve_carrier"])
                for t in range(NT):
                    dve.bn_aggr(mv[:, k, t], stats[:, k, t]).then_inc(found, 1)

            def inverse_root(v, r, m, done):
                y, a, b = r[:, 0], r[:, 1], r[:, 2]
                dve.tensor_scalar(y.bitcast(I32), v.bitcast(I32), -0.5, ROOT_BITS, ALU.mult, ALU.add
                                  ).then_inc(done, 1)
                for it in range(3):
                    dve.wait_ge(done, 10 * m + 3 * it + 1)
                    dve.scalar_tensor_tensor(out=a, in0=v, scalar=-0.5, in1=y, op0=ALU.mult, op1=ALU.mult
                                             ).then_inc(done, 1)
                    dve.wait_ge(done, 10 * m + 3 * it + 2)
                    dve.tensor_tensor(b, a, y, ALU.mult).then_inc(done, 1)
                    dve.wait_ge(done, 10 * m + 3 * it + 3)
                    dve.scalar_tensor_tensor(out=y, in0=b, scalar=1.5, in1=y, op0=ALU.add, op1=ALU.mult
                                             ).then_inc(done, 1)
                dve.wait_ge(done, 10 * m + 10)

            def tile_of(buf, m):
                return lambda t: buf[:, at(NT * m + t, 1)].rearrange("p a d -> p (a d)")

            def edge_sum(m):
                dve.wait_ge(sem["abs_ready"], 2 * (m + 1))
                dve.tensor_tensor(Hb[:, at(NT * m, NT)], edge[:, 0], edge[:, 1], ALU.add).then_inc(sem["h_ready"], 1)
                wait_apart(dve, sem["h_ready"], m + 1, sem["dve_carrier"])
                norm_stats(0, m, tile_of(Hb, m), sem["stats1"], sem["mv1"])

            def first_norms(m):
                v = mv[:, 0, :, 1]
                dve.wait_ge(sem["mv1"], NT * (m + 1))
                dve.tensor_scalar(vars1[:, 0], v, EPS, None, ALU.add).then_inc(sem["vars1"], 1)
                dve.tensor_scalar(vars1[:, 1], v, 1.0 + EPS, EPS * EPS, ALU.mult, ALU.add
                                  ).then_inc(sem["vars1"], 1)
                dve.wait_ge(sem["vars1"], 2 * (m + 1))
                inverse_root(vars1[:], root1, m, sem["root1"])

            def normalize_tokens(m, v):
                w(dve, sem["x2_ready"], m - 1)
                for t in range(NT):
                    dve.tensor_scalar(x1[:, v, t], tile_of(Hb, m)(t), mv[:, 0, t, 0:1],
                                      root1[:, 0, 0, t:t + 1], ALU.subtract, ALU.mult).then_inc(sem["x1_ready"], 1)

            def normalize_first(m):
                w(dve, sem["xT_done"], m)
                for t in range(NT):
                    dve.tensor_scalar(xhat[:, t], tile_of(Hb, m)(t), mv[:, 0, t, 0:1],
                                      root1[:, 0, 1, t:t + 1], ALU.subtract, ALU.mult).then_inc(sem["xhat_ready"], 1)

            def rope(m, t):
                dve.wait_ge(sem["qk_done"], NT * m + t + 1)
                w(dve, sem["rope_ready"], NT * (m - 1) + t + 1)
                qk = Fb[1 - t][:].rearrange("p (a h d) -> p a h d", a=2, h=HEADS)
                half = HD // 2
                cos = cosT[:, t].unsqueeze(2).broadcast_to([P, 2, HEADS, HD])
                sin = sinT[:, t].unsqueeze(2).broadcast_to([P, 2, HEADS, HD])
                dve.tensor_tensor(rcos[:, t], qk, cos, ALU.mult).then_inc(sem["rope_terms"], 1)
                dve.tensor_tensor(rsin[:, t, :, :, 0:half], qk[:, :, :, half:HD], sin[:, :, :, 0:half], ALU.mult
                                  ).then_inc(sem["rope_terms"], 1)
                dve.tensor_tensor(rsin[:, t, :, :, half:HD], qk[:, :, :, 0:half], sin[:, :, :, half:HD], ALU.mult
                                  ).then_inc(sem["rope_terms"], 1)

            def qkT_copy(m, v, n):
                t, qk = n // 4, n // 2 % 2
                dve.wait_ge(sem["qkT_done"], 8 * m + n + 1)
                dve.tensor_copy(QKT[:, v, qk, 4:8, t * P:t * P + P], Fb[0][:].rearrange("p (j k) -> p j k", j=4)
                                ).then_inc(sem["qkT_dve"], 1)

            def scale_out(l):
                dve.wait_ge(sem["wo_done"], l + 1)
                dve.tensor_tensor(wos[:], Fb[1][:].rearrange("p (t d) -> p t d", t=NT),
                                  ls1[:].unsqueeze(1).broadcast_to([P, NT, D]), ALU.mult).then_inc(sem["wo_scaled"], 1)

            def second_stats(l):
                wait_apart(dve, sem["x2_ready"], l + 1, sem["dve_carrier"])
                norm_stats(1, l, lambda t: x2[:, t], sem["stats2"], sem["mv2"])

            def second_norm(l):
                dve.wait_ge(sem["mv2"], NT * (l + 1))
                dve.tensor_scalar(vars2[:, 0], mv[:, 1, :, 1], EPS, None, ALU.add).then_inc(sem["vars2"], 1)
                dve.wait_ge(sem["vars2"], l + 1)
                inverse_root(vars2[:], root2, l, sem["root2"])
                for t in range(NT):
                    dve.tensor_scalar(xhat2[:, t], x2[:, t], mv[:, 1, t, 0:1], root2[:, 0, 0, t:t + 1],
                                      ALU.subtract, ALU.mult).then_inc(sem["xhat2_ready"], 1)

            def row_max(i, u, n):
                k = n % 3
                heads = 4 if k == 0 else 2
                dve.wait_ge(sem["scores_done"], UNITS * i + n + 1)
                dve.tensor_reduce(negmax[:, u, n, 0:heads], S[k][:].rearrange("p (h k) -> p h k", h=heads),
                                  AX.X, ALU.max, negate=True).then_inc(sem["negmax_ready"], 1)

            def pT_copy(i, n):
                dve.wait_ge(sem["pT_done"], UNITS * i + n + 1)
                w(dve, sem["pv_done"], UNITS * i + n - 2)
                dve.tensor_copy(pT[:, n % 3], TP[n % 2][:].rearrange("p (q k) -> p q k", q=4)).then_inc(sem["pT_copied"], 1)

            def divide(i, u, g):
                dve.wait_ge(sem["pv_done"], UNITS * i + 3 * (g + 1))
                dve.reciprocal(rinv[:, g], Ov[:, :, :, HD]).then_inc(sem["recip_ready"], 1)
                dve.wait_ge(sem["recip_ready"], NG * i + g + 1)
                ao = AO[:, u].rearrange("p t (a j b d) -> p t a j b d", a=2, j=4, d=HD)[:, :, g // 2, :, g % 2]
                dve.tensor_tensor(ao, Ov[:, :, :, 0:HD], rinv[:, g].unsqueeze(3).broadcast_to([P, NT, 4, HD]),
                                  ALU.mult).then_inc(sem["ao_ready"], 1)

            def step(i, u, front, tail):
                row_max(i, u, 0)
                row_max(i, u, 1)
                for n in range(UNITS):
                    if n + 2 < UNITS:
                        row_max(i, u, n + 2)
                    if front and n == 0:
                        edge_sum(i + 1)
                    if front and n == 1:
                        first_norms(i + 1)
                    if front and n == 2:
                        normalize_first(i + 1)
                    if tail and n == 2:
                        scale_out(i - 1)
                    if tail and n == 4:
                        second_stats(i - 1)
                    if front and n in (4, 5):
                        rope(i + 1, n - 4)
                    if tail and n == 6:
                        second_norm(i - 1)
                    if front and n == 6:
                        normalize_tokens(i + 1, 1 - u)
                    if front and n >= 8:
                        qkT_copy(i + 1, 1 - u, 2 * (n - 8) + 1)
                    pT_copy(i, n)
                    if n % 3 == 0 and n:
                        divide(i, u, n // 3 - 1)
                divide(i, u, NG - 1)

            dve.wait_ge(sem["filter_loaded"], 16 * len(filters))
            for dy in range(3):
                if dy:
                    dve.wait_ge(sem["band_part"], 6 * dy)
                for f in range(2):
                    for dx in range(3):
                        tap = schr[:, 9 * f + 3 * dy + dx:9 * f + 3 * dy + dx + 1]
                        o = band[:, f, dx]
                        done = sem["band_ready"] if dy == 2 else sem["band_part"]
                        if dy == 0:
                            dve.tensor_scalar(o, shf[:, dy], tap, None, ALU.mult).then_inc(done, 1)
                        else:
                            dve.scalar_tensor_tensor(out=o, in0=shf[:, dy], scalar=tap, in1=o,
                                                     op0=ALU.mult, op1=ALU.add).then_inc(done, 1)
            edge_sum(0)
            first_norms(0)
            normalize_first(0)
            normalize_tokens(0, 0)
            dve.wait_ge(sem["const_a"], 16 * len(first_constants))
            rope(0, 0)
            rope(0, 1)
            for n in range(1, 8, 2):
                qkT_copy(0, 0, n)
            dve.wait_ge(sem["const_b"], 16 * len(later_constants))
            step(0, 0, True, False)
            with dve.Fori(0, (NIMG - 2) // 2) as j:
                step(2 * j + 1, 1, True, True)
                step(2 * j + 2, 0, True, True)
            step(NIMG - 1, 1, False, True)
            scale_out(NIMG - 1)
            second_stats(NIMG - 1)
            second_norm(NIMG - 1)

            dve.sem_inc(sem["ffn_bias"], CREDIT_BIAS)
            dve.wait_ge(sem["base_ready"], CREDIT_LOW + NIMG)
            with dve.Fori(0, NBLK // 2) as j:
                for q in range(4):
                    r = 4 * j + q
                    dve.wait_ge(sem["ffn2_done"], CREDIT_FFN2 + r + 1)
                    y = fb[:, q % 2]
                    dve.tensor_tensor(y, Y[q % 2][:].rearrange("p (t d) -> p t d", t=2),
                                      b2[:].unsqueeze(1).broadcast_to([P, 2, D]), ALU.add).then_inc(sem["ffn_bias"], 1)
                    dve.wait_ge(sem["ffn_bias"], CREDIT_BIAS + r + 1)
                    dve.tensor_tensor(fs[:, q % 2], y, ls2[:].unsqueeze(1).broadcast_to([P, 2, D]),
                                      ALU.mult).then_inc(sem["ffn_scaled"], 1)
                    dve.wait_ge(sem["ffn_scaled"], r + 1)
                    h = Hb[:, at(2 * r, 2)]
                    dve.tensor_tensor(h, h, fs[:, q % 2], ALU.add).then_inc(sem["h3_ready"], 1)
                    wait_apart(dve, sem["h3_ready"], r + 1, sem["dve_carrier"])
                    for t in range(2):
                        dve.bn_stats(stats3[:, at(2 * r + t, 1)].rearrange("p a d -> p (a d)"),
                                     tile_of(Hb, r)(t)).then_inc(sem["stats3"], 1)

            dve.wait_ge(sem["stats3"], TILES)
            for k in range(TILES):
                dve.bn_aggr(mv3[:, k], stats3[:, k]).then_inc(sem["mv3"], 1)
            dve.wait_ge(sem["mv3"], TILES)
            dve.tensor_scalar(vars3[:, 0], mv3[:, :, 1], EPS, None, ALU.add).then_inc(sem["vars3"], 1)
            dve.wait_ge(sem["vars3"], 1)
            inverse_root(vars3[:], root3, 0, sem["root3"])
            dve.sem_inc(sem["xfT_low"], CREDIT_XFT)

            def low_part(k):
                dve.wait_ge(sem["xfT_copied"], k + 1)
                tokens = slice(k * T, k * T + T)
                dve.tensor_tensor(XTlow[:, :, tokens], bank[k % 2][:].rearrange("p (c k) -> p c k", c=KC),
                                  XT[:, :, tokens].bitcast(F32), ALU.subtract).then_inc(sem["xfT_low"], 1)

            for k in range(NIMG):
                w(dve, sem["xfT_done"], k - 1)
                for t in range(NT):
                    n = NT * k + t
                    dve.tensor_scalar(XF[:, k % 2, t], Hb[:, n], mv3[:, n, 0:1], root3[:, 0, 0, n:n + 1],
                                      ALU.subtract, ALU.mult).then_inc(sem["xf_ready"], 1)
                if k:
                    low_part(k - 1)
            low_part(NIMG - 1)
            dve.wait_ge(sem["gate_high"], 1)
            dve.tensor_tensor(gatelow[:], gate[:], gatehigh[:].bitcast(F32), ALU.subtract).then_inc(sem["gate_low"], 1)
            dve.memset(comb[:, EXPERTS], 1.0).then_inc(sem["keys_set"], 1)
            for k in range(TOPK):
                dve.memset(gexp[:, :, EXPERTS + k:EXPERTS + k + 1], -1.0 - k).then_inc(sem["keys_set"], 1)
                dve.memset(keys[:, :, TOPK + k:TOPK + k + 1], -1.0 - k).then_inc(sem["keys_set"], 1)
            logits = gate_bank[:, 0:TILES * EXPERTS].rearrange("p (k e) -> p k e", e=EXPERTS)
            dve.wait_ge(sem["gate_done"], 1)
            dve.tensor_reduce(gmax[:], logits, AX.X, ALU.max).then_inc(sem["gate_max"], 1)
            dve.wait_ge(sem["gate_max"], 1)
            dve.tensor_tensor(gsh[:], logits, gmax[:].unsqueeze(2).broadcast_to([P, TILES, EXPERTS]),
                              ALU.subtract).then_inc(sem["gate_shift"], 1)
            dve.wait_ge(sem["gate_exp"], 1)
            for k in range(TILES):
                dve.max(top8[:, k], gexp[:, k, 0:EXPERTS]).then_inc(sem["top_ready"], 1)
            dve.wait_ge(sem["top_ready"], TILES)
            dve.wait_ge(sem["keys_set"], 9)
            dve.tensor_copy(keys[:, :, 0:TOPK], top8[:, :, 0:TOPK]).then_inc(sem["keys_ready"], 1)
            dve.tensor_reduce(tsum[:], top8[:, :, 0:TOPK], AX.X, ALU.add).then_inc(sem["sum_ready"], 1)
            dve.wait_ge(sem["keys_ready"], 1)
            for k in range(TILES):
                dve.match_replace(repl[:, k], keys[:, k], gexp[:, k], -9.0).then_inc(sem["replaced"], 1)
            dve.wait_ge(sem["sum_ready"], 1)
            dve.reciprocal(tinv[:], tsum[:]).then_inc(sem["inv_ready"], 1)
            dve.wait_ge(sem["replaced"], TILES)
            dve.scalar_tensor_tensor(out=pick[:], in0=repl[:, :, 0:EXPERTS], scalar=-8.0, in1=gexp[:, :, 0:EXPERTS],
                                     op0=ALU.is_lt, op1=ALU.mult).then_inc(sem["picked"], 1)
            dve.wait_ge(sem["picked"], 1)
            dve.wait_ge(sem["inv_ready"], 1)
            dve.tensor_tensor(comb[:, 0:EXPERTS].rearrange("p e k -> p k e"), pick[:],
                              tinv[:].unsqueeze(2).broadcast_to([P, TILES, EXPERTS]), ALU.mult
                              ).then_inc(sem["combine_ready"], 1)

            def product(n, q):
                dve.wait_ge(sem["silu_done"], n + 1)
                dve.wait_ge(sem["hid_low"], CREDIT_HID + n - 1)
                dve.tensor_tensor(hid[:, q % 2], silu[:, q % 2], bank[2 + q % 2][:], ALU.mult
                                  ).then_inc(sem["prod_ready"], 1)

            def accumulate(n, q, e):
                for t in range(BT):
                    if t % 2 == 0:
                        dve.wait_ge(sem["moe_out_done"], CREDIT_OUT + 2 * n + t // 2 + 1)
                    k = BT * (q % NBLK) + t
                    y = bank[4 + 2 * (q % 2) + t // 2][:, (t % 2) * D:(t % 2) * D + D]
                    dve.wait_ge(sem["acc_ready"], CREDIT_ACC + BT * (n - 1) + t)
                    dve.scalar_tensor_tensor(out=Hb[:, k], in0=y,
                                             scalar=comb[:, at(e, 1), k:k + 1].rearrange("p a b -> p (a b)"),
                                             in1=Hb[:, k], op0=ALU.mult, op1=ALU.add).then_inc(sem["acc_ready"], 1)

            dve.sem_inc(sem["prod_ready"], CREDIT_PROD)
            dve.sem_inc(sem["acc_ready"], CREDIT_ACC)
            dve.wait_ge(sem["combine_ready"], 1)
            product(0, 0)
            with dve.Fori(0, EXPERTS // 2) as j:
                for q in range(2 * NBLK):
                    product(2 * NBLK * j + q + 1, (q + 1) % (2 * NBLK))
                    accumulate(2 * NBLK * j + q, q, 2 * j + q // NBLK)
            for q in range(NBLK):
                if q + 1 < NBLK:
                    product(NBLK * EXPERTS + q + 1, q + 1)
                accumulate(NBLK * EXPERTS + q, q, EXPERTS)


def kernel(**inputs):
    import concourse.bacc as bacc
    import ml_dtypes
    from concourse.bass_utils import run_bass_kernel_spmd

    f = {k: np.asarray(v) for k, v in inputs.items()}

    def chunks(a, rows=P):
        return np.ascontiguousarray(a.reshape(-1, rows, a.shape[-1]).transpose(1, 0, 2))

    def rows(a):
        return np.ascontiguousarray(np.broadcast_to(a, (P, a.size)))

    def columns(a):
        return np.ascontiguousarray(a.reshape(-1, P).T)

    k, m = np.arange(P)[:, None], np.arange(P)[None, :]
    shift = np.stack([(k == m + dy - 1) for dy in range(3)], 1).astype(np.float32)
    ident = np.eye(P, dtype=np.float32)
    q = np.arange(P)[:, None]
    far = np.arange(2 * P)[None, :]
    mask0 = np.where((q - m >= 0) & (q - m < WINDOW), 0.0, MASKED).astype(ml_dtypes.bfloat16)
    mask1 = np.where((P + q - far >= 0) & (P + q - far < WINDOW), 0.0, MASKED).astype(ml_dtypes.bfloat16)
    inv_freq = (np.float32(1.0) / np.float32(10000.0) ** (np.arange(0, HD, 2, dtype=np.float32) / np.float32(HD)))
    angle = np.outer(np.arange(T, dtype=np.float32), inv_freq.astype(np.float32)).astype(np.float32)
    cos = np.concatenate([np.cos(angle), np.cos(angle)], 1)
    sin = np.concatenate([-np.sin(angle), np.sin(angle)], 1)
    scale = np.float32(HD ** -0.5)

    def table(a):
        both = np.stack([a * scale, a], 1).astype(np.float32)
        return np.ascontiguousarray(both.reshape(NT, P, 2, HD).transpose(1, 0, 2, 3))

    a = "L0_attn_"
    e1 = np.concatenate([f["L0_ffn_w1"], f["L0_ffn_sw1"][None]])
    e3 = np.concatenate([f["L0_ffn_w3"], f["L0_ffn_sw3"][None]])
    e2 = np.concatenate([f["L0_ffn_w2"], f["L0_ffn_sw2"][None]])
    e13 = np.concatenate([e1, e3], 1).transpose(0, 2, 1)
    arrays = {
        "x": f["x"], "shift": shift, "scharr_rows": rows(f["L0_tok_scharr"].reshape(-1)),
        "scharr": f["L0_tok_scharr"], "ident": ident, "ident16": ident.astype(ml_dtypes.bfloat16),
        "mask0": mask0, "mask1": mask1, "rope_cos_t": table(cos), "rope_sin_t": table(sin),
        "wqkT": chunks(np.concatenate([f[a + "wq"].T, f[a + "wk"].T], 1)), "wvT": chunks(f[a + "wv"].T),
        "woT": chunks(f[a + "wo"].T), "ls1_rows": rows(f[a + "ls1"]),
        "n1w": columns(f[a + "norm1_w"]), "n1b": columns(f[a + "norm1_b"]),
        "n2w": columns(f[a + "norm2_w"]), "n2b": columns(f[a + "norm2_b"]),
        "w1T": chunks(f[a + "w1"].T), "b1": columns(f[a + "b1"]), "w2T": chunks(f[a + "w2"].T),
        "b2_rows": rows(f[a + "b2"]), "ls2_rows": rows(f[a + "ls2"]), "gateT": chunks(f["L0_ffn_gate_w"].T),
        "e13T": np.ascontiguousarray(e13.reshape(EXPERTS + 1, KC, P, 2 * HID).transpose(2, 0, 1, 3)),
        "e2T": np.ascontiguousarray(e2.transpose(2, 0, 1)),
    }
    nc = bacc.Bacc("TRN2", target_bir_lowering=False, num_devices=1)
    aps = {k: nc.dram_tensor(f"in_{k}", v.shape, mybir.dt.from_np(v.dtype), kind="ExternalInput").ap()
           for k, v in arrays.items()}
    result = nc.dram_tensor("result", (NIMG, T, D), F32, kind="ExternalOutput").ap()
    build(nc, out=result, **aps)
    r = run_bass_kernel_spmd(nc, [{f"in_{k}": v for k, v in arrays.items()}], core_ids=[0])
    return r.results[0]["result"]
```

```python
from contextlib import ExitStack

import numpy as np

import concourse.bass as bass
from concourse import mybir

F32 = mybir.dt.float32
F32R = mybir.dt.float32r
I32 = mybir.dt.int32
BF16 = mybir.dt.bfloat16
ALU = mybir.AluOpType
ACT = mybir.ActivationFunctionType
AX = mybir.AxisListType

P = 128
NIMG, NCH, D = 8, 3, 256
T = 256
NT = T // P
KC = D // P
TILES = NIMG * NT
HEADS, HD = 16, 16
PARTS = 4
PAIRS = HEADS // 2
ROWS = PARTS * HD
WINDOW = 125
FFN = 1024
FC = FFN // P
EXPERTS, HID, TOPK = 16, 128, 4
BLK = 512
NBLK = NIMG * T // BLK
BT = BLK // P
GRAY = (0.2989, 0.587, 0.114)
EPS = 1e-5
ROOT_BITS = float(0x5F3759DF)
MASKED = -1e30
NG = 4
RAW_SLOTS = (3, 4, 5, 6, 8, 9, 10, 11)
UNITS = 3 * NG

STAGES = """
x_loaded0 x_loaded1 halo_loaded0 halo_loaded1 halo_band_loaded filter_loaded const_a const_b w_loaded0 w_loaded1 memset_done pool_carrier dve_carrier pe_carrier ones_set
gray_first gray_part gray_ready band_part band_ready conv_done abs_ready h_ready
stats1 mv1 vars1 root1 x1_ready xhat_ready
xT_done hT_ready qk_done v_done rope_terms rope_ready rope_high rope_low v_ready qkT_done qkT_act qkT_dve
scores_done negmax_ready exp_done pT_done pT_copied pv_done recip_ready ao_ready
aoT_done aoT_copied wo_done wo_scaled x2_ready base_part base_ready bias_scaled
stats2 mv2 vars2 root2 xhat2_ready x2T_done h2_ready h2T_ready h2T_low
w1_high w1_low w2_high w2_low ffn1_done raw_saved gelu_done hidden_high hidden_low ffn2_done ffn_scaled h3_ready stats3 mv3 vars3 root3 xf_ready
xfT_done xfT_copied xfT_low gate_high gate_low gateT_done gateT_copied gate_done gate_max gate_shift gate_exp top_ready keys_set keys_ready replaced picked
sum_ready inv_ready combine_ready we_high we_low moe_h_done silu_done prod_ready hid_high hid_low moe_out_done acc_ready out_stored
""".split()


def build(nc, x, shift, scharr_rows, scharr, ident, ident16, mask0, mask1, rope_cos_t, rope_sin_t,
          wqkT, wvT, woT, ls1_rows, n1w, n1b, n2w, n2b, w1T, b1, w2T, b2_rows, ls2_rows,
          gateT, e13T, e2T, out):
    with ExitStack() as ctx:
        def sb(name, shape, dt=F32, until=ctx):
            return until.enter_context(nc.sbuf_tensor(name, shape, dt))

        def ps(name, shape):
            return ctx.enter_context(nc.psum_tensor(name, shape, F32))

        sem = {n: ctx.enter_context(nc.semaphore(n)) for n in STAGES}

        idf = sb("idf", [P, P])
        idb = sb("idb", [P, P], BF16)
        msk0 = sb("msk0", [P, P], BF16)
        msk1 = sb("msk1", [P, 2 * P], BF16)
        wo = sb("wo", [P, KC, D])
        ls1 = sb("ls1", [P, D])
        ls2 = sb("ls2", [P, D])
        b2 = sb("b2", [P, D])
        norm_wb = sb("norm_wb", [P, 4, KC])
        w1 = sb("w1", [P, KC, FFN])
        b1c = sb("b1c", [P, FC])
        w2 = sb("w2", [P, FC, D])
        gate = sb("gate", [P, KC, EXPERTS])

        Hb = sb("Hb", [P, TILES, D])
        XT = sb("XT", [P, KC, NIMG * T], F32R)
        XTlow = sb("XTlow", [P, KC, NIMG * T], F32R)
        stats3 = sb("stats3", [P, BT, 6])
        mv3 = sb("mv3", [P, BT, 2])
        vars3 = sb("vars3", [P, 1, BT])
        root3 = sb("root3", [P, 3, 1, BT])

        with ExitStack() as phase:
            xin = sb("xin", [P, 2, NCH, NT, D], until=phase)
            gray = sb("gray", [P, 2, NT, D + 2], until=phase)
            halo = sb("halo", [3, 2, NT, D], until=phase)
            edge = sb("edge", [P, 2, NT, D], until=phase)
            xhat = sb("xhat", [P, NT, D], until=phase)
            hT = sb("hT", [P, KC, T], until=phase)
            rcos = sb("rcos", [P, 2, 2, HEADS, HD], until=phase)
            rsin = sb("rsin", [P, 2, 2, HEADS, HD], until=phase)
            cosT = sb("cosT", [P, NT, 2, HD], until=phase)
            sinT = sb("sinT", [P, NT, 2, HD], until=phase)
            shf = sb("shf", [P, 3, P], until=phase)
            schr = sb("schr", [P, 18], until=phase)
            band = sb("band", [P, 2, 3, P], until=phase)
            halo_band = sb("halo_band", [3, 2, NT, P], until=phase)
            wqk = sb("wqk", [P, KC, 2 * D], until=phase)
            wv = sb("wv", [P, KC, D], until=phase)
            qkr = sb("qkr", [P, NT, 2, HEADS, HD], until=phase)
            qks = sb("qks", [P, NT, 2, HEADS, PARTS, HD], F32R, phase)
            V = sb("V", [P, 2, NT, HEADS, HD + 1], until=phase)
            QKT = sb("QKT", [P, 2, 2, PAIRS, T], F32R, phase)
            negmax = sb("negmax", [P, 2, UNITS, 4], until=phase)
            prob = sb("prob", [P, 2, 512], until=phase)
            pT = sb("pT", [P, 3, 4, P], until=phase)
            rinv = sb("rinv", [P, NG, NT, 4], until=phase)
            AO = sb("AO", [P, 2, NT, D], until=phase)
            x1 = sb("x1", [P, 2, NT, D], until=phase)
            x2 = sb("x2", [P, NT, D], until=phase)
            aoT = sb("aoT", [P, KC, T], until=phase)
            wos = sb("wos", [P, NT, D], until=phase)
            xhat2 = sb("xhat2", [P, NT, D], until=phase)
            h2 = sb("h2", [P, KC, T], until=phase)
            stats = sb("stats", [P, 2, NT, 6], until=phase)
            mv = sb("mv", [P, 2, NT, 2], until=phase)
            vars1 = sb("vars1", [P, 2, NT], until=phase)
            vars2 = sb("vars2", [P, 1, NT], until=phase)
            root1 = sb("root1", [P, 3, 2, NT], until=phase)
            root2 = sb("root2", [P, 3, 1, NT], until=phase)

        w13 = sb("w13", [P, 2, KC, 2 * HID])
        we2 = sb("we2", [P, 2, D])
        w1high = sb("w1high", [P, KC, FFN], F32R)
        w1low = sb("w1low", [P, KC, FFN], F32R)
        w2high = sb("w2high", [P, FC, D], F32R)
        w2low = sb("w2low", [P, FC, D], F32R)
        with ExitStack() as first_block:
            raw = sb("raw", [P, FC, BLK], until=first_block)
        G = sb("G", [P, FC, BLK], F32R)
        Glow = sb("Glow", [P, FC, BLK], F32R)
        gelu = sb("gelu", [P, 2, BLK])
        fs = sb("fs", [P, 2, 2, D])
        XF = sb("XF", [P, 2, NT, D])
        gatehigh = sb("gatehigh", [P, KC, EXPERTS], F32R)
        gatelow = sb("gatelow", [P, KC, EXPERTS], F32R)
        logitsT = sb("logitsT", [EXPERTS, BLK])
        gmax = sb("gmax", [P, BT])
        gsh = sb("gsh", [P, BT, EXPERTS])
        gexp = sb("gexp", [P, BT, EXPERTS + TOPK])
        top8 = sb("top8", [P, BT, 8])
        keys = sb("keys", [P, BT, 8])
        repl = sb("repl", [P, BT, EXPERTS + TOPK])
        pick = sb("pick", [P, BT, EXPERTS])
        tsum = sb("tsum", [P, BT])
        tinv = sb("tinv", [P, BT])
        comb = sb("comb", [P, EXPERTS + 1, TILES])
        w13high = sb("w13high", [P, 2, KC, 2 * HID], F32R)
        w13low = sb("w13low", [P, 2, KC, 2 * HID], F32R)
        we2high = sb("we2high", [P, 2, D], F32R)
        we2low = sb("we2low", [P, 2, D], F32R)
        silu = sb("silu", [P, 2, BLK])
        hid = sb("hid", [P, 2, BLK])
        hidhigh = sb("hidhigh", [P, 2, BLK], F32R)
        hidlow = sb("hidlow", [P, 2, BLK], F32R)

        bank = [ps(f"bank{n}", [P, 512]) for n in range(8)]
        S, TP, O, Fb = bank[0:3], bank[3:5], bank[5], bank[6:8]
        Ov = O[:, 0:NT * 4 * (HD + 1)].rearrange("p (t h d) -> p t h d", t=NT, h=4)

        def w(eng, signal, value):
            if not (isinstance(value, int) and value <= 0):
                eng.wait_ge(signal, value)

        def wait_apart(eng, signal, value, carrier):
            eng.wait_ge(signal, value)
            if not isinstance(value, int):
                eng.sem_inc(carrier, 1)

        filters = ((shf[:], shift), (schr[:], scharr_rows))
        first_constants = (
            (idf[:], ident), (wqk[:], wqkT), (wv[:], wvT),
            (norm_wb[:, 0], n1w), (norm_wb[:, 1], n1b), (cosT[:], rope_cos_t), (sinT[:], rope_sin_t),
            (idb[:], ident16), (msk0[:], mask0), (msk1[:], mask1))
        later_constants = (
            (wo[:], woT), (ls1[:], ls1_rows), (norm_wb[:, 2], n2w), (norm_wb[:, 3], n2b),
            (w1[:], w1T), (b1c[:], b1), (w2[:], w2T), (b2[:], b2_rows), (ls2[:], ls2_rows), (gate[:], gateT))

        def at(n, count):
            return slice(n, n + count) if isinstance(n, int) else bass.ds(n, count)

        xv = x.rearrange("i c (t p) d -> p i c t d", p=P)
        ov = out.rearrange("i (t p) d -> p (i t) d", p=P)
        x_loaded = (sem["x_loaded0"], sem["x_loaded1"])
        halo_loaded = (sem["halo_loaded0"], sem["halo_loaded1"])
        w_loaded = (sem["w_loaded0"], sem["w_loaded1"])
        Y = [bank[4], bank[5]]
        turn_bank = [bank[6], bank[7]]
        gate_bank = bank[7]
        CREDIT_GELU, CREDIT_SCALED = 4, 2
        CREDIT_PROD, CREDIT_OUT, CREDIT_ACC = 2, 4, 8
        CREDIT_HIDDEN, CREDIT_HID, CREDIT_LOW = 2, 2, 1

        def tap(f, dy, dx):
            k = 9 * f + 3 * dy + dx
            return schr[:, k:k + 1]

        block = ctx.enter_context(nc.Block())

        @block.sync
        def _(sp):
            def load_x(i, u):
                w(sp, sem["gray_ready"], i - 1)
                for c in range(NCH):
                    sp.dma_start(xin[:, u, c], xv[:, at(i, 1), c].rearrange("p i t d -> p (i t) d")
                                 ).then_inc(x_loaded[u], 16)

            def load_halo(m, u):
                sp.wait_ge(sem["gray_ready"], m + 1)
                for t in range(NT):
                    row = gray[(0, P - 1)[t]:(1, P)[t], u, 1 - t, :]
                    shifts = bass.AP(tensor=row.tensor, offset=row.offset, ap=[row.ap[0], [1, 3], [1, D]])
                    sp.dma_start(halo[:, u, t], shifts).then_inc(halo_loaded[u], 16)

            load_x(0, 0)
            for dst, src in filters:
                sp.dma_start(dst, src).then_inc(sem["filter_loaded"], 16)
            sp.wait_ge(sem["memset_done"], 1)
            for t in range(NT):
                dy, col = (2, P - 1) if t == 0 else (0, 0)
                for f in range(2):
                    sp.dma_start(halo_band[:, f, t, col:col + 1],
                                 scharr[f, 0, dy:dy + 1, :].rearrange("a d -> d a")
                                 ).then_inc(sem["halo_band_loaded"], 16)
            for dst, src in first_constants[:5]:
                sp.dma_start(dst, src).then_inc(sem["const_a"], 16)
            load_halo(0, 0)
            for dst, src in first_constants[5:]:
                sp.dma_start(dst, src).then_inc(sem["const_a"], 16)
            load_x(1, 1)
            for dst, src in later_constants:
                sp.dma_start(dst, src).then_inc(sem["const_b"], 16)

            def load_expert(e, u):
                w(sp, sem["we_low"], 2 * (e - 1))
                sp.dma_start(w13[:, u], e13T[:, at(e, 1)].rearrange("p e c h -> p (e c) h")).then_inc(w_loaded[u], 16)
                sp.dma_start(we2[:, u], e2T[:, at(e, 1)].rearrange("p e d -> p (e d)")).then_inc(w_loaded[u], 16)

            load_halo(1, 1)
            with sp.Fori(1, NIMG // 2) as j:
                for u in range(2):
                    load_x(2 * j + u, u)
                    load_halo(2 * j + u, u)
            load_expert(0, 0)
            load_expert(1, 1)
            with sp.Fori(1, EXPERTS // 2) as j:
                for u in range(2):
                    load_expert(2 * j + u, u)
            load_expert(EXPERTS, 0)
            for b in range(NBLK):
                sp.wait_ge(sem["acc_ready"], CREDIT_ACC + BT * (NBLK * EXPERTS + b + 1))
                sp.dma_start(ov[:, BT * b:BT * b + BT], Hb[:, BT * b:BT * b + BT]).then_inc(sem["out_stored"], 16)
            sp.wait_ge(sem["out_stored"], 16 * NBLK)

        @block.gpsimd
        def _(pool):
            pool.sem_inc(sem["h2T_low"], CREDIT_LOW)
            pool.sem_inc(sem["base_ready"], CREDIT_LOW)
            pool.memset(halo_band[:], 0.0).then_inc(sem["memset_done"], 1)
            pool.memset(gray[:], 0.0).then_inc(sem["memset_done"], 1)
            pool.wait_ge(sem["memset_done"], 2)

            def make_gray(i, u):
                w(pool, sem["conv_done"], 2 * (i - 1))
                wait_apart(pool, x_loaded[u], 8 * NCH * (i - u) + 16 * NCH, sem["pool_carrier"])
                g = gray[:, u, :, 1:D + 1]
                for c in range(NCH):
                    pool.tensor_scalar(xin[:, u, c], xin[:, u, c], GRAY[c], None, ALU.mult).then_inc(sem["gray_part"], 1)
                pool.wait_ge(sem["gray_part"], 4 * i - 1)
                pool.tensor_tensor(g, xin[:, u, 0], xin[:, u, 1], ALU.add).then_inc(sem["gray_part"], 1)
                pool.wait_ge(sem["gray_part"], 4 * i)
                pool.tensor_tensor(g, g, xin[:, u, 2], ALU.add).then_inc(sem["gray_ready"], 1)

            def rope_add(m, t):
                pool.wait_ge(sem["rope_terms"], 3 * (NT * m + t + 1))
                w(pool, sem["rope_low"], 4 * (m - 1) + 2 * t + 2)
                pool.tensor_tensor(qkr[:, t], rcos[:, t], rsin[:, t], ALU.add).then_inc(sem["rope_ready"], 1)

            def rope_low(m, t):
                for qk, (high, low) in enumerate(((slice(0, 4, 2), slice(1, 4, 2)), (slice(0, 2), slice(2, 4)))):
                    pool.wait_ge(sem["rope_high"], 4 * m + 2 * t + qk + 1)
                    pool.tensor_tensor(qks[:, t, qk, :, low], qkr[:, t, qk].unsqueeze(2).broadcast_to([P, HEADS, 2, HD]),
                                       qks[:, t, qk, :, high].bitcast(F32), ALU.subtract).then_inc(sem["rope_low"], 1)

            def residual(l, u):
                pool.wait_ge(sem["wo_scaled"], l + 1)
                pool.wait_ge(sem["base_ready"], CREDIT_LOW + l)
                pool.tensor_tensor(x2[:], wos[:], x1[:, u], ALU.add).then_inc(sem["x2_ready"], 1)

            def base_bias(l):
                h = Hb[:, at(NT * l, NT)]
                pool.tensor_tensor(h, h, b2[:].unsqueeze(1).broadcast_to([P, NT, D]), ALU.add
                                   ).then_inc(sem["base_part"], 1)

            def base(l):
                h = Hb[:, at(NT * l, NT)]
                pool.wait_ge(sem["x2_ready"], l + 1)
                wait_apart(pool, sem["base_part"], l + 1, sem["pool_carrier"])
                pool.tensor_tensor(h, h, x2[:], ALU.add).then_inc(sem["base_ready"], 1)

            def h2_low(l):
                pool.wait_ge(sem["h2T_ready"], l + 1)
                at_l = at(l * T, T)
                pool.tensor_tensor(XTlow[:, :, at_l], h2[:], XT[:, :, at_l].bitcast(F32), ALU.subtract
                                   ).then_inc(sem["h2T_low"], 1)

            def step(i, u, front, tail, gray_next):
                if gray_next:
                    make_gray(i + 2, u)
                if tail:
                    residual(i - 1, 1 - u)
                    base_bias(i - 1)
                    base(i - 1)
                if front:
                    for t in range(NT):
                        rope_add(i + 1, t)
                    for t in range(NT):
                        rope_low(i + 1, t)
                if tail:
                    h2_low(i - 1)

            pool.memset(V[:], 1.0).then_inc(sem["ones_set"], 1)
            pool.wait_ge(sem["gray_first"], NCH)
            pool.sem_inc(sem["gray_ready"], 1)
            make_gray(1, 1)
            for t in range(NT):
                rope_add(0, t)
            for t in range(NT):
                rope_low(0, t)
            pool.wait_ge(sem["const_b"], 16 * len(later_constants))
            pool.tensor_tensor(b2[:], b2[:], ls2[:], ALU.mult).then_inc(sem["bias_scaled"], 1)
            pool.wait_ge(sem["bias_scaled"], 1)
            step(0, 0, True, False, True)
            with pool.Fori(0, (NIMG - 4) // 2) as j:
                step(2 * j + 1, 1, True, True, True)
                step(2 * j + 2, 0, True, True, True)
            step(NIMG - 3, 1, True, True, True)
            step(NIMG - 2, 0, True, True, False)
            pool.wait_ge(sem["w1_high"], 1)
            pool.tensor_tensor(w1low[:], w1[:], w1high[:].bitcast(F32), ALU.subtract).then_inc(sem["w1_low"], 1)
            residual(NIMG - 2, 0)
            base_bias(NIMG - 2)
            base(NIMG - 2)
            pool.wait_ge(sem["w2_high"], 1)
            pool.tensor_tensor(w2low[:], w2[:], w2high[:].bitcast(F32), ALU.subtract).then_inc(sem["w2_low"], 1)
            h2_low(NIMG - 2)
            base_bias(NIMG - 1)

            pool.sem_inc(sem["hidden_low"], CREDIT_HIDDEN)

            def block_low(b, columns):
                for f in columns:
                    pool.wait_ge(sem["hidden_high"], FC * b + f + 1)
                    pool.tensor_tensor(Glow[:, f], gelu[:, f % 2], G[:, f].bitcast(F32), ALU.subtract
                                       ).then_inc(sem["hidden_low"], 1)

            block_low(0, range(0, 3))
            residual(NIMG - 1, 1)
            block_low(0, range(3, FC))
            pool.wait_ge(sem["gate_high"], 1)
            pool.tensor_tensor(gatelow[:], gate[:], gatehigh[:].bitcast(F32), ALU.subtract).then_inc(sem["gate_low"], 1)
            base(NIMG - 1)
            h2_low(NIMG - 1)
            with pool.Fori(1, NBLK) as b:
                block_low(b, range(FC))

            def weights_low(e, u, part):
                pool.wait_ge(sem["we_high"], 2 * e + part + 1)
                whole, high, low = ((w13, w13high, w13low), (we2, we2high, we2low))[part]
                pool.tensor_tensor(low[:, u], whole[:, u], high[:, u].bitcast(F32), ALU.subtract
                                   ).then_inc(sem["we_low"], 1)

            def hidden_low(n, q):
                pool.wait_ge(sem["hid_high"], n + 1)
                pool.tensor_tensor(hidlow[:, q % 2], hid[:, q % 2], hidhigh[:, q % 2].bitcast(F32), ALU.subtract
                                   ).then_inc(sem["hid_low"], 1)

            weights_low(0, 0, 0)
            weights_low(0, 0, 1)
            pool.sem_inc(sem["hid_low"], CREDIT_HID)
            hidden_low(0, 0)
            hidden_low(1, 1)
            with pool.Fori(0, EXPERTS // 2) as j:
                for q in range(2, 2 * NBLK + 2):
                    hidden_low(2 * NBLK * j + q, q)
                    if q % NBLK in (2, 3):
                        weights_low(2 * j + q // NBLK + 1, (q // NBLK + 1) % 2, q % NBLK - 2)
            for q in range(2, NBLK):
                hidden_low(NBLK * EXPERTS + q, q)

        @block.tensor
        def _(pe):
            def in_parts(pe, dst, factors, first=True, last=True):
                factors = [(tuple(a), tuple(b)) for a, b in factors]
                steps = ([(a[0], y) for a, b in factors for y in b] + [(a[1], b[0]) for a, b in factors])
                for n, (left, right) in enumerate(steps):
                    mm = pe.matmul(dst, left, right, start=(first and n == 0), stop=(last and n == len(steps) - 1))
                return mm

            def conv(m, v):
                pe.wait_ge(sem["gray_ready"], m + 1)
                w(pe, sem["qkT_act"], 4 * m)
                w(pe, sem["qkT_dve"], 4 * m)
                for f in range(2):
                    for dx in range(3):
                        pe.matmul(Fb[f][:], band[:, f, dx], gray[:, v, :, dx:dx + D], start=(dx == 0), stop=False)
                    if f == 0:
                        pe.wait_ge(halo_loaded[v], 8 * NT * (m - v) + 16 * NT)
                    for t in range(NT):
                        mm = pe.matmul(Fb[f][:, t * D:t * D + D], halo_band[:, f, t],
                                       halo[:, v, t],
                                       start=False, stop=(t == NT - 1))
                    mm.then_inc(sem["conv_done"], 1)

            def turn(dst, src):
                for c in range(KC):
                    for t in range(NT):
                        mm = pe.transpose(dst[:, c * T + t * P:c * T + t * P + P], src[:, t, c * P:c * P + P], idf[:])
                return mm

            def project(dst, src, weights):
                for t in range(NT):
                    for c in range(KC):
                        mm = pe.matmul(dst[:, t * D:t * D + D], src[:, c, t * P:t * P + P], weights[:, c],
                                       start=(c == 0), stop=(c == KC - 1))
                return mm

            def norm_turn(m):
                pe.wait_ge(sem["xhat_ready"], NT * (m + 1))
                w(pe, sem["aoT_copied"], m - 1)
                turn(Fb[0], xhat).then_inc(sem["xT_done"], 1)

            def project_qk(m, t):
                if t == 0:
                    pe.wait_ge(sem["hT_ready"], KC * (m + 1))
                    w(pe, sem["wo_scaled"], m - 1)
                for c in range(KC):
                    mm = pe.matmul(Fb[1 - t][:], hT[:, c, t * P:t * P + P], wqk[:, c],
                                   start=(c == 0), stop=(c == KC - 1))
                mm.then_inc(sem["qk_done"], 1)

            def project_v(m):
                pe.wait_ge(sem["rope_terms"], 6 * m + 3)
                project(Fb[1], hT, wv).then_inc(sem["v_done"], 1)

            def turn_qk(m, n):
                t, qk, half = n // 4, n // 2 % 2, n % 2
                pe.wait_ge(sem["rope_low"], 4 * m + 2 * t + qk + 1)
                if n == 0:
                    pe.wait_ge(sem["v_ready"], m + 1)
                if n == 1:
                    pe.wait_ge(sem["rope_terms"], 6 * m + 6)
                    w(pe, sem["h2_ready"], KC * (m - 1))
                if n >= 2:
                    pe.wait_ge(sem["qkT_dve"] if half else sem["qkT_act"], 4 * m + n // 2)
                for j in range(4):
                    heads = slice(8 * half + 2 * j, 8 * half + 2 * j + 2)
                    mm = pe.transpose(Fb[1 - half][:, j * P:j * P + P],
                                      qks[:, t, qk, heads].rearrange("p h a d -> p (h a d)").bitcast(F32), idf[:])
                mm.then_inc(sem["qkT_done"], 1)

            def heads_out(l, v, front):
                pe.wait_ge(sem["ao_ready"], NG * (l + 1))
                if front:
                    pe.wait_ge(sem["abs_ready"], 2 * (l + 3))
                else:
                    pe.wait_ge(sem["h2_ready"], KC * l)
                turn(Fb[0], AO[:, v]).then_inc(sem["aoT_done"], 1)

            def project_out(l):
                pe.wait_ge(sem["aoT_copied"], l + 1)
                project(Fb[1], aoT, wo).then_inc(sem["wo_done"], 1)

            def norm2_turn(l, front):
                pe.wait_ge(sem["xhat2_ready"], NT * (l + 1))
                if front:
                    pe.wait_ge(sem["rope_terms"], 6 * (l + 3))
                turn(Fb[0], xhat2).then_inc(sem["x2T_done"], 1)

            def scores(i, u, n):
                g, k = n // 3, n % 3
                if n == 0:
                    pe.wait_ge(sem["qkT_act"], 4 * i + 2)
                if n == 1:
                    pe.wait_ge(sem["qkT_act"], 4 * i + 4)
                if n == UNITS // 2:
                    pe.wait_ge(sem["qkT_dve"], 4 * i + 4)
                w(pe, sem["exp_done"], UNITS * i + n - 2)
                heads = range(4) if k == 0 else range(2 * k - 2, 2 * k)
                keys = P if k == 0 else 2 * P
                m = (msk0 if k == 0 else msk1)[:].unsqueeze(1).broadcast_to([P, len(heads), keys])
                pe.matmul(S[k][:].rearrange("p (h k) -> p h k", k=keys), idb[:], m, start=True, stop=False)
                r = slice(ROWS * (g % 2), ROWS * (g % 2) + ROWS)
                for slot, j in enumerate(heads):
                    pair = 4 * (g // 2) + j
                    mm = pe.matmul(S[k][:, slot * keys:slot * keys + keys],
                                   QKT[r, u, 0, pair, 0:P] if k == 0 else QKT[r, u, 0, pair, P:T],
                                   QKT[r, u, 1, pair, 0:keys], start=False, stop=(slot == len(heads) - 1))
                mm.then_inc(sem["scores_done"], 1)

            def turn_probs(i, n):
                pe.wait_ge(sem["exp_done"], UNITS * i + n + 1)
                w(pe, sem["pT_copied"], UNITS * i + n - 1)
                for q in range(4):
                    mm = pe.transpose(TP[n % 2][:, q * P:q * P + P], prob[:, n % 2, q * P:q * P + P], idf[:])
                mm.then_inc(sem["pT_done"], 1)

            def head(g, j):
                return 8 * (g // 2) + 2 * j + g % 2

            def attend(i, u, n):
                g, k = n // 3, n % 3
                pe.wait_ge(sem["pT_copied"], UNITS * i + n + 1)
                if k == 0:
                    w(pe, sem["ao_ready"], NG * i + g)
                    if n == 0:
                        pe.wait_ge(sem["v_ready"], i + 1)
                    for j in range(4):
                        mm = pe.matmul(Ov[:, 0, j], pT[:, n % 3, j], V[:, u, 0, head(g, j)], start=True, stop=True)
                else:
                    for slot in range(2):
                        j = 2 * k - 2 + slot
                        for t in range(NT):
                            mm = pe.matmul(Ov[:, 1, j], pT[:, n % 3, 2 * slot + t], V[:, u, t, head(g, j)],
                                           start=(t == 0), stop=(t == NT - 1))
                mm.then_inc(sem["pv_done"], 1)

            def hidden_column(b, f, dst):
                mm = in_parts(pe, dst, (
                    ((part[:, c, f * P:f * P + P] for part in (w1high, w1low)),
                     (part[:, c, at(b * BLK, BLK)] for part in (XT, XTlow))) for c in range(KC)))
                mm.then_inc(sem["ffn1_done"], 1)

            def raw_column(f):
                if f == 0:
                    pe.wait_ge(sem["w1_low"], 1)
                    pe.wait_ge(sem["h2T_low"], CREDIT_LOW + BLK // T)
                    pe.wait_ge(sem["wo_scaled"], NIMG - 1)
                else:
                    pe.wait_ge(sem["raw_saved"], f)
                hidden_column(0, f, Fb[1][:])

            def step(i, u, front, tail):
                for n in range(UNITS):
                    if n + 2 < UNITS:
                        scores(i, u, n + 2)
                    turn_probs(i, n)
                    if not front and n in RAW_SLOTS:
                        raw_column(RAW_SLOTS.index(n))
                    if front and n == 0:
                        conv(i + 1, 1 - u)
                    if tail and n == 1:
                        heads_out(i - 1, 1 - u, front)
                    if tail and n == 2:
                        project_out(i - 1)
                    if front and n == 4:
                        project_qk(i + 1, 0)
                        project_qk(i + 1, 1)
                    if front and n == 5:
                        project_v(i + 1)
                    if tail and n == 7:
                        norm2_turn(i - 1, front)
                    if front and n >= 8:
                        turn_qk(i + 1, 2 * (n - 8))
                        turn_qk(i + 1, 2 * (n - 8) + 1)
                    if n >= 2:
                        attend(i, u, n - 2)
                    if front and n == 3:
                        norm_turn(i + 1)
                if front:
                    scores(i + 1, 1 - u, 0)
                attend(i, u, UNITS - 2)
                attend(i, u, UNITS - 1)
                if front:
                    scores(i + 1, 1 - u, 1)

            pe.wait_ge(sem["band_ready"], 6)
            pe.wait_ge(sem["halo_band_loaded"], 16 * 4)
            conv(0, 0)
            pe.wait_ge(sem["const_a"], 16 * len(first_constants))
            norm_turn(0)
            project_qk(0, 0)
            project_qk(0, 1)
            project_v(0)
            for n in range(8):
                turn_qk(0, n)
            scores(0, 0, 0)
            scores(0, 0, 1)
            pe.wait_ge(sem["const_b"], 16 * len(later_constants))
            step(0, 0, True, False)
            with pe.Fori(0, (NIMG - 2) // 2) as j:
                step(2 * j + 1, 1, True, True)
                step(2 * j + 2, 0, True, True)
            step(NIMG - 1, 1, False, True)

            def hidden_layer(b, columns):
                for f in columns:
                    pe.wait_ge(sem["gelu_done"], CREDIT_GELU + FC * b + f - 3)
                    hidden_column(b, f, bank[f % 4][:])

            def output_layer(b, columns):
                for f in columns:
                    if f == 0:
                        pe.wait_ge(sem["ffn_scaled"], CREDIT_SCALED + 2 * b)
                    pe.wait_ge(sem["hidden_low"], CREDIT_HIDDEN + FC * b + f + 1)
                    for t in range(BT):
                        mm = in_parts(pe, Y[t // 2][:, (t % 2) * D:(t % 2) * D + D], [
                            ((part[:, f, t * P:t * P + P] for part in (G, Glow)),
                             (part[:, f] for part in (w2high, w2low)))],
                            f == 0 and t % 2 == 0, f == FC - 1 and t % 2 == 1)
                        if f == FC - 1 and t % 2 == 1:
                            mm.then_inc(sem["ffn2_done"], 1)

            def turn_experts_input(b):
                for half in range(2):
                    pe.wait_ge(sem["xf_ready"], NT * (2 * b + half + 1))
                    turn(turn_bank[half], XF[:, half]).then_inc(sem["xfT_done"], 1)

            def gate_product(b):
                pe.wait_ge(sem["gate_low"], 1)
                pe.wait_ge(sem["xfT_low"], 2 * b + 2)
                in_parts(pe, turn_bank[0][0:EXPERTS, :], (
                    ((part[:, c] for part in (gatehigh, gatelow)),
                     (part[:, c, at(b * BLK, BLK)] for part in (XT, XTlow))) for c in range(KC))
                    ).then_inc(sem["gateT_done"], 1)

            def turn_gate(b):
                wait_apart(pe, sem["gateT_copied"], b + 1, sem["pe_carrier"])
                for t in range(BT):
                    mm = pe.transpose(gate_bank[:, t * EXPERTS:t * EXPERTS + EXPERTS], logitsT[:, t * P:t * P + P],
                                      idf[0:EXPERTS, 0:EXPERTS])
                mm.then_inc(sem["gate_done"], 1)

            heads_out(NIMG - 1, 1, False)
            pe.wait_ge(sem["raw_saved"], FC)
            project_out(NIMG - 1)
            pe.wait_ge(sem["w2_low"], 1)
            pe.wait_ge(sem["ao_ready"], NG * NIMG)
            pe.wait_ge(sem["pT_copied"], UNITS * NIMG)
            output_layer(0, range(FC))
            norm2_turn(NIMG - 1, False)
            with pe.Fori(1, NBLK) as b:
                pe.wait_ge(sem["h2T_low"], CREDIT_LOW + BLK // T * (b + 1))
                hidden_layer(b, range(0, FC - 2))
                turn_experts_input(b - 1)
                hidden_layer(b, range(FC - 2, FC))
                gate_product(b - 1)
                output_layer(b, range(0, FC // 2))
                turn_gate(b - 1)
                output_layer(b, range(FC // 2, FC))

            def moe_hidden(n, q, e):
                b, u = q % NBLK, q // NBLK
                if b == 0:
                    pe.wait_ge(sem["we_low"], 2 * e + 1)
                pe.wait_ge(sem["prod_ready"], CREDIT_PROD + n - 1)
                for which in range(2):
                    mm = in_parts(pe, bank[2 * which + q % 2][:], (
                        ((part[:, u, c, which * HID:which * HID + HID] for part in (w13high, w13low)),
                         (part[:, c, b * BLK:b * BLK + BLK] for part in (XT, XTlow))) for c in range(KC)))
                mm.then_inc(sem["moe_h_done"], 1)

            def moe_out(n, q, e):
                if q % NBLK == 0:
                    pe.wait_ge(sem["we_low"], 2 * e + 2)
                pe.wait_ge(sem["hid_low"], CREDIT_HID + n + 1)
                for half in range(2):
                    pe.wait_ge(sem["acc_ready"], CREDIT_ACC + BT * (n - 2) + 2 * half + 2)
                    for t in range(2):
                        k = (2 * half + t) * P
                        mm = in_parts(pe, bank[4 + 2 * (q % 2) + half][:, t * D:t * D + D], [
                            ((part[:, q % 2, k:k + P] for part in (hidhigh, hidlow)),
                             (part[:, q // NBLK] for part in (we2high, we2low)))])
                    mm.then_inc(sem["moe_out_done"], 1)

            moe_hidden(0, 0, 0)
            turn_experts_input(NBLK - 1)
            moe_hidden(1, 1, 0)
            gate_product(NBLK - 1)
            turn_gate(NBLK - 1)
            pe.wait_ge(sem["ffn_scaled"], CREDIT_SCALED + 2 * NBLK)
            pe.sem_inc(sem["moe_out_done"], CREDIT_OUT)
            with pe.Fori(0, EXPERTS // 2) as j:
                for q in range(2 * NBLK):
                    moe_hidden(2 * NBLK * j + q + 2, (q + 2) % (2 * NBLK), 2 * j + (q + 2) // NBLK)
                    moe_out(2 * NBLK * j + q, q, 2 * j + q // NBLK)
            for q in range(NBLK):
                if q + 2 < NBLK:
                    moe_hidden(NBLK * EXPERTS + q + 2, q + 2, EXPERTS)
                moe_out(NBLK * EXPERTS + q, q, EXPERTS)

        @block.scalar
        def _(act):
            def edges(m):
                w(act, sem["h_ready"], m)
                for f in range(2):
                    act.wait_ge(sem["conv_done"], 2 * m + f + 1)
                    act.activation(edge[:, f], Fb[f][:].rearrange("p (t d) -> p t d", t=NT), ACT.Abs,
                                   scale=0.5).then_inc(sem["abs_ready"], 1)

            def norm_copy(m):
                act.wait_ge(sem["xT_done"], m + 1)
                w(act, sem["v_done"], m)
                for c in range(KC):
                    act.activation(hT[:, c], Fb[0][:, c * T:c * T + T], ACT.Identity,
                                   scale=norm_wb[:, 0, c:c + 1], bias=norm_wb[:, 1, c:c + 1]).then_inc(sem["hT_ready"], 1)

            def v_copy(m, v):
                act.wait_ge(sem["v_done"], m + 1)
                w(act, sem["pv_done"], UNITS * (m - 1))
                act.activation(V[:, v, :, :, 0:HD], Fb[1][:].rearrange("p (t h d) -> p t h d", t=NT, h=HEADS),
                               ACT.Identity).then_inc(sem["v_ready"], 1)

            def rope_high(m, t):
                act.wait_ge(sem["rope_ready"], NT * m + t + 1)
                w(act, sem["qkT_done"], 8 * m)
                for qk, high in enumerate((slice(0, 4, 2), slice(0, 2))):
                    act.activation(qks[:, t, qk, :, high], qkr[:, t, qk].unsqueeze(2).broadcast_to([P, HEADS, 2, HD]),
                                   ACT.Identity).then_inc(sem["rope_high"], 1)

            def qkT_copy(m, v, n):
                t, qk = n // 4, n // 2 % 2
                act.wait_ge(sem["qkT_done"], 8 * m + n + 1)
                act.activation(QKT[:, v, qk, 0:4, t * P:t * P + P], Fb[1][:].rearrange("p (j k) -> p j k", j=4),
                               ACT.Identity).then_inc(sem["qkT_act"], 1)

            def ao_copy(l):
                act.wait_ge(sem["aoT_done"], l + 1)
                act.activation(aoT[:], Fb[0][:].rearrange("p (c k) -> p c k", c=KC), ACT.Identity
                               ).then_inc(sem["aoT_copied"], 1)

            def h2_high(l):
                act.wait_ge(sem["h2_ready"], KC * (l + 1))
                act.activation(XT[:, :, at(l * T, T)], h2[:], ACT.Identity).then_inc(sem["h2T_ready"], 1)

            def norm2_copy(l):
                act.wait_ge(sem["x2T_done"], l + 1)
                act.wait_ge(sem["h2T_low"], CREDIT_LOW + l)
                for c in range(KC):
                    act.activation(h2[:, c], Fb[0][:, c * T:c * T + T], ACT.Identity,
                                   scale=norm_wb[:, 2, c:c + 1], bias=norm_wb[:, 3, c:c + 1]).then_inc(sem["h2_ready"], 1)

            def exps(i, u, n):
                k = n % 3
                heads, keys = (4, P) if k == 0 else (2, 2 * P)
                act.wait_ge(sem["negmax_ready"], UNITS * i + n + 1)
                w(act, sem["pT_done"], UNITS * i + n - 1)
                for h in range(heads):
                    a = act.activation(prob[:, n % 2, h * keys:h * keys + keys], S[k][:, h * keys:h * keys + keys],
                                       ACT.Exp, bias=negmax[:, u, n, h:h + 1])
                a.then_inc(sem["exp_done"], 1)

            def raw_copy(f):
                act.wait_ge(sem["ffn1_done"], f + 1)
                act.activation(raw[:, f], Fb[1][:], ACT.Identity).then_inc(sem["raw_saved"], 1)

            def step(i, u, front, tail):
                exps(i, u, 0)
                for n in range(UNITS):
                    if n + 1 < UNITS:
                        exps(i, u, n + 1)
                    if not front and n in RAW_SLOTS:
                        raw_copy(RAW_SLOTS.index(n))
                    if front and n == 0:
                        edges(i + 1)
                    if tail and n == 1:
                        ao_copy(i - 1)
                    if front and n == 3:
                        norm_copy(i + 1)
                    if front and n == 5:
                        v_copy(i + 1, 1 - u)
                    if tail and n == 7:
                        norm2_copy(i - 1)
                    if front and n in (6, 7):
                        rope_high(i + 1, n - 6)
                    if tail and n == 10:
                        h2_high(i - 1)
                    if front and n >= 8:
                        qkT_copy(i + 1, 1 - u, 2 * (n - 8))

            act.wait_ge(sem["filter_loaded"], 16 * len(filters))
            for f in range(2):
                for dx in range(3):
                    act.activation(band[:, f, dx], shf[:, 0], ACT.Identity, scale=tap(f, 0, dx)
                                   ).then_inc(sem["band_part"], 1)
            edges(0)
            act.wait_ge(sem["const_a"], 16 * len(first_constants))
            norm_copy(0)
            act.wait_ge(sem["ones_set"], 1)
            v_copy(0, 0)
            for t in range(NT):
                rope_high(0, t)
            for n in range(0, 8, 2):
                qkT_copy(0, 0, n)
            act.wait_ge(sem["const_b"], 16 * len(later_constants))
            step(0, 0, True, False)
            with act.Fori(0, (NIMG - 2) // 2) as j:
                step(2 * j + 1, 1, True, True)
                step(2 * j + 2, 0, True, True)
            act.wait_ge(sem["conv_done"], 2 * NIMG)
            act.wait_ge(sem["h_ready"], NIMG)
            act.wait_ge(sem["v_done"], NIMG)
            act.wait_ge(sem["rope_ready"], NT * NIMG)
            act.wait_ge(sem["qkT_done"], 8 * NIMG)
            act.activation(w1high[:], w1[:], ACT.Identity).then_inc(sem["w1_high"], 1)
            act.activation(w2high[:], w2[:], ACT.Identity).then_inc(sem["w2_high"], 1)
            step(NIMG - 1, 1, False, True)

            def hidden_layer(b, columns):
                for f in columns:
                    if isinstance(b, int) and b == 0:
                        src = raw[:, f]
                        act.wait_ge(sem["raw_saved"], f + 1)
                    else:
                        src = bank[f % 4][:]
                        act.wait_ge(sem["ffn1_done"], FC * b + f + 1)
                    act.wait_ge(sem["hidden_low"], CREDIT_HIDDEN + FC * b + f - 1)
                    act.activation(gelu[:, f % 2], src, ACT.Gelu, bias=b1c[:, f:f + 1]
                                   ).then_inc(sem["gelu_done"], 1)
                    act.wait_ge(sem["gelu_done"], CREDIT_GELU + FC * b + f + 1)
                    act.activation(G[:, f], gelu[:, f % 2], ACT.Identity).then_inc(sem["hidden_high"], 1)

            def experts_input(b, half):
                r = 2 * b + half
                act.wait_ge(sem["xfT_done"], r + 1)
                act.activation(XT[:, :, at(r * T, T)], turn_bank[half][:].rearrange("p (c k) -> p c k", c=KC),
                               ACT.Identity).then_inc(sem["xfT_copied"], 1)

            def gate_copy(b):
                act.wait_ge(sem["gateT_done"], b + 1)
                act.activation(logitsT[:], turn_bank[0][0:EXPERTS, :], ACT.Identity).then_inc(sem["gateT_copied"], 1)

            def gate_exp(b):
                act.wait_ge(sem["gate_shift"], b + 1)
                act.activation(gexp[:, :, 0:EXPERTS], gsh[:], ACT.Exp).then_inc(sem["gate_exp"], 1)

            act.sem_inc(sem["gelu_done"], CREDIT_GELU)
            act.wait_ge(sem["pv_done"], UNITS * NIMG)
            hidden_layer(0, range(0, 1))
            ao_copy(NIMG - 1)
            hidden_layer(0, range(1, FC // 2))
            act.activation(gatehigh[:], gate[:], ACT.Identity).then_inc(sem["gate_high"], 1)
            hidden_layer(0, range(FC // 2, FC))
            norm2_copy(NIMG - 1)
            h2_high(NIMG - 1)
            act.wait_ge(w_loaded[0], 32)
            act.activation(w13high[:, 0], w13[:, 0], ACT.Identity).then_inc(sem["we_high"], 1)
            act.activation(we2high[:, 0], we2[:, 0], ACT.Identity).then_inc(sem["we_high"], 1)
            with act.Fori(1, NBLK) as b:
                hidden_layer(b, range(0, FC - 3))
                experts_input(b - 1, 0)
                experts_input(b - 1, 1)
                hidden_layer(b, range(FC - 3, FC))
                gate_copy(b - 1)
                gate_exp(b - 1)

            def gated(n, q):
                act.wait_ge(sem["moe_h_done"], n + 1)
                act.wait_ge(sem["prod_ready"], CREDIT_PROD + n - 1)
                act.activation(silu[:, q % 2], bank[q % 2][:], ACT.Silu).then_inc(sem["silu_done"], 1)

            def hidden_high(n, q):
                act.wait_ge(sem["prod_ready"], CREDIT_PROD + n + 1)
                if not isinstance(n, int) or n >= 2:
                    act.wait_ge(sem["moe_out_done"], CREDIT_OUT + 2 * (n - 1))
                act.activation(hidhigh[:, q % 2], hid[:, q % 2], ACT.Identity).then_inc(sem["hid_high"], 1)

            def weights_high(e, u):
                act.wait_ge(w_loaded[u], 16 * (e - u) + 32)
                act.wait_ge(sem["moe_out_done"], CREDIT_OUT + 2 * NBLK * (e - 1))
                act.activation(w13high[:, u], w13[:, u], ACT.Identity).then_inc(sem["we_high"], 1)
                act.activation(we2high[:, u], we2[:, u], ACT.Identity).then_inc(sem["we_high"], 1)

            gated(0, 0)
            experts_input(NBLK - 1, 0)
            experts_input(NBLK - 1, 1)
            gated(1, 1)
            gate_copy(NBLK - 1)
            hidden_high(0, 0)
            hidden_high(1, 1)
            gate_exp(NBLK - 1)
            with act.Fori(0, EXPERTS // 2) as j:
                for q in range(2, 2 * NBLK + 2):
                    gated(2 * NBLK * j + q, q)
                    hidden_high(2 * NBLK * j + q, q)
                    if q % NBLK == 2:
                        weights_high(2 * j + q // NBLK + 1, (q // NBLK + 1) % 2)
            for q in range(2, NBLK):
                gated(NBLK * EXPERTS + q, q)
                hidden_high(NBLK * EXPERTS + q, q)

        @block.vector
        def _(dve):
            def norm_stats(k, m, src, counted, found):
                for t in range(NT):
                    dve.bn_stats(stats[:, k, t], src(t)).then_inc(counted, 1)
                wait_apart(dve, counted, NT * (m + 1), sem["dve_carrier"])
                for t in range(NT):
                    dve.bn_aggr(mv[:, k, t], stats[:, k, t]).then_inc(found, 1)

            def inverse_root(v, r, m, done):
                y, a, b = r[:, 0], r[:, 1], r[:, 2]
                dve.tensor_scalar(y.bitcast(I32), v.bitcast(I32), -0.5, ROOT_BITS, ALU.mult, ALU.add
                                  ).then_inc(done, 1)
                for it in range(3):
                    dve.wait_ge(done, 10 * m + 3 * it + 1)
                    dve.scalar_tensor_tensor(out=a, in0=v, scalar=-0.5, in1=y, op0=ALU.mult, op1=ALU.mult
                                             ).then_inc(done, 1)
                    dve.wait_ge(done, 10 * m + 3 * it + 2)
                    dve.tensor_tensor(b, a, y, ALU.mult).then_inc(done, 1)
                    dve.wait_ge(done, 10 * m + 3 * it + 3)
                    dve.scalar_tensor_tensor(out=y, in0=b, scalar=1.5, in1=y, op0=ALU.add, op1=ALU.mult
                                             ).then_inc(done, 1)
                dve.wait_ge(done, 10 * m + 10)

            def tile_of(buf, m):
                return lambda t: buf[:, at(NT * m + t, 1)].rearrange("p a d -> p (a d)")

            def edge_sum(m):
                dve.wait_ge(sem["abs_ready"], 2 * (m + 1))
                dve.tensor_tensor(Hb[:, at(NT * m, NT)], edge[:, 0], edge[:, 1], ALU.add).then_inc(sem["h_ready"], 1)
                wait_apart(dve, sem["h_ready"], m + 1, sem["dve_carrier"])
                norm_stats(0, m, tile_of(Hb, m), sem["stats1"], sem["mv1"])

            def first_norms(m):
                v = mv[:, 0, :, 1]
                dve.wait_ge(sem["mv1"], NT * (m + 1))
                dve.tensor_scalar(vars1[:, 0], v, EPS, None, ALU.add).then_inc(sem["vars1"], 1)
                dve.tensor_scalar(vars1[:, 1], v, 1.0 + EPS, EPS * EPS, ALU.mult, ALU.add
                                  ).then_inc(sem["vars1"], 1)
                dve.wait_ge(sem["vars1"], 2 * (m + 1))
                inverse_root(vars1[:], root1, m, sem["root1"])

            def normalize_tokens(m, v):
                w(dve, sem["x2_ready"], m - 1)
                for t in range(NT):
                    dve.tensor_scalar(x1[:, v, t], tile_of(Hb, m)(t), mv[:, 0, t, 0:1],
                                      root1[:, 0, 0, t:t + 1], ALU.subtract, ALU.mult).then_inc(sem["x1_ready"], 1)

            def normalize_first(m):
                w(dve, sem["xT_done"], m)
                for t in range(NT):
                    dve.tensor_scalar(xhat[:, t], tile_of(Hb, m)(t), mv[:, 0, t, 0:1],
                                      root1[:, 0, 1, t:t + 1], ALU.subtract, ALU.mult).then_inc(sem["xhat_ready"], 1)

            def rope(m, t):
                dve.wait_ge(sem["qk_done"], NT * m + t + 1)
                w(dve, sem["rope_ready"], NT * (m - 1) + t + 1)
                qk = Fb[1 - t][:].rearrange("p (a h d) -> p a h d", a=2, h=HEADS)
                half = HD // 2
                cos = cosT[:, t].unsqueeze(2).broadcast_to([P, 2, HEADS, HD])
                sin = sinT[:, t].unsqueeze(2).broadcast_to([P, 2, HEADS, HD])
                dve.tensor_tensor(rcos[:, t], qk, cos, ALU.mult).then_inc(sem["rope_terms"], 1)
                dve.tensor_tensor(rsin[:, t, :, :, 0:half], qk[:, :, :, half:HD], sin[:, :, :, 0:half], ALU.mult
                                  ).then_inc(sem["rope_terms"], 1)
                dve.tensor_tensor(rsin[:, t, :, :, half:HD], qk[:, :, :, 0:half], sin[:, :, :, half:HD], ALU.mult
                                  ).then_inc(sem["rope_terms"], 1)

            def qkT_copy(m, v, n):
                t, qk = n // 4, n // 2 % 2
                dve.wait_ge(sem["qkT_done"], 8 * m + n + 1)
                dve.tensor_copy(QKT[:, v, qk, 4:8, t * P:t * P + P], Fb[0][:].rearrange("p (j k) -> p j k", j=4)
                                ).then_inc(sem["qkT_dve"], 1)

            def scale_out(l):
                dve.wait_ge(sem["wo_done"], l + 1)
                dve.tensor_tensor(wos[:], Fb[1][:].rearrange("p (t d) -> p t d", t=NT),
                                  ls1[:].unsqueeze(1).broadcast_to([P, NT, D]), ALU.mult).then_inc(sem["wo_scaled"], 1)

            def second_stats(l):
                wait_apart(dve, sem["x2_ready"], l + 1, sem["dve_carrier"])
                norm_stats(1, l, lambda t: x2[:, t], sem["stats2"], sem["mv2"])

            def second_norm(l):
                dve.wait_ge(sem["mv2"], NT * (l + 1))
                dve.tensor_scalar(vars2[:, 0], mv[:, 1, :, 1], EPS, None, ALU.add).then_inc(sem["vars2"], 1)
                dve.wait_ge(sem["vars2"], l + 1)
                inverse_root(vars2[:], root2, l, sem["root2"])
                for t in range(NT):
                    dve.tensor_scalar(xhat2[:, t], x2[:, t], mv[:, 1, t, 0:1], root2[:, 0, 0, t:t + 1],
                                      ALU.subtract, ALU.mult).then_inc(sem["xhat2_ready"], 1)

            def row_max(i, u, n):
                k = n % 3
                heads = 4 if k == 0 else 2
                dve.wait_ge(sem["scores_done"], UNITS * i + n + 1)
                dve.tensor_reduce(negmax[:, u, n, 0:heads], S[k][:].rearrange("p (h k) -> p h k", h=heads),
                                  AX.X, ALU.max, negate=True).then_inc(sem["negmax_ready"], 1)

            def pT_copy(i, n):
                dve.wait_ge(sem["pT_done"], UNITS * i + n + 1)
                w(dve, sem["pv_done"], UNITS * i + n - 2)
                dve.tensor_copy(pT[:, n % 3], TP[n % 2][:].rearrange("p (q k) -> p q k", q=4)).then_inc(sem["pT_copied"], 1)

            def divide(i, u, g):
                dve.wait_ge(sem["pv_done"], UNITS * i + 3 * (g + 1))
                dve.reciprocal(rinv[:, g], Ov[:, :, :, HD]).then_inc(sem["recip_ready"], 1)
                dve.wait_ge(sem["recip_ready"], NG * i + g + 1)
                ao = AO[:, u].rearrange("p t (a j b d) -> p t a j b d", a=2, j=4, d=HD)[:, :, g // 2, :, g % 2]
                dve.tensor_tensor(ao, Ov[:, :, :, 0:HD], rinv[:, g].unsqueeze(3).broadcast_to([P, NT, 4, HD]),
                                  ALU.mult).then_inc(sem["ao_ready"], 1)

            def step(i, u, front, tail):
                for n in range(UNITS):
                    if n % 3 == 2 and n > 2:
                        divide(i, u, n // 3 - 1)
                    if n + 2 < UNITS:
                        row_max(i, u, n + 2)
                    pT_copy(i, n)
                    if front and n == 0:
                        edge_sum(i + 1)
                    if front and n == 1:
                        first_norms(i + 1)
                    if front and n == 1:
                        normalize_first(i + 1)
                    if tail and n == 2:
                        scale_out(i - 1)
                    if tail and n == 3:
                        second_stats(i - 1)
                    if front and n in (4, 5):
                        rope(i + 1, n - 4)
                    if tail and n == 5:
                        second_norm(i - 1)
                    if front and n == 9:
                        normalize_tokens(i + 1, 1 - u)
                    if front and n >= 8:
                        qkT_copy(i + 1, 1 - u, 2 * (n - 8) + 1)
                if front:
                    row_max(i + 1, 1 - u, 0)
                divide(i, u, NG - 1)
                if front:
                    row_max(i + 1, 1 - u, 1)

            dve.sem_inc(sem["ffn_scaled"], CREDIT_SCALED)
            dve.sem_inc(sem["prod_ready"], CREDIT_PROD)
            dve.wait_ge(sem["memset_done"], 2)
            dve.wait_ge(x_loaded[0], 16 * NCH)
            g = gray[:, 0, :, 1:D + 1]
            dve.tensor_scalar(g, xin[:, 0, 0], GRAY[0], None, ALU.mult).then_inc(sem["gray_first"], 1)
            for c in (1, 2):
                dve.wait_ge(sem["gray_first"], c)
                dve.scalar_tensor_tensor(out=g, in0=xin[:, 0, c], scalar=GRAY[c], in1=g, op0=ALU.mult, op1=ALU.add
                                         ).then_inc(sem["gray_first"], 1)
            dve.wait_ge(sem["filter_loaded"], 16 * len(filters))
            for dy in (1, 2):
                dve.wait_ge(sem["band_part"], 6 * dy)
                for f in range(2):
                    for dx in range(3):
                        o = band[:, f, dx]
                        done = sem["band_ready"] if dy == 2 else sem["band_part"]
                        dve.scalar_tensor_tensor(out=o, in0=shf[:, dy], scalar=tap(f, dy, dx), in1=o,
                                                 op0=ALU.mult, op1=ALU.add).then_inc(done, 1)
            edge_sum(0)
            first_norms(0)
            normalize_first(0)
            normalize_tokens(0, 0)
            dve.wait_ge(sem["const_a"], 16 * len(first_constants))
            rope(0, 0)
            rope(0, 1)
            for n in range(1, 8, 2):
                qkT_copy(0, 0, n)
            row_max(0, 0, 0)
            row_max(0, 0, 1)
            dve.wait_ge(sem["const_b"], 16 * len(later_constants))
            step(0, 0, True, False)
            with dve.Fori(0, (NIMG - 2) // 2) as j:
                step(2 * j + 1, 1, True, True)
                step(2 * j + 2, 0, True, True)
            step(NIMG - 1, 1, False, True)
            scale_out(NIMG - 1)
            second_stats(NIMG - 1)
            second_norm(NIMG - 1)

            def output_rows(b):
                for half in range(2):
                    dve.wait_ge(sem["ffn2_done"], 2 * b + half + 1)
                    dve.tensor_tensor(fs[:, half], Y[half][:].rearrange("p (t d) -> p t d", t=2),
                                      ls2[:].unsqueeze(1).broadcast_to([P, 2, D]), ALU.mult
                                      ).then_inc(sem["ffn_scaled"], 1)
                dve.wait_ge(sem["base_ready"], CREDIT_LOW + BLK // T * (b + 1))
                for half in range(2):
                    dve.wait_ge(sem["ffn_scaled"], CREDIT_SCALED + 2 * b + half + 1)
                    h = Hb[:, at(BT * b + 2 * half, 2)]
                    dve.tensor_tensor(h, h, fs[:, half], ALU.add).then_inc(sem["h3_ready"], 1)
                wait_apart(dve, sem["h3_ready"], 2 * (b + 1), sem["dve_carrier"])
                rows = [Hb[:, at(BT * b + t, 1)].rearrange("p a d -> p (a d)") for t in range(BT)]
                for t in range(BT):
                    dve.bn_stats(stats3[:, t], rows[t]).then_inc(sem["stats3"], 1)
                wait_apart(dve, sem["stats3"], BT * (b + 1), sem["dve_carrier"])
                for t in range(BT):
                    dve.bn_aggr(mv3[:, t], stats3[:, t]).then_inc(sem["mv3"], 1)
                dve.wait_ge(sem["mv3"], BT * (b + 1))
                dve.tensor_scalar(vars3[:, 0], mv3[:, :, 1], EPS, None, ALU.add).then_inc(sem["vars3"], 1)
                dve.wait_ge(sem["vars3"], b + 1)
                inverse_root(vars3[:], root3, b, sem["root3"])
                w(dve, sem["xfT_done"], 2 * b)
                for t in range(BT):
                    dve.tensor_scalar(XF[:, t // 2, t % 2], rows[t], mv3[:, t, 0:1], root3[:, 0, 0, t:t + 1],
                                      ALU.subtract, ALU.mult).then_inc(sem["xf_ready"], 1)

            def low_part(b, half):
                r = 2 * b + half
                dve.wait_ge(sem["xfT_copied"], r + 1)
                tokens = at(r * T, T)
                dve.tensor_tensor(XTlow[:, :, tokens], turn_bank[half][:].rearrange("p (c k) -> p c k", c=KC),
                                  XT[:, :, tokens].bitcast(F32), ALU.subtract).then_inc(sem["xfT_low"], 1)

            logits = gate_bank[:, 0:BT * EXPERTS].rearrange("p (k e) -> p k e", e=EXPERTS)

            def gate_shift(b):
                dve.wait_ge(sem["gate_done"], b + 1)
                dve.tensor_reduce(gmax[:], logits, AX.X, ALU.max).then_inc(sem["gate_max"], 1)
                dve.wait_ge(sem["gate_max"], b + 1)
                dve.tensor_tensor(gsh[:], logits, gmax[:].unsqueeze(2).broadcast_to([P, BT, EXPERTS]),
                                  ALU.subtract).then_inc(sem["gate_shift"], 1)
                dve.wait_ge(sem["gate_shift"], b + 1)

            def combine(b):
                wait_apart(dve, sem["gate_exp"], b + 1, sem["dve_carrier"])
                for k in range(BT):
                    dve.max(top8[:, k], gexp[:, k, 0:EXPERTS]).then_inc(sem["top_ready"], 1)
                dve.wait_ge(sem["top_ready"], BT * (b + 1))
                dve.tensor_copy(keys[:, :, 0:TOPK], top8[:, :, 0:TOPK]).then_inc(sem["keys_ready"], 1)
                dve.tensor_reduce(tsum[:], top8[:, :, 0:TOPK], AX.X, ALU.add).then_inc(sem["sum_ready"], 1)
                wait_apart(dve, sem["keys_ready"], b + 1, sem["dve_carrier"])
                for k in range(BT):
                    dve.match_replace(repl[:, k], keys[:, k], gexp[:, k], -9.0).then_inc(sem["replaced"], 1)
                dve.wait_ge(sem["sum_ready"], b + 1)
                dve.reciprocal(tinv[:], tsum[:]).then_inc(sem["inv_ready"], 1)
                dve.wait_ge(sem["replaced"], BT * (b + 1))
                dve.scalar_tensor_tensor(out=pick[:], in0=repl[:, :, 0:EXPERTS], scalar=-8.0,
                                         in1=gexp[:, :, 0:EXPERTS], op0=ALU.is_lt, op1=ALU.mult
                                         ).then_inc(sem["picked"], 1)
                dve.wait_ge(sem["picked"], b + 1)
                dve.wait_ge(sem["inv_ready"], b + 1)
                dve.tensor_tensor(comb[:, 0:EXPERTS, at(BT * b, BT)].rearrange("p e k -> p k e"), pick[:],
                                  tinv[:].unsqueeze(2).broadcast_to([P, BT, EXPERTS]), ALU.mult
                                  ).then_inc(sem["combine_ready"], 1)
                dve.wait_ge(sem["combine_ready"], b + 1)

            dve.wait_ge(sem["base_ready"], CREDIT_LOW + NIMG - 1)
            dve.memset(comb[:, EXPERTS], 1.0).then_inc(sem["keys_set"], 1)
            for k in range(TOPK):
                dve.memset(gexp[:, :, EXPERTS + k:EXPERTS + k + 1], -1.0 - k).then_inc(sem["keys_set"], 1)
                dve.memset(keys[:, :, TOPK + k:TOPK + k + 1], -1.0 - k).then_inc(sem["keys_set"], 1)
            dve.wait_ge(sem["keys_set"], 9)
            output_rows(0)
            def block_rows(b):
                low_part(b - 1, 0)
                low_part(b - 1, 1)
                gate_shift(b - 1)
                output_rows(b)

            with dve.Fori(1, NBLK - 1) as b:
                block_rows(b)
                combine(b - 1)
            block_rows(NBLK - 1)

            def product(n, q):
                dve.wait_ge(sem["silu_done"], n + 1)
                dve.wait_ge(sem["hid_low"], CREDIT_HID + n - 1)
                dve.tensor_tensor(hid[:, q % 2], silu[:, q % 2], bank[2 + q % 2][:], ALU.mult
                                  ).then_inc(sem["prod_ready"], 1)

            def accumulate(n, q, e):
                for t in range(BT):
                    if t % 2 == 0:
                        dve.wait_ge(sem["moe_out_done"], CREDIT_OUT + 2 * n + t // 2 + 1)
                    k = BT * (q % NBLK) + t
                    y = bank[4 + 2 * (q % 2) + t // 2][:, (t % 2) * D:(t % 2) * D + D]
                    dve.wait_ge(sem["acc_ready"], CREDIT_ACC + BT * (n - 1) + t)
                    dve.scalar_tensor_tensor(out=Hb[:, k], in0=y,
                                             scalar=comb[:, at(e, 1), k:k + 1].rearrange("p a b -> p (a b)"),
                                             in1=Hb[:, k], op0=ALU.mult, op1=ALU.add).then_inc(sem["acc_ready"], 1)

            product(0, 0)
            low_part(NBLK - 1, 0)
            low_part(NBLK - 1, 1)
            combine(NBLK - 2)
            product(1, 1)
            gate_shift(NBLK - 1)
            dve.sem_inc(sem["acc_ready"], CREDIT_ACC)
            combine(NBLK - 1)
            with dve.Fori(0, EXPERTS // 2) as j:
                for q in range(2 * NBLK):
                    product(2 * NBLK * j + q + 2, (q + 2) % (2 * NBLK))
                    accumulate(2 * NBLK * j + q, q, 2 * j + q // NBLK)
            for q in range(NBLK):
                if q + 2 < NBLK:
                    product(NBLK * EXPERTS + q + 2, q + 2)
                accumulate(NBLK * EXPERTS + q, q, EXPERTS)


def kernel(**inputs):
    import concourse.bacc as bacc
    import ml_dtypes
    from concourse.bass_utils import run_bass_kernel_spmd

    f = {k: np.asarray(v) for k, v in inputs.items()}

    def chunks(a, rows=P):
        return np.ascontiguousarray(a.reshape(-1, rows, a.shape[-1]).transpose(1, 0, 2))

    def rows(a):
        return np.ascontiguousarray(np.broadcast_to(a, (P, a.size)))

    def columns(a):
        return np.ascontiguousarray(a.reshape(-1, P).T)

    k, m = np.arange(P)[:, None], np.arange(P)[None, :]
    shift = np.stack([(k == m + dy - 1) for dy in range(3)], 1).astype(np.float32)
    ident = np.eye(P, dtype=np.float32)
    q = np.arange(P)[:, None]
    far = np.arange(2 * P)[None, :]
    mask0 = np.where((q - m >= 0) & (q - m < WINDOW), 0.0, MASKED).astype(ml_dtypes.bfloat16)
    mask1 = np.where((P + q - far >= 0) & (P + q - far < WINDOW), 0.0, MASKED).astype(ml_dtypes.bfloat16)
    inv_freq = (np.float32(1.0) / np.float32(10000.0) ** (np.arange(0, HD, 2, dtype=np.float32) / np.float32(HD)))
    angle = np.outer(np.arange(T, dtype=np.float32), inv_freq.astype(np.float32)).astype(np.float32)
    cos = np.concatenate([np.cos(angle), np.cos(angle)], 1)
    sin = np.concatenate([-np.sin(angle), np.sin(angle)], 1)
    scale = np.float32(HD ** -0.5)

    def table(a):
        both = np.stack([a * scale, a], 1).astype(np.float32)
        return np.ascontiguousarray(both.reshape(NT, P, 2, HD).transpose(1, 0, 2, 3))

    a = "L0_attn_"
    e1 = np.concatenate([f["L0_ffn_w1"], f["L0_ffn_sw1"][None]])
    e3 = np.concatenate([f["L0_ffn_w3"], f["L0_ffn_sw3"][None]])
    e2 = np.concatenate([f["L0_ffn_w2"], f["L0_ffn_sw2"][None]])
    e13 = np.concatenate([e1, e3], 1).transpose(0, 2, 1)
    arrays = {
        "x": f["x"], "shift": shift, "scharr_rows": rows(f["L0_tok_scharr"].reshape(-1)),
        "scharr": f["L0_tok_scharr"], "ident": ident, "ident16": ident.astype(ml_dtypes.bfloat16),
        "mask0": mask0, "mask1": mask1, "rope_cos_t": table(cos), "rope_sin_t": table(sin),
        "wqkT": chunks(np.concatenate([f[a + "wq"].T, f[a + "wk"].T], 1)), "wvT": chunks(f[a + "wv"].T),
        "woT": chunks(f[a + "wo"].T), "ls1_rows": rows(f[a + "ls1"]),
        "n1w": columns(f[a + "norm1_w"]), "n1b": columns(f[a + "norm1_b"]),
        "n2w": columns(f[a + "norm2_w"]), "n2b": columns(f[a + "norm2_b"]),
        "w1T": chunks(f[a + "w1"].T), "b1": columns(f[a + "b1"]), "w2T": chunks(f[a + "w2"].T),
        "b2_rows": rows(f[a + "b2"]), "ls2_rows": rows(f[a + "ls2"]), "gateT": chunks(f["L0_ffn_gate_w"].T),
        "e13T": np.ascontiguousarray(e13.reshape(EXPERTS + 1, KC, P, 2 * HID).transpose(2, 0, 1, 3)),
        "e2T": np.ascontiguousarray(e2.transpose(2, 0, 1)),
    }
    nc = bacc.Bacc("TRN2", target_bir_lowering=False, num_devices=1)
    aps = {k: nc.dram_tensor(f"in_{k}", v.shape, mybir.dt.from_np(v.dtype), kind="ExternalInput").ap()
           for k, v in arrays.items()}
    result = nc.dram_tensor("result", (NIMG, T, D), F32, kind="ExternalOutput").ap()
    build(nc, out=result, **aps)
    r = run_bass_kernel_spmd(nc, [{f"in_{k}": v for k, v in arrays.items()}], core_ids=[0])
    return r.results[0]["result"]
```
